# Optimizing a Trainium2 kernel written in Bass

```python
import numpy as np
import jax
import jax.numpy as jnp

def _softmax(x, axis=-1):
    return jax.nn.softmax(x, axis=axis)

def _gelu(x):
    return jax.nn.gelu(x, approximate=True)

def _silu(x):
    return jax.nn.silu(x)

def _sigmoid(x):
    return jax.nn.sigmoid(x)

def _layernorm(x, axis=-1, eps=1e-05):
    m = jnp.mean(x, axis=axis, keepdims=True)
    v = jnp.var(x, axis=axis, keepdims=True)
    return (x - m) / jnp.sqrt(v + eps)

def _scatter_add(tgt, idx, src, axis=0):
    return tgt.at[idx].add(src)

def _segment_sum(src, seg, n):
    return jax.ops.segment_sum(src, seg, n)
kernel_name = 'mk_seq_preln_d2_jaxref_r8_4b84d8'

def setup_inputs(seed: int=0):
    np.random.seed(seed)
    _w = jnp.asarray

    def _L0_attn_setup():
        import jax, jax.numpy as jnp
        import numpy as np
        B, S, D, H = (2, 256, 128, 16)
        DH = D // H
        key = jax.random.key(seed)
        ks = jax.random.split(key, 5)
        scale = 1.0 / np.sqrt(D)
        return {'in_features': jax.random.normal(ks[0], (B, S, D), jnp.float32), 'Wq': jax.random.normal(ks[1], (D, D), jnp.float32) * scale, 'Wk': jax.random.normal(ks[2], (D, D), jnp.float32) * scale, 'Wv': jax.random.normal(ks[3], (D, D), jnp.float32) * scale, 'Wo': jax.random.normal(ks[4], (D, D), jnp.float32) * scale}
    _L0_attn_in = _L0_attn_setup()

    def _L0_ffn_setup():
        import jax, jax.numpy as jnp
        import numpy as np
        NEG_INF = -1e+30

        def _moe_forward(x, router_w, router_b, w1, b1, w2, b2, top_k=2):
            B, S, D = x.shape
            E = router_w.shape[1]
            logits = jnp.einsum('bsd,de->bse', x, router_w) + router_b
            top_vals, top_idx = jax.lax.top_k(logits, top_k)
            keep = jax.nn.one_hot(top_idx, E, dtype=logits.dtype).sum(-2) > 0
            sparse_logits = jnp.where(keep, logits, NEG_INF)
            gating = jax.nn.softmax(sparse_logits, axis=-1)
            xf = x.reshape(-1, D)
            gf = gating.reshape(-1, E)
            h = jax.nn.relu(jnp.einsum('td,edh->eth', xf, w1) + b1[:, None, :])
            y = jnp.einsum('eth,ehd->etd', h, w2) + b2[:, None, :]
            out = jnp.einsum('etd,te->td', y, gf)
            return out.reshape(B, S, D)
        key = jax.random.key(seed)
        ks = jax.random.split(key, 5)
        B, S, D, E, H = (2, 256, 128, 8, 512)
        scale = 0.02
        return {'x': jax.random.normal(ks[0], (B, S, D), dtype=jnp.float32), 'router_w': jax.random.normal(ks[1], (D, E), dtype=jnp.float32) * scale, 'router_b': jnp.zeros((E,), dtype=jnp.float32), 'w1': jax.random.normal(ks[2], (E, D, H), dtype=jnp.float32) * scale, 'b1': jnp.zeros((E, H), dtype=jnp.float32), 'w2': jax.random.normal(ks[3], (E, H, D), dtype=jnp.float32) * scale, 'b2': jnp.zeros((E, D), dtype=jnp.float32)}
    _L0_ffn_in = _L0_ffn_setup()

    def _L1_attn_setup():
        import jax, jax.numpy as jnp
        import numpy as np
        import math
        B, N, E, D = (4, 1024, 128, 64)
        key = jax.random.key(seed)
        kx, kq, kk, kv, ko = jax.random.split(key, 5)
        x = jax.random.normal(kx, (B, N, E), dtype=jnp.float32)
        wq = jnp.sign(jax.random.normal(kq, (D, E), dtype=jnp.float32)) / math.sqrt(E)
        wk = jnp.sign(jax.random.normal(kk, (D, E), dtype=jnp.float32)) / math.sqrt(E)
        wv = jnp.sign(jax.random.normal(kv, (D, E), dtype=jnp.float32)) / math.sqrt(E)
        wo = jnp.sign(jax.random.normal(ko, (E, D), dtype=jnp.float32)) / math.sqrt(D)
        return {'x': x, 'wq': wq, 'wk': wk, 'wv': wv, 'wo': wo}
    _L1_attn_in = _L1_attn_setup()

    def _L1_ffn_setup():
        import jax, jax.numpy as jnp
        import numpy as np
        D_MODEL = 128
        MLP_DIM = 512
        N_EXPERTS = 8
        B, T = (4, 128)
        key = jax.random.key(seed)
        ks = jax.random.split(key, 7)
        scale_in = (1.0 / D_MODEL) ** 0.5
        scale_out = (1.0 / MLP_DIM) ** 0.5
        bound_g = (1.0 / D_MODEL) ** 0.5
        w_gate = jax.random.uniform(ks[0], (D_MODEL, N_EXPERTS), minval=-bound_g, maxval=bound_g, dtype=jnp.float32)
        b_gate = jax.random.uniform(ks[1], (N_EXPERTS,), minval=-bound_g, maxval=bound_g, dtype=jnp.float32)
        W1 = jax.random.uniform(ks[2], (N_EXPERTS, D_MODEL, MLP_DIM), minval=-scale_in, maxval=scale_in, dtype=jnp.float32)
        b1 = jnp.zeros((N_EXPERTS, MLP_DIM), dtype=jnp.float32)
        W2 = jax.random.uniform(ks[3], (N_EXPERTS, MLP_DIM, D_MODEL), minval=-scale_out, maxval=scale_out, dtype=jnp.float32)
        b2 = jnp.zeros((N_EXPERTS, D_MODEL), dtype=jnp.float32)
        x = jax.random.normal(ks[4], (B, T, D_MODEL), dtype=jnp.float32)
        return {'x': x, 'w_gate': w_gate, 'b_gate': b_gate, 'W1': W1, 'b1': b1, 'W2': W2, 'b2': b2}
    _L1_ffn_in = _L1_ffn_setup()
    _d = {'L0_attn_in_features': _L0_attn_in['in_features'], 'L0_attn_Wq': _L0_attn_in['Wq'], 'L0_attn_Wk': _L0_attn_in['Wk'], 'L0_attn_Wv': _L0_attn_in['Wv'], 'L0_attn_Wo': _L0_attn_in['Wo'], 'L0_ffn_router_w': _L0_ffn_in['router_w'], 'L0_ffn_router_b': _L0_ffn_in['router_b'], 'L0_ffn_w1': _L0_ffn_in['w1'], 'L0_ffn_b1': _L0_ffn_in['b1'], 'L0_ffn_w2': _L0_ffn_in['w2'], 'L0_ffn_b2': _L0_ffn_in['b2'], 'L1_attn_wq': _L1_attn_in['wq'], 'L1_attn_wk': _L1_attn_in['wk'], 'L1_attn_wv': _L1_attn_in['wv'], 'L1_attn_wo': _L1_attn_in['wo'], 'L1_ffn_w_gate': _L1_ffn_in['w_gate'], 'L1_ffn_b_gate': _L1_ffn_in['b_gate'], 'L1_ffn_W1': _L1_ffn_in['W1'], 'L1_ffn_b1': _L1_ffn_in['b1'], 'L1_ffn_W2': _L1_ffn_in['W2'], 'L1_ffn_b2': _L1_ffn_in['b2']}
    _x0 = _d['L0_attn_in_features']
    _d['L0_attn_in_features'] = jax.random.normal(jax.random.fold_in(jax.random.key(seed), 1), (16, 256, 128), dtype=_x0.dtype)
    del _x0
    return _d

def reference(L0_attn_in_features, L0_attn_Wq, L0_attn_Wk, L0_attn_Wv, L0_attn_Wo, L0_ffn_router_w, L0_ffn_router_b, L0_ffn_w1, L0_ffn_b1, L0_ffn_w2, L0_ffn_b2, L1_attn_wq, L1_attn_wk, L1_attn_wv, L1_attn_wo, L1_ffn_w_gate, L1_ffn_b_gate, L1_ffn_W1, L1_ffn_b1, L1_ffn_W2, L1_ffn_b2):

    def _L0_attn_ref(in_features, Wq, Wk, Wv, Wo):
        import jax, jax.numpy as jnp
        import numpy as np
        B, S, D, H = (2, 256, 128, 16)
        DH = D // H
        seq_len = in_features.shape[-2]
        q = in_features @ Wq.T
        k = in_features @ Wk.T
        v = in_features @ Wv.T

        def split(x):
            return jnp.moveaxis(x.reshape(*x.shape[:-1], H, DH), -3, -2)
        q, k, v = (split(q), split(k), split(v))
        scores = jnp.einsum('...hqd,...hkd->...hqk', q, k) / np.sqrt(DH)
        causal = jnp.triu(jnp.ones((seq_len, seq_len), bool), k=1)
        scores = jnp.where(causal, jnp.float32(-1000000000.0), scores)
        weights = jax.nn.softmax(scores, axis=-1)
        out = jnp.einsum('...hqk,...hkd->...hqd', weights, v)
        out = jnp.moveaxis(out, -3, -2).reshape(*in_features.shape[:-1], D)
        return out @ Wo.T

    def _L0_ffn_ref(x, router_w, router_b, w1, b1, w2, b2):
        import jax, jax.numpy as jnp
        import numpy as np
        NEG_INF = -1e+30

        def _moe_forward(x, router_w, router_b, w1, b1, w2, b2, top_k=2):
            B, S, D = x.shape
            E = router_w.shape[1]
            logits = jnp.einsum('bsd,de->bse', x, router_w) + router_b
            top_vals, top_idx = jax.lax.top_k(logits, top_k)
            keep = jax.nn.one_hot(top_idx, E, dtype=logits.dtype).sum(-2) > 0
            sparse_logits = jnp.where(keep, logits, NEG_INF)
            gating = jax.nn.softmax(sparse_logits, axis=-1)
            xf = x.reshape(-1, D)
            gf = gating.reshape(-1, E)
            h = jax.nn.relu(jnp.einsum('td,edh->eth', xf, w1) + b1[:, None, :])
            y = jnp.einsum('eth,ehd->etd', h, w2) + b2[:, None, :]
            out = jnp.einsum('etd,te->td', y, gf)
            return out.reshape(B, S, D)
        return _moe_forward(x, router_w, router_b, w1, b1, w2, b2, top_k=2)

    def _L1_attn_ref(x, wq, wk, wv, wo):
        import jax, jax.numpy as jnp
        import numpy as np
        import math
        B, N, E, D = (4, 1024, 128, 64)
        Q = jnp.einsum('bne,de->bnd', x, wq)
        K = jnp.einsum('bne,de->bnd', x, wk)
        V = jnp.einsum('bne,de->bnd', x, wv)
        energy = jnp.einsum('bnd,bne->bde', K, V)
        context = jnp.einsum('bnd,bde->bne', Q, energy)
        context = context * jnp.asarray(math.sqrt(3.0 / D), dtype=context.dtype)
        out = jnp.einsum('bnd,ed->bne', context, wo)
        return out

    def _L1_ffn_ref(x, w_gate, b_gate, W1, b1, W2, b2):
        import jax, jax.numpy as jnp
        import numpy as np
        D_MODEL = 128
        MLP_DIM = 512
        N_EXPERTS = 8
        B, T = (4, 128)
        b, t, d = x.shape
        x_flat = x.reshape(b * t, d)
        logits = x_flat @ w_gate + b_gate
        probs = jax.nn.softmax(logits, axis=-1)
        route_p = jnp.max(probs, axis=-1)
        route_idx = jnp.argmax(probs, axis=-1)
        h = jnp.einsum('nd,edm->enm', x_flat, W1) + b1[:, None, :]
        h = jax.nn.relu(h)
        y = jnp.einsum('enm,emd->end', h, W2) + b2[:, None, :]
        n = b * t
        out = y[route_idx, jnp.arange(n)] * route_p[:, None]
        return out.reshape(b, t, d)
    x = L0_attn_in_features
    x = x + _L0_attn_ref(_layernorm(x, axis=-1), L0_attn_Wq, L0_attn_Wk, L0_attn_Wv, L0_attn_Wo)
    x = x + _L0_ffn_ref(_layernorm(x, axis=-1), L0_ffn_router_w, L0_ffn_router_b, L0_ffn_w1, L0_ffn_b1, L0_ffn_w2, L0_ffn_b2)
    x = x + _L1_attn_ref(_layernorm(x, axis=-1), L1_attn_wq, L1_attn_wk, L1_attn_wv, L1_attn_wo)
    x = x + _L1_ffn_ref(_layernorm(x, axis=-1), L1_ffn_w_gate, L1_ffn_b_gate, L1_ffn_W1, L1_ffn_b1, L1_ffn_W2, L1_ffn_b2)
    return x

_drawn_inputs = setup_inputs


def setup_inputs(seed=0):
    import zlib

    import numpy as np

    out = dict(_drawn_inputs(seed))
    spreads = {'L0_ffn_router_b': (0.0, 0.1),
     'L0_ffn_b1': (0.0, 0.1),
     'L0_ffn_b2': (0.0, 0.1),
     'L1_ffn_b1': (0.0, 0.8),
     'L1_ffn_b2': (0.0, 2.0)}
    factors = {'L1_ffn_w_gate': 8.0, 'L1_ffn_b_gate': 8.0, 'L1_ffn_W1': 8.0, 'L1_ffn_W2': 8.0}
    for name, (base, spread) in spreads.items():
        noise = np.random.default_rng([zlib.crc32(name.encode()), seed]).standard_normal(out[name].shape)
        drawn = base * np.exp(spread * noise) if base else spread * noise
        out[name] = jnp.asarray(drawn.astype(out[name].dtype))
    for name, factor in factors.items():
        out[name] = (out[name] * factor).astype(out[name].dtype)
    return out
```

```python
import concourse.bass as bass
from concourse import mybir
from concourse.alu_op_type import AluOpType as ALU
from contextlib import ExitStack

F32 = mybir.dt.float32
BF16 = mybir.dt.bfloat16
ACT = mybir.ActivationFunctionType
AX = mybir.AxisListType

P = 128
NSEQ, S, D = 16, 256, 128
TPS = S // P
NT = NSEQ * TPS
H, DH = 16, 8
NQ = H // 4
EPS = 1e-5
NPART = 3
KS = NPART * NPART * DH
KM = KS + NPART
MASKED = -1e30


def counts(value):
    return not isinstance(value, int) or value > 0


def value(eng, v):
    return v if isinstance(v, int) else eng.to_reg(v)


def load_inputs(nc, t, dram, xs):
    with ExitStack() as ctx:
        loaded = ctx.enter_context(nc.semaphore("loaded"))
        iota_base = ctx.enter_context(nc.semaphore("iota_base"))
        zeroed = ctx.enter_context(nc.semaphore("zeroed"))
        block = ctx.enter_context(nc.Block())

        @block.sync
        def _(sp):
            n = 0
            sp.dma_start(t["x"][:, 0:NT // 2, :], dram["x"].rearrange("(t p) d -> p t d", p=P)[:, 0:NT // 2, :]).then_inc(loaded, 16)
            sp.dma_start(t["x"][:, NT // 2:NT, :], dram["x"].rearrange("(t p) d -> p t d", p=P)[:, NT // 2:NT, :]).then_inc(loaded, 16)
            for name in ("wq0", "wk0", "wv0", "wo0", "wr0", "wr1", "wq1", "wkv1", "wo1", "cst", "tri"):
                sp.dma_start(t[name][:], dram[name]).then_inc(loaded, 16)
                n += 1
            for name in ("br0", "br1"):
                sp.dma_start(t[name][:], dram[name].to_broadcast([P, E])).then_inc(loaded, 16)
                n += 1
            sp.wait_ge(loaded, 16 * (n + 2))
            for name in ("wpack0", "wpack1"):
                sp.dma_start(t[name][:], dram[name]).then_inc(t["packs_loaded"], 16)
            sp.wait_ge(zeroed, 3)
            z = t["zeros"][:].rearrange("p (s d) -> p s d", d=D)
            dst = xs.rearrange("(n s p) d -> p n s d", p=P, s=6)
            t["n_fills"] = dst.shape[1]
            for k in range(dst.shape[1]):
                sp.dma_start(dst[:, k], z).then_inc(t["zero_filled"], 16)

        @block.gpsimd
        def _(pool):
            nc.gpsimd.memset(t["ident"][:], 0.0).then_inc(iota_base, 1)
            nc.gpsimd.memset(t["identb"][:], 0.0).then_inc(iota_base, 1)
            nc.gpsimd.memset(t["mask_qk"][:], 0.0).then_inc(iota_base, 1)
            nc.gpsimd.memset(t["mask_kq"][:], 0.0).then_inc(iota_base, 1)
            pool.wait_ge(iota_base, 4)
            for name in ("ident", "identb"):
                nc.gpsimd.affine_select(out=t[name][:], in_=t[name][:], compare_op=ALU.not_equal, fill=1.0,
                                        base=0, pattern=[[-1, P]], channel_multiplier=1)
            nc.gpsimd.affine_select(out=t["mask_qk"][:], in_=t["mask_qk"][:], compare_op=ALU.is_ge, fill=MASKED,
                                    base=0, pattern=[[0, 4], [-1, P]], channel_multiplier=1)
            nc.gpsimd.affine_select(out=t["mask_kq"][:], in_=t["mask_kq"][:], compare_op=ALU.is_ge, fill=MASKED,
                                    base=0, pattern=[[0, 4], [1, P]], channel_multiplier=-1)

        @block.vector
        def _(dve):
            for par in range(2):
                nc.vector.memset(t["kst"][par][:], 1.0)
                nc.vector.memset(t["vaug"][par][:], 0.0).then_inc(zeroed, 1)
                dve.wait_ge(zeroed, par + 1)
                nc.vector.memset(t["vaug"][par][:, :, :, DH:DH + 1], 1.0)
            nc.vector.memset(t["eps"][:], EPS)
            nc.vector.memset(t["zeros"][:], 0.0).then_inc(zeroed, 1)
            dve.wait_ge(loaded, 16 * 15)
            nc.vector.tensor_copy(t["before"][:], t["tri"][:, 0:P])
            nc.vector.tensor_copy(t["onesb"][:], t["tri"][:, P:2 * P])


def norm_scales(nc, t, first=False):
    with ExitStack() as ctx:
        step = ctx.enter_context(nc.semaphore("norm_step"))
        var_ready = ctx.enter_context(nc.semaphore("var_ready"))
        std_ready = ctx.enter_context(nc.semaphore("std_ready"))
        block = ctx.enter_context(nc.Block())
        stats, mean, rstd, tmp = t["stats"], t["mean"], t["rstd"], t["ntmp"]
        me, m2e, mo, m2o = stats[:, :, 1], stats[:, :, 2], stats[:, :, 4], stats[:, :, 5]

        @block.vector
        def _(dve):
            if first:
                with dve.Fori(0, NT) as i:
                    nc.vector.bn_stats(stats[:, bass.ds(i, 1), :], t["x"][:, bass.ds(i, 1), :]).then_inc(step, 1)
            base = NT if first else 0
            if counts(base):
                dve.wait_ge(step, base)
            nc.vector.tensor_tensor(mean[:], me, mo, ALU.add)
            nc.vector.tensor_tensor(tmp[:, 0, :], me, mo, ALU.subtract)
            nc.vector.tensor_tensor(tmp[:, 1, :], m2e, m2o, ALU.add).then_inc(step, 1)
            dve.wait_ge(step, base + 1)
            nc.vector.tensor_scalar(mean[:], mean[:], 0.5, None, ALU.mult)
            nc.vector.scalar_tensor_tensor(out=tmp[:, 2, :], in0=tmp[:, 0, :], scalar=0.25, in1=tmp[:, 0, :],
                                           op0=ALU.mult, op1=ALU.mult).then_inc(step, 1)
            dve.wait_ge(step, base + 2)
            nc.vector.scalar_tensor_tensor(out=tmp[:, 3, :], in0=tmp[:, 1, :], scalar=1.0 / D, in1=tmp[:, 2, :],
                                           op0=ALU.mult, op1=ALU.add).then_inc(var_ready, 1)
            dve.wait_ge(std_ready, 1)
            nc.vector.reciprocal(rstd[:], tmp[:, 4, :])

        @block.scalar
        def _(act):
            act.wait_ge(var_ready, 1)
            nc.scalar.activation(tmp[:, 4, :], tmp[:, 3, :], ACT.Sqrt, bias=t["eps"][:]).then_inc(std_ready, 1)


def causal_attention(nc, t, scratch):
    NU = 6
    WR, LD = 2 * NPART, 2 * NPART * NPART
    x, mean, rstd = t["x"], t["mean"], t["rstd"]
    with ExitStack() as ctx:
        def sb(name, shape, dt):
            return ctx.enter_context(nc.sbuf_tensor(name, shape, dt))

        def sem(name):
            return ctx.enter_context(nc.semaphore(name))

        xn = sb("xn", [P, TPS, D], F32)
        xnT = [sb(f"xnT{i}", [D, S], F32) for i in range(2)]
        parts = sb("parts", [P, NPART, 2, S], BF16)
        resid = sb("resid", [P, 2 * S], F32)
        mx = sb("mx", [P, TPS, H], F32)
        mres = sb("mres", [P, TPS, H], F32)
        mpad = sb("mpad", [P, TPS, P], BF16)
        mparts = mpad[:, :, 0:NPART * H].rearrange("p s (a h) -> p s a h", h=H)
        mT = sb("mT", [NPART * H, S], BF16)
        pT = [sb(f"pT{u}", [P, 3 * 512], F32) for u in range(NQ)]
        oT = [sb(f"oT{i}", [P, NQ, S], F32) for i in range(2)]
        rcp = sb("rcp", [P, TPS, H], F32)
        on = sb("on", [P, TPS, D], F32)
        onT = sb("onT", [D, S], F32)
        qst, kst, vaug = t["qst"], t["kst"], t["vaug"]
        ident, identb = t["ident"], t["identb"]

        max_ps = ctx.enter_context(nc.psum_tensor("max_ps", [P, 2, 512], F32))
        sc_ps = ctx.enter_context(nc.psum_tensor("sc_ps", [P, 3, 512], F32))
        av_ps = ctx.enter_context(nc.psum_tensor("av_ps", [P, 512], F32))
        mix_ps = ctx.enter_context(nc.psum_tensor("mix_ps", [P, 2, 512], F32))

        xn_ready, xnT_done, xnT_ready = sem("xn_ready"), sem("xnT_done"), sem("xnT_ready")
        qk_done, part1_ready, resid_ready = sem("qk_done"), sem("part1_ready"), sem("resid_ready")
        part2_ready, parts_ready = sem("part2_ready"), sem("parts_ready")
        parts_stored = [sem(f"parts_stored{i}") for i in range(2)]
        stack_loaded = [sem(f"stack_loaded{i}") for i in range(2)]

        def transfers(c, par, k):
            return (c + (2 - par)) * (k * 16 // 2)

        unit_done, unit_reduced = sem("unit_done"), sem("unit_reduced")
        msplit, mparts_ready = sem("msplit"), sem("mparts_ready")
        mT_done, mT_ready, mrows_loaded = sem("mT_done"), sem("mT_ready"), sem("mrows_loaded")
        v_done, v_ready = sem("v_done"), sem("v_ready")
        scores_done, probs_ready, av_done, oT_ready = sem("scores_done"), sem("probs_ready"), sem("av_done"), sem("oT_ready")
        o_done, rcp_ready, on_ready = sem("o_done"), sem("rcp_ready"), sem("on_ready")
        onT_done, onT_ready, out_done, x_added = sem("onT_done"), sem("onT_ready"), sem("out_done"), sem("x_added")
        stats_done = sem("stats_done")

        block = ctx.enter_context(nc.Block())

        def run(eng, body, prologue, tail):
            prologue()
            body(0, 0, s4=False)
            body(1, 1)
            with eng.Fori(1, 6) as i:
                body(i * 2, 0)
                body(i * 2 + 1, 1)
            body(12, 0)
            body(13, 1)
            body(14, 0, s1=False)
            body(15, 1, s1=False, s2=False)
            tail(15, 1)

        @block.tensor
        def _(pe):
            def transpose_x(c, par):
                pe.wait_ge(xn_ready, c + 1)
                if counts(c):
                    pe.wait_ge(xnT_ready, c)
                if counts(c - 1):
                    pe.wait_ge(mT_ready, c - 1)
                for s in range(TPS):
                    last = nc.tensor.transpose(max_ps[:, 0, s * P:(s + 1) * P], xn[:, s, :], ident[:])
                last.then_inc(xnT_done, 1)

            def project_qk(c, par):
                pe.wait_ge(xnT_ready, c + 1)
                if counts(c):
                    pe.wait_ge(resid_ready, c)
                if counts(NU * (c - 1)):
                    pe.wait_ge(unit_reduced, NU * (c - 1))
                nc.tensor.matmul(max_ps[:, 1, 0:S], t["wq0"][:], xnT[par][:], start=True, stop=True)
                nc.tensor.matmul(max_ps[:, 1, S:2 * S], t["wk0"][:], xnT[par][:], start=True, stop=True).then_inc(qk_done, 1)

            def project_v(c, par, normed):
                pe.wait_ge(xnT_ready, c + 1)
                if counts(c):
                    pe.wait_ge(v_ready, c)
                if counts(normed):
                    pe.wait_ge(on_ready, normed)
                for s in range(TPS):
                    last = nc.tensor.matmul(mix_ps[:, 1, s * P:(s + 1) * P], xnT[par][:, s * P:(s + 1) * P],
                                            t["wv0"][:], start=True, stop=True)
                last.then_inc(v_done, 1)

            def unit(c, par, k, projected):
                if k == 0:
                    pe.wait_ge(stack_loaded[par], transfers(c, par, LD))
                    if counts(projected):
                        pe.wait_ge(xnT_ready, projected)
                    if counts(projected):
                        pe.wait_ge(resid_ready, projected)
                if counts(c * NU + k):
                    pe.wait_ge(unit_reduced, c * NU + k)
                s = 0 if k < 2 else 1
                heads = range(8 * k, 8 * k + 8) if s == 0 else range(4 * (k - 2), 4 * (k - 2) + 4)
                keys = P * (s + 1)
                per_bank = 512 // keys
                for n, h in enumerate(heads):
                    bank = max_ps[:, n // per_bank, :].rearrange("p (h k) -> p h k", k=keys)
                    if n % per_bank == 0:
                        nc.tensor.matmul(bank[:, :, keys - P:keys], identb[:], t["mask_qk"][:, 0:per_bank, :],
                                         start=True, stop=False, skip_group_check=True)
                    last = nc.tensor.matmul(bank[:, n % per_bank, :], qst[par][0:KS, h, s * P:(s + 1) * P],
                                            kst[par][0:KS, h, 0:keys], start=False, stop=True, skip_group_check=True)
                last.then_inc(unit_done, 1)

            def transpose_max(c, par):
                pe.wait_ge(mparts_ready, c + 1)
                out = max_ps[:, 0, :].bitcast(BF16)
                for s in range(TPS):
                    last = nc.tensor.transpose(out[:, s * P:(s + 1) * P], mpad[:, s, :], identb[:])
                last.then_inc(mT_done, 1)

            def scores(c, par, u):
                if u == 0:
                    pe.wait_ge(stack_loaded[par], transfers(c, par, LD))
                    pe.wait_ge(mrows_loaded, (c + 1) * 16)
                if counts(c * NQ + u):
                    pe.wait_ge(probs_ready, c * NQ + u)
                for bk in range(3):
                    keys = slice(0, P) if bk < 2 else slice(P, S)
                    if bk < 2:
                        diag = sc_ps[:, bk, :].rearrange("p (h q) -> p h q", q=S)[:, :, 0:P]
                        nc.tensor.matmul(diag, identb[:], t["mask_kq"][:, 0:2, :], start=True, stop=False, skip_group_check=True)
                        for n in range(2):
                            h = 4 * u + 2 * bk + n
                            last = nc.tensor.matmul(sc_ps[:, bk, n * S:(n + 1) * S], kst[par][0:KM, h, keys],
                                                    qst[par][0:KM, h, :], start=False, stop=True, skip_group_check=True)
                    else:
                        nc.tensor.matmul(sc_ps[:, 2, :].rearrange("p (h q) -> p h q", q=P), identb[:], t["mask_kq"][:],
                                         start=True, stop=False, skip_group_check=True)
                        for n in range(4):
                            last = nc.tensor.matmul(sc_ps[:, 2, n * P:(n + 1) * P], kst[par][0:KM, 4 * u + n, keys],
                                                    qst[par][0:KM, 4 * u + n, P:S], start=False, stop=True, skip_group_check=True)
                last.then_inc(scores_done, 1)

            def values(c, par, heads):
                for h in heads:
                    u, j = h // 4, h % 4
                    if j == 0:
                        if u == 0:
                            pe.wait_ge(v_ready, c + 1)
                        pe.wait_ge(probs_ready, c * NQ + u + 1)
                        if u % 2 == 0:
                            if counts(c * 2 + u // 2):
                                pe.wait_ge(oT_ready, c * 2 + u // 2)
                    col = (u % 2) * S
                    rows = slice(32 * j, 32 * j + 32)
                    nc.tensor.matmul(av_ps[rows, col:col + S], vaug[par][:, 0, h, :], pT[u][:, j * S:(j + 1) * S],
                                     start=True, stop=False, tile_position=(0, 32 * j))
                    last = nc.tensor.matmul(av_ps[rows, col + P:col + S], vaug[par][:, 1, h, :],
                                            pT[u][:, 4 * S + j * P:4 * S + (j + 1) * P], start=False, stop=True,
                                            tile_position=(0, 32 * j))
                    if j == 3:
                        last.then_inc(av_done, 1)

            def transpose_o(c, par):
                pe.wait_ge(oT_ready, 2 * (c + 1))
                if counts(c):
                    pe.wait_ge(x_added, c)
                if counts(t_v(c)):
                    pe.wait_ge(v_ready, t_v(c))
                for s in range(TPS):
                    for u in range(NQ):
                        last = nc.tensor.transpose(mix_ps[:, s, u * P:(u + 1) * P], oT[par][:, u, s * P:(s + 1) * P], ident[:])
                last.then_inc(o_done, 1)

            def t_v(c):
                return c + 2 if not isinstance(c, int) else min(c + 2, NSEQ)

            def transpose_on(c, par):
                pe.wait_ge(on_ready, c + 1)
                for s in range(TPS):
                    last = nc.tensor.transpose(mix_ps[:, 0, s * P:(s + 1) * P], on[:, s, :], ident[:])
                last.then_inc(onT_done, 1)

            def project_out(c, par):
                pe.wait_ge(onT_ready, c + 1)
                for s in range(TPS):
                    last = nc.tensor.matmul(mix_ps[:, 0, S + s * P:S + (s + 1) * P], onT[:, s * P:(s + 1) * P],
                                            t["wo0"][:], start=True, stop=True)
                last.then_inc(out_done, 1)

            def prologue():
                for c in range(2):
                    transpose_x(c, c)
                    project_qk(c, c)
                project_v(0, 0, 0)
                for k in range(NU):
                    unit(0, 0, k, 2)
                transpose_max(0, 0)

            def body(b, par, s1=True, s2=True, s4=True):
                if s4:
                    transpose_o(b - 1, 1 - par)
                if s1:
                    transpose_x(b + 2, par)
                scores(b, par, 0)
                if s4:
                    transpose_on(b - 1, 1 - par)
                if s1:
                    project_qk(b + 2, par)
                scores(b, par, 1)
                values(b, par, range(0, 4))
                scores(b, par, 2)
                if s2:
                    project_v(b + 1, 1 - par, b)
                if s4:
                    project_out(b - 1, 1 - par)
                values(b, par, range(4, 6))
                scores(b, par, 3)
                after = [range(6, 8), range(8, 10), range(10, 12), range(12, 13), range(13, 14), range(14, 16)]
                for k in range(NU):
                    if s2:
                        unit(b + 1, 1 - par, k, b + 3 if s1 else NSEQ)
                    values(b, par, after[k])
                if s2:
                    transpose_max(b + 1, 1 - par)

            def tail(b, par):
                transpose_o(b, par)
                transpose_on(b, par)
                project_out(b, par)

            run(pe, body, prologue, tail)

        @block.scalar
        def _(act):
            def copy_xT(c, par):
                act.wait_ge(xnT_done, c + 1)
                if counts(c - 1):
                    act.wait_ge(v_done, c - 1)
                if counts(c - 1):
                    act.wait_ge(qk_done, c - 1)
                nc.scalar.copy(xnT[par][:], max_ps[:, 0, 0:S]).then_inc(xnT_ready, 1)

            def first_part(c, par):
                act.wait_ge(qk_done, c + 1)
                if counts(transfers(c - 1, 1 - par, WR)):
                    act.wait_ge(parts_stored[1 - par], transfers(c - 1, 1 - par, WR))
                nc.scalar.copy(parts[:, 0, :, :].rearrange("p a s -> p (a s)"), max_ps[:, 1, :]).then_inc(part1_ready, 1)

            def copy_mT(c, par):
                act.wait_ge(mT_done, c + 1)
                if counts(c * 16):
                    act.wait_ge(mrows_loaded, c * 16)
                nc.scalar.copy(mT[:], max_ps[:, 0, :].bitcast(BF16)[0:NPART * H, 0:S]).then_inc(mT_ready, 1)
                act.wait_ge(mT_ready, c + 1)
                if counts(NQ * (c - 1)):
                    act.wait_ge(scores_done, NQ * (c - 1))
                act.dma_start(qst[par][KS:KM, :, :], mT[:]).then_inc(mrows_loaded, 16)

            def exp(c, u):
                act.wait_ge(scores_done, c * NQ + u + 1)
                if counts((c - 1) * NQ + u + 1):
                    act.wait_ge(av_done, (c - 1) * NQ + u + 1)
                nc.scalar.activation(pT[u][:], sc_ps[:].rearrange("p a s -> p (a s)"), ACT.Exp,
                                     scale=float(DH) ** -0.5).then_inc(probs_ready, 1)

            def copy_onT(c):
                act.wait_ge(onT_done, c + 1)
                if counts(c):
                    act.wait_ge(out_done, c)
                nc.scalar.copy(onT[:], mix_ps[:, 0, 0:S]).then_inc(onT_ready, 1)

            def prologue():
                for c in range(2):
                    copy_xT(c, c)
                    first_part(c, c)
                copy_mT(0, 0)

            def body(b, par, s1=True, s2=True, s4=True):
                if s1:
                    copy_xT(b + 2, par)
                exp(b, 0)
                if s4:
                    copy_onT(b - 1)
                if s1:
                    first_part(b + 2, par)
                for u in range(1, NQ):
                    exp(b, u)
                if s2:
                    copy_mT(b + 1, 1 - par)

            def tail(b, par):
                copy_onT(b)

            run(act, body, prologue, tail)

        @block.vector
        def _(dve):
            def normalise(c):
                if counts(c):
                    dve.wait_ge(xnT_done, c)
                for s in range(TPS):
                    i = c * TPS + s
                    last = nc.vector.tensor_scalar(xn[:, s, :], x[:, bass.ds(i, 1), :].rearrange("p a d -> p (a d)"),
                                                   mean[:, bass.ds(i, 1)], rstd[:, bass.ds(i, 1)], ALU.subtract, ALU.mult)
                last.then_inc(xn_ready, 1)

            def residual(c):
                dve.wait_ge(part1_ready, c + 1)
                if counts(c):
                    dve.wait_ge(parts_ready, c)
                nc.vector.tensor_tensor(resid[:], max_ps[:, 1, :], parts[:, 0, :, :].rearrange("p a s -> p (a s)"),
                                        ALU.subtract).then_inc(resid_ready, 1)
                dve.wait_ge(resid_ready, c + 1)
                nc.vector.tensor_copy(parts[:, 1, :, :].rearrange("p a s -> p (a s)"), resid[:]).then_inc(part2_ready, 1)

            def take_v(c, par):
                dve.wait_ge(v_done, c + 1)
                if counts(NQ * (c - 1)):
                    dve.wait_ge(av_done, NQ * (c - 1))
                nc.vector.tensor_copy(vaug[par][:, :, :, 0:DH].rearrange("p s h d -> p (s h) d"),
                                      mix_ps[:, 1, 0:S].rearrange("p (g d) -> p g d", d=DH)).then_inc(v_ready, 1)

            def reduce_unit(c, k):
                dve.wait_ge(unit_done, c * NU + k + 1)
                if k == 0:
                    if counts(3 * c):
                        dve.wait_ge(msplit, 3 * c)
                    if counts(c):
                        dve.wait_ge(mparts_ready, c)
                s = 0 if k < 2 else 1
                h0, n = (8 * k, 8) if s == 0 else (4 * (k - 2), 4)
                nc.vector.reduce_max(mx[:, s, h0:h0 + n],
                                     max_ps[:].rearrange("p a s -> p (a s)").rearrange("p (h k) -> p h k", h=n),
                                     axis=AX.X).then_inc(unit_reduced, 1)

            def split_max(c):
                dve.wait_ge(unit_reduced, NU * (c + 1))
                if counts(c):
                    dve.wait_ge(mT_done, c)
                nc.vector.tensor_scalar(mparts[:, :, 0, :], mx[:], -1.0, None, ALU.mult).then_inc(msplit, 1)
                dve.wait_ge(msplit, 3 * c + 1)
                nc.vector.scalar_tensor_tensor(out=mres[:], in0=mx[:], scalar=-1.0, in1=mparts[:, :, 0, :],
                                               op0=ALU.mult, op1=ALU.subtract).then_inc(msplit, 1)
                dve.wait_ge(msplit, 3 * c + 2)
                nc.vector.tensor_copy(mparts[:, :, 1, :], mres[:]).then_inc(msplit, 1)
                dve.wait_ge(msplit, 3 * c + 3)
                nc.vector.tensor_tensor(mparts[:, :, 2, :], mres[:], mparts[:, :, 1, :], ALU.subtract).then_inc(mparts_ready, 1)

            def take_oT(c, par, pair):
                dve.wait_ge(av_done, NQ * c + 2 * pair + 2)
                if counts(c - 1):
                    dve.wait_ge(o_done, c - 1)
                nc.vector.tensor_copy(oT[par][:, 2 * pair:2 * pair + 2, :].rearrange("p u s -> p (u s)"),
                                      av_ps[:]).then_inc(oT_ready, 1)

            def normalise_o(c):
                dve.wait_ge(o_done, c + 1)
                o = mix_ps[:].rearrange("p s (h r) -> p s h r", r=32)
                if counts(c):
                    dve.wait_ge(on_ready, c)
                nc.vector.reciprocal(rcp[:], o[:, :, :, DH]).then_inc(rcp_ready, 1)
                dve.wait_ge(rcp_ready, c + 1)
                if counts(c):
                    dve.wait_ge(onT_done, c)
                nc.vector.tensor_tensor(on[:].rearrange("p s (h d) -> p s h d", d=DH), o[:, :, :, 0:DH],
                                        rcp[:].unsqueeze(3).to_broadcast([P, TPS, H, DH]), ALU.mult).then_inc(on_ready, 1)

            def add_x(c):
                dve.wait_ge(out_done, c + 1)
                xs = x[:, bass.ds(c * TPS, TPS), :].rearrange("p s d -> p (s d)")
                nc.vector.tensor_tensor(xs, mix_ps[:, 0, S:2 * S], xs, ALU.add).then_inc(x_added, 1)
                dve.wait_ge(x_added, c + 1)
                for s in range(TPS):
                    last = nc.vector.bn_stats(t["stats"][:, bass.ds(c * TPS + s, 1), :], x[:, bass.ds(c * TPS + s, 1), :])
                last.then_inc(stats_done, 1)

            def prologue():
                nc.vector.memset(mpad[:], 0.0)
                for c in range(2):
                    normalise(c)
                    residual(c)
                take_v(0, 0)
                for k in range(NU):
                    reduce_unit(0, k)
                split_max(0)
                normalise(2)

            def body(b, par, s1=True, s2=True, s4=True):
                if s4:
                    normalise_o(b - 1)
                if s1:
                    residual(b + 2)
                if s2:
                    take_v(b + 1, 1 - par)
                if s4:
                    add_x(b - 1)
                for k in range(NU):
                    if s2:
                        reduce_unit(b + 1, k)
                    if k == 1:
                        take_oT(b, par, 0)
                if s2:
                    split_max(b + 1)
                if s1 and not (isinstance(b, int) and b + 3 >= NSEQ):
                    normalise(b + 3)
                take_oT(b, par, 1)

            def tail(b, par):
                normalise_o(b)
                add_x(b)

            run(dve, body, prologue, tail)

        @block.gpsimd
        def _(pool):
            def other_parts(c):
                pool.wait_ge(part2_ready, c + 1)
                nc.gpsimd.tensor_tensor(parts[:, 2, :, :].rearrange("p a s -> p (a s)"), resid[:],
                                        parts[:, 1, :, :].rearrange("p a s -> p (a s)"),
                                        ALU.subtract).then_inc(parts_ready, 1)

            def prologue():
                other_parts(0)
                other_parts(1)

            def body(b, par, s1=True, s2=True, s4=True):
                if s1:
                    other_parts(b + 2)

            run(pool, body, prologue, lambda b, par: None)

        @block.sync
        def _(sp):
            def store_parts(c, par):
                ready, readers = value(sp, c + 1), value(sp, transfers(c - 2, par, LD))
                sp.wait_ge(parts_ready, ready)
                if counts(readers):
                    sp.wait_ge(stack_loaded[par], readers)
                for a in range(NPART):
                    for w in range(2):
                        sp.dma_start(scratch[par][a, w].rearrange("d h s -> h d s"), parts[:, a, w, :]).then_inc(parts_stored[par], 16)

            def load_stack(c, par):
                stored, read = value(sp, transfers(c, par, WR)), value(sp, NQ * (c - 1))
                sp.wait_ge(parts_stored[par], stored)
                if counts(read):
                    sp.wait_ge(scores_done, read)
                for i in range(NPART):
                    for j in range(NPART):
                        r = (NPART * i + j) * DH
                        for st, w, a in ((qst, 0, i), (kst, 1, j)):
                            sp.dma_start(st[par][r:r + DH, :, :], scratch[par][a, w]).then_inc(stack_loaded[par], 16)

            def prologue():
                for c in range(2):
                    store_parts(c, c)
                    load_stack(c, c)

            def body(b, par, s1=True, s2=True, s4=True):
                if s1:
                    store_parts(b + 2, par)
                    load_stack(b + 2, par)

            run(sp, body, prologue, lambda b, par: None)


E, FF = 8, 512
FC = FF // P
RT = 2 * P
PK = 2 * FF + FC + 1
GT = 4


def n_tiles(slots):
    return (slots * NT * P - E) // RT + E


def route_and_dispatch(nc, t, slots, w, xs):
    NTL, J = n_tiles(slots), slots * NT
    x, mean, rstd, cst = t["x"], t["mean"], t["rstd"], t["cst"]
    rev, thr, tix = cst[:, 0:E], cst[:, E:E + 16], cst[:, E + 16:E + 16 + NTL]
    gates, pos, eidx = t["gates"], t["pos"], t["eidx"]
    with ExitStack() as ctx:
        def sb(name, shape, dt):
            return ctx.enter_context(nc.sbuf_tensor(f"{name}_{w}", shape, dt))

        def ps(name, shape):
            return ctx.enter_context(nc.psum_tensor(f"{name}_{w}", shape, F32))

        def sem(name):
            return ctx.enter_context(nc.semaphore(name))

        xr = [sb(f"xr{i}", [P, GT, D], F32) for i in range(2)]
        xrT = [sb(f"xrT{i}", [P, GT * P], F32) for i in range(2)]
        xall = sb("xall", [P, NT, D], F32)
        lg, cand, l2 = sb("lg", [P, NT, E], F32), sb("cand", [P, NT, E], F32), sb("l2", [P, NT, E], F32)
        top, cmax = sb("top", [P, 2, NT], F32), sb("cmax", [P, NT], F32)
        gtmp = sb("gtmp", [P, 3, NT], F32)
        pick = sb("pick", [P, slots, NT, E], BF16)
        scan = [sb(f"scan{i}", [P, J, E], F32) for i in range(3)]
        place = sb("place", [P, J, E], F32)
        tcmp, tl, start = sb("tcmp", [P, E, 16], F32), sb("tl", [P, E], F32), sb("start", [P, E], F32)
        tscan = [sb(f"tscan{i}", [P, E], F32) for i in range(2)]
        ecmp, ef, posf = sb("ecmp", [P, NTL, E], F32), sb("ef", [P, NTL], F32), sb("posf", [P, J], F32)
        xT_ps = [ps(f"xT_ps{i}", [P, 512]) for i in range(2)]
        lg_ps, pre_ps, tot_ps = ps("lg_ps", [P, NT, E]), ps("pre_ps", [P, J, E]), ps("tot_ps", [P, J, E])

        xr_ready, xr_kept, xT_done, xT_ready = sem("xr_ready"), sem("xr_kept"), sem("xT_done"), sem("xT_ready")
        lg_done, counted = sem("lg_done"), sem("counted")
        gate_in, gate_exp, places_ready, scattered = sem("gate_in"), sem("gate_exp"), sem("places_ready"), sem("scattered")
        step = sem("step")
        block = ctx.enter_context(nc.Block())

        def run(eng, body):
            body(0, 0)
            body(1, 1)
            with eng.Fori(1, NT // GT // 2) as i:
                body(i * 2, 0)
                body(i * 2 + 1, 1)

        @block.vector
        def _(dve):
            def body(g, par):
                if counts(g - 1):
                    dve.wait_ge(xT_done, g - 1)
                if counts(g - 1):
                    dve.wait_ge(xr_kept, g - 1)
                for k in range(GT):
                    i = g * GT + k
                    last = nc.vector.tensor_scalar(xr[par][:, k, :], x[:, bass.ds(i, 1), :].rearrange("p a d -> p (a d)"),
                                                   mean[:, bass.ds(i, 1)], rstd[:, bass.ds(i, 1)], ALU.subtract, ALU.mult)
                last.then_inc(xr_ready, 1)

            run(dve, body)
            done = [0]

            def link(ins):
                done[0] += 1
                ins.then_inc(step, 1)
                dve.wait_ge(step, done[0])

            def over_e(a):
                return a.unsqueeze(2).to_broadcast([P, a.shape[1], E])

            def pick_first(src, k):
                link(nc.vector.reduce_max(top[:, k, :], src[:], axis=AX.X))
                link(nc.vector.tensor_tensor(cand[:], src[:], over_e(top[:, k, :]), ALU.is_equal))
                link(nc.vector.tensor_tensor(cand[:], cand[:], rev.unsqueeze(1).to_broadcast([P, NT, E]), ALU.mult))
                link(nc.vector.reduce_max(cmax[:], cand[:], axis=AX.X))
                link(nc.vector.tensor_tensor(pick[:, k, :, :], cand[:], over_e(cmax[:]), ALU.is_equal))

            dve.wait_ge(lg_done, NT // GT)
            link(nc.vector.tensor_tensor(lg[:], lg_ps[:], t[f"br{w}"][:].unsqueeze(1).to_broadcast([P, NT, E]), ALU.add))
            pick_first(lg, 0)
            if slots == 2:
                link(nc.vector.scalar_tensor_tensor(out=l2[:], in0=pick[:, 0, :, :], scalar=MASKED, in1=lg[:],
                                                    op0=ALU.mult, op1=ALU.add))
                pick_first(l2, 1)
                nc.vector.tensor_tensor(gtmp[:, 0, :], top[:, 1, :], top[:, 0, :], ALU.subtract).then_inc(gate_in, 1)
            else:
                nc.vector.tensor_tensor(l2[:], lg[:], over_e(top[:, 0, :]), ALU.subtract).then_inc(gate_in, 1)
            dve.wait_ge(counted, 1)
            link(nc.vector.tensor_copy(scan[2][:], tot_ps[:]))
            src, dst, k = scan[2], scan[0], 1
            while k < J:
                nc.vector.tensor_copy(dst[:, 0:k, :], src[:, 0:k, :])
                link(nc.vector.tensor_tensor(dst[:, k:J, :], src[:, k:J, :], src[:, 0:J - k, :], ALU.add))
                src, dst, k = dst, (scan[1] if dst is scan[0] else scan[0]), 2 * k
            total = src[:, J - 1, :]
            link(nc.vector.tensor_tensor(tcmp[:], total.unsqueeze(2).to_broadcast([P, E, 16]),
                                         thr.unsqueeze(1).to_broadcast([P, E, 16]), ALU.is_gt))
            link(nc.vector.reduce_sum(tl[:], tcmp[:], axis=AX.X))
            a, b, k = tl, tscan[0], 1
            while k < E:
                nc.vector.tensor_copy(b[:, 0:k], a[:, 0:k])
                link(nc.vector.tensor_tensor(b[:, k:E], a[:, k:E], a[:, 0:E - k], ALU.add))
                a, b, k = b, (tscan[1] if b is tscan[0] else tscan[0]), 2 * k
            ends = a
            link(nc.vector.tensor_tensor(start[:], ends[:], tl[:], ALU.subtract))
            link(nc.vector.tensor_scalar(start[:], start[:], float(RT), None, ALU.mult))
            link(nc.vector.tensor_tensor(place[:], pre_ps[:], src[:], ALU.add))
            link(nc.vector.tensor_tensor(place[:], place[:], scan[2][:], ALU.subtract))
            link(nc.vector.tensor_tensor(place[:], place[:], start[:].unsqueeze(1).to_broadcast([P, J, E]), ALU.add))
            link(nc.vector.tensor_tensor(place[:], place[:], pick[:].rearrange("p k t e -> p (k t) e"), ALU.mult))
            link(nc.vector.reduce_sum(posf[:], place[:], axis=AX.X))
            nc.vector.tensor_copy(pos[:, 0:J], posf[:]).then_inc(places_ready, 1)
            link(nc.vector.tensor_tensor(ecmp[:], ends[:].unsqueeze(1).to_broadcast([P, NTL, E]), over_e(tix), ALU.is_le))
            link(nc.vector.reduce_sum(ef[:], ecmp[:], axis=AX.X))
            nc.vector.tensor_scalar(eidx[:, 0:NTL], ef[:], float(E - 1), None, ALU.min)
            dve.wait_ge(gate_exp, 1)
            if slots == 2:
                link(nc.vector.tensor_scalar(gtmp[:, 2, :], gtmp[:, 1, :], 1.0, None, ALU.add))
                link(nc.vector.reciprocal(gates[:, 0, :], gtmp[:, 2, :]))
                nc.vector.tensor_tensor(gates[:, 1, :], gtmp[:, 1, :], gates[:, 0, :], ALU.mult)
            else:
                link(nc.vector.reduce_sum(gtmp[:, 2, :], cand[:], axis=AX.X))
                nc.vector.reciprocal(gates[:, 0, :], gtmp[:, 2, :])

        @block.scalar
        def _(act):
            def body(g, par):
                act.wait_ge(xT_done, g + 1)
                if counts(g - 1):
                    act.wait_ge(lg_done, g - 1)
                nc.scalar.copy(xrT[par][:], xT_ps[par][:]).then_inc(xT_ready, 1)

            run(act, body)
            act.wait_ge(gate_in, 1)
            if slots == 2:
                nc.scalar.activation(gtmp[:, 1, :], gtmp[:, 0, :], ACT.Exp).then_inc(gate_exp, 1)
            else:
                nc.scalar.activation(cand[:], l2[:], ACT.Exp).then_inc(gate_exp, 1)

        @block.tensor
        def _(pe):
            def body(g, par):
                pe.wait_ge(xr_ready, g + 1)
                if counts(g - 1):
                    pe.wait_ge(xT_ready, g - 1)
                for k in range(GT):
                    last = nc.tensor.transpose(xT_ps[par][:, k * P:(k + 1) * P], xr[par][:, k, :], t["ident"][:])
                last.then_inc(xT_done, 1)
                pe.wait_ge(xT_ready, g + 1)
                for k in range(GT):
                    last = nc.tensor.matmul(lg_ps[:, bass.ds(g * GT + k, 1), :].rearrange("p a e -> p (a e)"),
                                            xrT[par][:, k * P:(k + 1) * P], t[f"wr{w}"][:], start=True, stop=True)
                last.then_inc(lg_done, 1)

            run(pe, body)
            pe.wait_ge(gate_in, 1)
            nc.tensor.matmul(pre_ps[:].rearrange("p j e -> p (j e)"), t["before"][:],
                             pick[:].rearrange("p k t e -> p (k t e)"), start=True, stop=True)
            nc.tensor.matmul(tot_ps[:].rearrange("p j e -> p (j e)"), t["onesb"][:],
                             pick[:].rearrange("p k t e -> p (k t e)"), start=True, stop=True).then_inc(counted, 1)

        @block.gpsimd
        def _(pool):
            def body(g, par):
                pool.wait_ge(xr_ready, g + 1)
                nc.gpsimd.tensor_copy(xall[:, bass.ds(g * GT, GT), :], xr[par][:]).then_inc(xr_kept, 1)

            run(pool, body)
            pool.wait_ge(xr_kept, NT // GT)
            pool.wait_ge(places_ready, 1)
            if w == 0:
                pool.wait_ge(t["zero_filled"], 16 * t["n_fills"])
            for j in range(J):
                nc.gpsimd.indirect_dma_start(out=xs, out_offset=bass.IndirectOffsetOnAxis(ap=pos[:, j:j + 1], axis=0),
                                             in_=xall[:, j % NT, :], in_offset=None).then_inc(scattered, 16)
            pool.wait_ge(scattered, 16 * J)


def experts(nc, t, slots, w, xs, ys):
    NTL = n_tiles(slots)
    ident, wpack, eidx = t["ident"], t[f"wpack{w}"], t["eidx"]
    xs_v = xs[0:NTL * RT, :].rearrange("(i s p) d -> p i s d", s=2, p=P)
    ys_v = ys[0:NTL * RT, :].rearrange("(i s p) d -> p i s d", s=2, p=P)
    with ExitStack() as ctx:
        def sb(name, shape):
            return [ctx.enter_context(nc.sbuf_tensor(f"{name}{i}_{w}", shape, F32)) for i in range(2)]

        def ps(name, shape):
            return ctx.enter_context(nc.psum_tensor(f"{name}_{w}", shape, F32))

        def sem(name):
            return ctx.enter_context(nc.semaphore(name))

        xt, xT, hT, yT, yt = sb("xt", [P, 2, D]), sb("xT", [P, RT]), sb("hT", [P, FC, RT]), sb("yT", [P, RT]), sb("yt", [P, 2, D])
        w1, w2 = sb("w1b", [P, FF + FC]), sb("w2b", [P, FF + 1])
        h_ps = [ps(f"h_ps{i}", [P, 2, 512]) for i in range(2)]
        xT_ps, yT_ps, y_ps = ps("xT_ps", [P, 512]), ps("yT_ps", [P, 512]), ps("y_ps", [P, 512])
        xt_loaded = [sem(f"xt_loaded{i}") for i in range(2)]
        y_stored = [sem(f"y_stored{i}") for i in range(2)]
        xT_done, xT_ready, w1_ready, w2_ready = sem("xT_done"), sem("xT_ready"), sem("w1_ready"), sem("w2_ready")
        h_done, hT_ready, yT_done, yT_ready, y_done, y_ready = (sem("h_done"), sem("hT_ready"), sem("yT_done"),
                                                                sem("yT_ready"), sem("y_done"), sem("y_ready"))
        block = ctx.enter_context(nc.Block())

        def run(eng, body):
            for i in range(4):
                body(i, i % 2)
            with eng.Fori(2, (NTL - 1) // 2) as i:
                body(i * 2, 0)
                body(i * 2 + 1, 1)
            body(NTL - 1, 0)
            body(NTL, 1)
            body(NTL + 1, 0)

        def has(i):
            return not isinstance(i, int) or 0 <= i < NTL

        @block.sync
        def _(sp):
            def load(i, par):
                free = value(sp, i - 1)
                if counts(free):
                    sp.wait_ge(xT_done, free)
                sp.dma_start(xt[par][:], xs_v[:, bass.ds(i, 1)].rearrange("p a s d -> p (a s) d")).then_inc(xt_loaded[par], 16)

            def store(i, par):
                ready = value(sp, i + 1)
                sp.wait_ge(y_ready, ready)
                sp.dma_start(ys_v[:, bass.ds(i, 1)].rearrange("p a s d -> p (a s) d"), yt[par][:]).then_inc(y_stored[par], 16)

            load(0, 0)
            load(1, 1)

            def body(i, par):
                if has(i + 2):
                    load(i + 2, par)
                if has(i - 2):
                    store(i - 2, par)

            for i in range(2):
                body(i, i % 2)
            with sp.Fori(1, (NTL - 3) // 2) as i:
                body(i * 2, 0)
                body(i * 2 + 1, 1)
            for i in range(NTL - 3, NTL + 2):
                body(i, i % 2)
            sp.wait_ge(y_stored[0], 16 * ((NTL + 1) // 2))
            sp.wait_ge(y_stored[1], 16 * (NTL // 2))

        @block.vector
        def _(dve):
            def expert(i):
                return nc.vector.value_load(eidx[0:1, bass.ds(i, 1)], min_val=0, max_val=E - 1)

            def copy_w1(i, par):
                e = expert(i)
                if counts(i - 1):
                    dve.wait_ge(h_done, i - 1)
                if counts(i - 1):
                    dve.wait_ge(hT_ready, i - 1)
                nc.vector.tensor_copy(w1[par][:], wpack[:, bass.ds(e, 1), 0:FF + FC].rearrange("p a f -> p (a f)")).then_inc(w1_ready, 1)

            def copy_w2(i, par):
                e = expert(i)
                if counts(i - 1):
                    dve.wait_ge(yT_done, i - 1)
                if counts(i - 1):
                    dve.wait_ge(yT_ready, i - 1)
                nc.vector.tensor_copy(w2[par][:], wpack[:, bass.ds(e, 1), FF + FC:PK].rearrange("p a f -> p (a f)")).then_inc(w2_ready, 1)

            def take_xT(i, par):
                dve.wait_ge(xT_done, i + 1)
                if counts(i - 1):
                    dve.wait_ge(h_done, i - 1)
                nc.vector.tensor_copy(xT[par][:], xT_ps[:, 0:RT]).then_inc(xT_ready, 1)

            def take_y(i, par):
                dve.wait_ge(y_done, i + 1)
                if not isinstance(i, int) or i >= 2:
                    if counts((i - par) * 8):
                        dve.wait_ge(y_stored[par], (i - par) * 8)
                nc.vector.tensor_copy(yt[par][:].rearrange("p s d -> p (s d)"), y_ps[:, 0:RT]).then_inc(y_ready, 1)

            dve.wait_ge(t["packs_loaded"], 32)
            copy_w1(0, 0)
            take_xT(0, 0)

            def body(i, par):
                if has(i - 2):
                    take_y(i - 2, par)
                if has(i + 1):
                    copy_w1(i + 1, 1 - par)
                    take_xT(i + 1, 1 - par)
                if has(i):
                    copy_w2(i, par)

            run(dve, body)

        @block.scalar
        def _(act):
            def relu(i, par):
                act.wait_ge(h_done, i + 1)
                if counts(i - 1):
                    act.wait_ge(yT_done, i - 1)
                for c in range(FC):
                    last = nc.scalar.activation(hT[par][:, c, :], h_ps[par][:, c // 2, (c % 2) * RT:(c % 2 + 1) * RT],
                                                ACT.Relu, bias=w1[par][:, FF + c:FF + c + 1])
                last.then_inc(hT_ready, 1)

            def take_yT(i, par):
                act.wait_ge(yT_done, i + 1)
                if counts(i - 1):
                    act.wait_ge(y_done, i - 1)
                nc.scalar.activation(yT[par][:], yT_ps[:, 0:RT], ACT.Identity, bias=w2[par][:, FF:FF + 1]).then_inc(yT_ready, 1)

            def body(i, par):
                if has(i):
                    relu(i, par)
                if has(i - 1):
                    take_yT(i - 1, 1 - par)

            run(act, body)

        @block.tensor
        def _(pe):
            def transpose_in(i, par):
                if isinstance(i, int):
                    if counts(16 * (i // 2 + 1)):
                        pe.wait_ge(xt_loaded[par], 16 * (i // 2 + 1))
                else:
                    if counts((i + (2 - par)) * 8):
                        pe.wait_ge(xt_loaded[par], (i + (2 - par)) * 8)
                if counts(i):
                    pe.wait_ge(xT_ready, i)
                for s in range(2):
                    last = nc.tensor.transpose(xT_ps[:, s * P:(s + 1) * P], xt[par][:, s, :], ident[:])
                last.then_inc(xT_done, 1)

            def hidden(i, par):
                pe.wait_ge(xT_ready, i + 1)
                pe.wait_ge(w1_ready, i + 1)
                if counts(i - 1):
                    pe.wait_ge(hT_ready, i - 1)
                for c in range(FC):
                    last = nc.tensor.matmul(h_ps[par][:, c // 2, (c % 2) * RT:(c % 2 + 1) * RT], w1[par][:, c * P:(c + 1) * P],
                                            xT[par][:], start=True, stop=True)
                last.then_inc(h_done, 1)

            def second(i, par):
                pe.wait_ge(hT_ready, i + 1)
                pe.wait_ge(w2_ready, i + 1)
                if counts(i):
                    pe.wait_ge(yT_ready, i)
                for c in range(FC):
                    last = nc.tensor.matmul(yT_ps[:, 0:RT], w2[par][:, c * P:(c + 1) * P], hT[par][:, c, :],
                                            start=(c == 0), stop=(c == FC - 1))
                last.then_inc(yT_done, 1)

            def transpose_back(i, par):
                pe.wait_ge(yT_ready, i + 1)
                if counts(i):
                    pe.wait_ge(y_ready, i)
                for s in range(2):
                    last = nc.tensor.transpose(y_ps[:, s * P:(s + 1) * P], yT[par][:, s * P:(s + 1) * P], ident[:])
                last.then_inc(y_done, 1)

            transpose_in(0, 0)

            def body(i, par):
                if has(i + 1):
                    transpose_in(i + 1, 1 - par)
                if has(i):
                    hidden(i, par)
                if has(i - 2):
                    transpose_back(i - 2, par)
                if has(i - 1):
                    second(i - 1, 1 - par)

            run(pe, body)


def combine(nc, t, slots, w, ys):
    J = slots * NT
    x, pos, gates = t["x"], t["pos"], t["gates"]
    with ExitStack() as ctx:
        back = ctx.enter_context(nc.sbuf_tensor(f"back_{w}", [P, J, D], F32))
        gathered = [ctx.enter_context(nc.semaphore(f"gathered{i}")) for i in range(8)]
        added = ctx.enter_context(nc.semaphore("added"))
        step = ctx.enter_context(nc.semaphore("step"))
        block = ctx.enter_context(nc.Block())

        @block.gpsimd
        def _(pool):
            for i in range(NT):
                for k in range(slots):
                    j = k * NT + i
                    nc.gpsimd.indirect_dma_start(out=back[:, j, :], out_offset=None, in_=ys,
                                                 in_offset=bass.IndirectOffsetOnAxis(ap=pos[:, j:j + 1], axis=0)
                                                 ).then_inc(gathered[i // 4], 16)

        @block.vector
        def _(dve):
            for i in range(NT):
                if i % 4 == 0:
                    dve.wait_ge(gathered[i // 4], 16 * 4 * slots)
                for k in range(slots):
                    nc.vector.scalar_tensor_tensor(out=x[:, i, :], in0=back[:, k * NT + i, :], scalar=gates[:, k, i:i + 1],
                                                   in1=x[:, i, :], op0=ALU.mult, op1=ALU.add).then_inc(added, 1)
                    dve.wait_ge(added, i * slots + k + 1)
                nc.vector.bn_stats(t["stats"][:, i, :], x[:, i, :])


DL = 64


def linear_attention(nc, t):
    x, mean, rstd, ident = t["x"], t["mean"], t["rstd"], t["ident"]
    LAST = 4
    with ExitStack() as ctx:
        def sb(name, shape):
            return [ctx.enter_context(nc.sbuf_tensor(f"{name}{i}", shape, F32)) for i in range(2)]

        def ps(name, shape):
            return ctx.enter_context(nc.psum_tensor(name, shape, F32))

        def sem(name):
            return ctx.enter_context(nc.semaphore(name))

        xn, xnT, kv = sb("lxn", [P, TPS, D]), sb("lxnT", [D, S]), sb("lkv", [P, TPS, 2 * DL])
        qT = [ctx.enter_context(nc.sbuf_tensor(f"lqT{i}", [DL, S], F32)) for i in range(4)]
        eT, f = sb("leT", [DL, P]), sb("lf", [DL, D])
        x_ps, e_ps, f_ps = ps("lx_ps", [P, 512]), ps("le_ps", [P, 512]), ps("lf_ps", [P, 512])
        qkv_ps = [ps(f"lqkv_ps{i}", [P, 512]) for i in range(2)]
        o_ps = [ps(f"lo_ps{i}", [P, 512]) for i in range(2)]
        zeroed, xn_ready, x_done, xnT_ready = sem("zeroed"), sem("xn_ready"), sem("x_done"), sem("xnT_ready")
        qkv_done, qkv_ready, e_done, e_ready = sem("qkv_done"), sem("qkv_ready"), sem("e_done"), sem("e_ready")
        f_done, f_ready, o_done, x_added, stats_done = sem("f_done"), sem("f_ready"), sem("o_done"), sem("x_added"), sem("stats_done")
        block = ctx.enter_context(nc.Block())

        def has(i):
            return not isinstance(i, int) or 0 <= i < NSEQ

        def run(eng, body):
            for i in range(6):
                body(i, i % 4)
            with eng.Fori(1, NSEQ // 4 - 1) as i:
                for r in range(4):
                    body(i * 4 + (2 + r), (2 + r) % 4)
            for i in range(NSEQ - 2, NSEQ + LAST):
                body(i, i % 4)

        @block.vector
        def _(dve):
            def normalise(i, r):
                if counts(i - 1):
                    dve.wait_ge(x_done, i - 1)
                for s in range(TPS):
                    k = i * TPS + s
                    last = nc.vector.tensor_scalar(xn[r % 2][:, s, :], x[:, bass.ds(k, 1), :].rearrange("p a d -> p (a d)"),
                                                   mean[:, bass.ds(k, 1)], rstd[:, bass.ds(k, 1)], ALU.subtract, ALU.mult)
                last.then_inc(xn_ready, 1)

            def add_x(i, r):
                dve.wait_ge(o_done, i + 1)
                xs = x[:, bass.ds(i * TPS, TPS), :].rearrange("p s d -> p (s d)")
                nc.vector.tensor_tensor(xs, o_ps[r % 2][:, 0:S], xs, ALU.add).then_inc(x_added, 1)
                dve.wait_ge(x_added, i + 1)
                for s in range(TPS):
                    last = nc.vector.bn_stats(t["stats"][:, bass.ds(i * TPS + s, 1), :], x[:, bass.ds(i * TPS + s, 1), :])
                last.then_inc(stats_done, 1)

            for i in range(2):
                nc.vector.memset(eT[i][:], 0.0).then_inc(zeroed, 1)
            normalise(0, 0)

            def body(i, r):
                if has(i + 1) and not (isinstance(i, int) and i + 1 >= NSEQ):
                    normalise_next(i, r)
                if has(i - 4):
                    add_x(i - 4, r)

            def normalise_next(i, r):
                normalise(i + 1, r + 1)

            run(dve, body)

        @block.scalar
        def _(act):
            act.wait_ge(zeroed, 2)

            def body(i, r):
                if has(i):
                    act.wait_ge(x_done, i + 1)
                    if counts(i - 1):
                        act.wait_ge(qkv_done, i - 1)
                    nc.scalar.copy(xnT[r % 2][:], x_ps[:, 0:S]).then_inc(xnT_ready, 1)
                if has(i - 1):
                    p = (r + 1) % 2
                    if counts(i):
                        act.wait_ge(qkv_done, i)
                    if counts(i - 3):
                        act.wait_ge(e_done, i - 3)
                    if counts(i - 4):
                        act.wait_ge(o_done, i - 4)
                    nc.scalar.copy(qT[(r + 3) % 4][:], qkv_ps[p][0:DL, 0:S])
                    nc.scalar.copy(kv[p][:].rearrange("p s d -> p (s d)"), qkv_ps[p][:, S:2 * S]).then_inc(qkv_ready, 1)
                if has(i - 2):
                    if counts(i - 1):
                        act.wait_ge(e_done, i - 1)
                    if counts(i - 4):
                        act.wait_ge(f_done, i - 4)
                    nc.scalar.copy(eT[r % 2][:, 0:DL], e_ps[0:DL, 0:DL]).then_inc(e_ready, 1)
                if has(i - 3):
                    if counts(i - 2):
                        act.wait_ge(f_done, i - 2)
                    if counts(i - 4):
                        act.wait_ge(o_done, i - 4)
                    nc.scalar.mul(f[(r + 1) % 2][:], f_ps[0:DL, 0:D], (3.0 / DL) ** 0.5).then_inc(f_ready, 1)

            run(act, body)

        @block.tensor
        def _(pe):
            def body(i, r):
                p, q = r % 2, (r + 1) % 2
                if has(i - 4):
                    if counts(i - 3):
                        pe.wait_ge(f_ready, i - 3)
                    if counts(i - 5):
                        pe.wait_ge(x_added, i - 5)
                    for s in range(TPS):
                        last = nc.tensor.matmul(o_ps[p][:, s * P:(s + 1) * P], qT[r % 4][:, s * P:(s + 1) * P], f[p][:],
                                                start=True, stop=True)
                    last.then_inc(o_done, 1)
                if has(i - 3):
                    if counts(i - 2):
                        pe.wait_ge(e_ready, i - 2)
                    if counts(i - 3):
                        pe.wait_ge(f_ready, i - 3)
                    nc.tensor.matmul(f_ps[:, 0:D], eT[q][:], t["wo1"][:], start=True, stop=True).then_inc(f_done, 1)
                if has(i - 2):
                    if counts(i - 1):
                        pe.wait_ge(qkv_ready, i - 1)
                    if counts(i - 2):
                        pe.wait_ge(e_ready, i - 2)
                    for s in range(TPS):
                        last = nc.tensor.matmul(e_ps[0:DL, 0:DL], kv[p][:, s, DL:2 * DL], kv[p][:, s, 0:DL],
                                                start=(s == 0), stop=(s == TPS - 1))
                    last.then_inc(e_done, 1)
                if has(i - 1):
                    if counts(i):
                        pe.wait_ge(xnT_ready, i)
                    if counts(i - 2):
                        pe.wait_ge(qkv_ready, i - 2)
                    nc.tensor.matmul(qkv_ps[q][0:DL, 0:S], t["wq1"][:], xnT[q][:], start=True, stop=True)
                    for s in range(TPS):
                        last = nc.tensor.matmul(qkv_ps[q][:, S + s * P:S + (s + 1) * P], xnT[q][:, s * P:(s + 1) * P],
                                                t["wkv1"][:], start=True, stop=True)
                    last.then_inc(qkv_done, 1)
                if has(i):
                    pe.wait_ge(xn_ready, i + 1)
                    if counts(i):
                        pe.wait_ge(xnT_ready, i)
                    for s in range(TPS):
                        last = nc.tensor.transpose(x_ps[:, s * P:(s + 1) * P], xn[p][:, s, :], ident[:])
                    last.then_inc(x_done, 1)

            run(pe, body)


def store_out(nc, t, dram):
    with ExitStack() as ctx:
        stored = ctx.enter_context(nc.semaphore("stored"))
        block = ctx.enter_context(nc.Block())

        @block.sync
        def _(sp):
            sp.dma_start(dram["out"].rearrange("(t p) d -> p t d", p=P), t["x"][:]).then_inc(stored, 16)
            sp.wait_ge(stored, 16)


def program(nc, dram, stages=5):
    rows = n_tiles(2) * RT
    xs = nc.dram_tensor("sorted_rows", (rows, D), F32).ap()
    ys = nc.dram_tensor("expert_rows", (rows, D), F32).ap()
    scratch = [nc.dram_tensor(f"parts_scratch{i}", (NPART, 2, DH, H, S), BF16).ap() for i in range(2)]
    with ExitStack() as ctx:
        t = {"zero_filled": ctx.enter_context(nc.semaphore("zero_filled")),
             "packs_loaded": ctx.enter_context(nc.semaphore("packs_loaded"))}

        def alloc(c, *named):
            for name, shape, dt in named:
                t[name] = c.enter_context(nc.sbuf_tensor(name, shape, dt))

        alloc(ctx, ("x", [P, NT, D], F32), ("stats", [P, NT, 6], F32), ("mean", [P, NT], F32), ("rstd", [P, NT], F32),
              ("ntmp", [P, 5, NT], F32), ("eps", [P, 1], F32), ("ident", [P, P], F32), ("identb", [P, P], BF16),
              ("wr0", [D, E], F32), ("br0", [P, E], F32), ("wr1", [D, E], F32), ("br1", [P, E], F32),
              ("cst", [P, E + 16 + n_tiles(2)], F32), ("tri", [P, 2 * P], F32), ("before", [P, P], BF16), ("onesb", [P, P], BF16),
              ("wq1", [D, DL], F32), ("wkv1", [D, 2 * DL], F32), ("wo1", [DL, D], F32),
              ("gates", [P, 2, NT], F32), ("pos", [P, 2 * NT], mybir.dt.uint32), ("eidx", [P, n_tiles(2)], mybir.dt.int32),
              ("wpack0", [P, E, PK], F32), ("wpack1", [P, E, PK], F32))
        with ExitStack() as c1:
            alloc(c1, ("wq0", [D, D], F32), ("wk0", [D, D], F32), ("wv0", [D, D], F32), ("wo0", [D, D], F32),
                  ("mask_qk", [P, 4, P], BF16), ("mask_kq", [P, 4, P], BF16), ("zeros", [P, 6 * D], F32))
            t["qst"] = [c1.enter_context(nc.sbuf_tensor(f"qst{i}", [P, H, S], BF16)) for i in range(2)]
            t["kst"] = [c1.enter_context(nc.sbuf_tensor(f"kst{i}", [P, H, S], BF16)) for i in range(2)]
            t["vaug"] = [c1.enter_context(nc.sbuf_tensor(f"vaug{i}", [P, TPS, H, 32], F32)) for i in range(2)]
            load_inputs(nc, t, dram, xs)
            norm_scales(nc, t, first=True)
            causal_attention(nc, t, scratch)
        if stages >= 2:
            norm_scales(nc, t)
            route_and_dispatch(nc, t, 2, 0, xs)
            experts(nc, t, 2, 0, xs, ys)
            combine(nc, t, 2, 0, ys)
        if stages >= 3:
            norm_scales(nc, t)
            linear_attention(nc, t)
        if stages >= 4:
            norm_scales(nc, t)
            route_and_dispatch(nc, t, 1, 1, xs)
            experts(nc, t, 1, 1, xs, ys)
            combine(nc, t, 1, 1, ys)
        store_out(nc, t, dram)


def kernel(**inputs):
    import numpy as _np
    import concourse.bacc as _bacc
    from concourse.bass_utils import run_bass_kernel_spmd as _run

    def lay(a):
        return _np.ascontiguousarray(a)

    def pack(w1, b1, w2, b2):
        w1, b1, w2, b2 = (_np.asarray(a) for a in (w1, b1, w2, b2))
        parts = [w1, b1.reshape(E, FC, P).transpose(0, 2, 1), w2.reshape(E, FC, P, D).transpose(0, 2, 1, 3).reshape(E, P, FF),
                 b2.reshape(E, P, 1)]
        return lay(_np.concatenate(parts, axis=2).transpose(1, 0, 2))

    nc = _bacc.Bacc("TRN2", target_bir_lowering=False, num_devices=1)
    i = {k: _np.asarray(v) for k, v in inputs.items()}
    x = i["L0_attn_in_features"]
    ntl = n_tiles(2)
    shape_constants = _np.concatenate([E - _np.arange(E), RT * _np.arange(16), _np.arange(ntl)]).astype(_np.float32)
    arrays = {
        "x": lay(x.reshape(NT * P, D)),
        "wq0": lay(i["L0_attn_Wq"].T), "wk0": lay(i["L0_attn_Wk"].T), "wv0": lay(i["L0_attn_Wv"].T), "wo0": lay(i["L0_attn_Wo"].T),
        "wr0": lay(i["L0_ffn_router_w"]), "br0": lay(i["L0_ffn_router_b"].reshape(1, E)),
        "wr1": lay(i["L1_ffn_w_gate"]), "br1": lay(i["L1_ffn_b_gate"].reshape(1, E)),
        "wq1": lay(i["L1_attn_wq"].T), "wkv1": lay(_np.concatenate([i["L1_attn_wk"].T, i["L1_attn_wv"].T], axis=1)),
        "wo1": lay(i["L1_attn_wo"].T),
        "wpack0": pack(i["L0_ffn_w1"], i["L0_ffn_b1"], i["L0_ffn_w2"], i["L0_ffn_b2"]),
        "wpack1": pack(i["L1_ffn_W1"], i["L1_ffn_b1"], i["L1_ffn_W2"], i["L1_ffn_b2"]),
        "cst": lay(_np.broadcast_to(shape_constants, (P, E + 16 + ntl))),
        "tri": lay(_np.concatenate([_np.triu(_np.ones((P, P), _np.float32), 1), _np.ones((P, P), _np.float32)], axis=1)),
    }
    dram = {k: nc.dram_tensor(f"in_{k}", a.shape, mybir.dt.from_np(a.dtype), kind="ExternalInput").ap() for k, a in arrays.items()}
    dram["out"] = nc.dram_tensor("out_x", (NT * P, D), F32, kind="ExternalOutput").ap()
    program(nc, dram)
    r = _run(nc, [{f"in_{k}": a for k, a in arrays.items()}], core_ids=[0])
    return r.results[0]["out_x"].reshape(x.shape)
```

```python
import concourse.bass as bass
from concourse import mybir
from concourse.alu_op_type import AluOpType as ALU
from contextlib import ExitStack

F32 = mybir.dt.float32
BF16 = mybir.dt.bfloat16
ACT = mybir.ActivationFunctionType
AX = mybir.AxisListType

P = 128
NSEQ, S, D = 16, 256, 128
TPS = S // P
NT = NSEQ * TPS
H, DH = 16, 8
NQ = H // 4
EPS = 1e-5
NPART = 3
KS = NPART * NPART * DH
KM = KS + NPART
MASKED = -1e30


def counts(value):
    return not isinstance(value, int) or value > 0


def value(eng, v):
    return v if isinstance(v, int) else eng.to_reg(v)


def load_inputs(nc, t, dram):
    with ExitStack() as ctx:
        loaded = ctx.enter_context(nc.semaphore("loaded"))
        iota_base = ctx.enter_context(nc.semaphore("iota_base"))
        zeroed = ctx.enter_context(nc.semaphore("zeroed"))
        block = ctx.enter_context(nc.Block())

        @block.sync
        def _(sp):
            n = 0
            sp.dma_start(t["x"][:, 0:NT // 2, :], dram["x"].rearrange("(t p) d -> p t d", p=P)[:, 0:NT // 2, :]).then_inc(loaded, 16)
            sp.dma_start(t["x"][:, NT // 2:NT, :], dram["x"].rearrange("(t p) d -> p t d", p=P)[:, NT // 2:NT, :]).then_inc(loaded, 16)
            for name in ("wq0", "wk0", "wv0", "wo0", "wr0", "wr1", "wq1", "wkv1", "wo1", "cst", "tri"):
                sp.dma_start(t[name][:], dram[name]).then_inc(loaded, 16)
                n += 1
            for name in ("br0", "br1"):
                sp.dma_start(t[name][:], dram[name].to_broadcast([P, E])).then_inc(loaded, 16)
                n += 1
            sp.wait_ge(loaded, 16 * (n + 2))
            sp.dma_start(t["wpack0"][:], dram["wpack0"]).then_inc(t["packs_loaded"], 16)

        @block.gpsimd
        def _(pool):
            nc.gpsimd.memset(t["ident"][:], 0.0).then_inc(iota_base, 1)
            nc.gpsimd.memset(t["identb"][:], 0.0).then_inc(iota_base, 1)
            nc.gpsimd.memset(t["mask_qk"][:], 0.0).then_inc(iota_base, 1)
            nc.gpsimd.memset(t["mask_kq"][:], 0.0).then_inc(iota_base, 1)
            pool.wait_ge(iota_base, 4)
            for name in ("ident", "identb"):
                nc.gpsimd.affine_select(out=t[name][:], in_=t[name][:], compare_op=ALU.not_equal, fill=1.0,
                                        base=0, pattern=[[-1, P]], channel_multiplier=1)
            nc.gpsimd.affine_select(out=t["mask_qk"][:], in_=t["mask_qk"][:], compare_op=ALU.is_ge, fill=MASKED,
                                    base=0, pattern=[[0, 4], [-1, P]], channel_multiplier=1)
            nc.gpsimd.affine_select(out=t["mask_kq"][:], in_=t["mask_kq"][:], compare_op=ALU.is_ge, fill=MASKED,
                                    base=0, pattern=[[0, 4], [1, P]], channel_multiplier=-1)

        @block.vector
        def _(dve):
            for kst in t["kst"]:
                nc.vector.memset(kst[64:P, :, :], 1.0)
            for n, vaug in enumerate(t["vaug"]):
                nc.vector.memset(vaug[:], 0.0).then_inc(zeroed, 1)
                dve.wait_ge(zeroed, n + 1)
                nc.vector.memset(vaug[:, :, :, DH:DH + 1], 1.0)
            nc.vector.memset(t["eps"][:], EPS)
            nc.vector.memset(t["zeros"][:], 0.0)
            dve.wait_ge(loaded, 16 * 15)
            nc.vector.tensor_copy(t["before"][:], t["tri"][:, 0:P])
            nc.vector.tensor_copy(t["onesb"][:], t["tri"][:, P:2 * P])


def norm_scales(nc, t, first=False):
    with ExitStack() as ctx:
        step = ctx.enter_context(nc.semaphore("norm_step"))
        var_ready = ctx.enter_context(nc.semaphore("var_ready"))
        std_ready = ctx.enter_context(nc.semaphore("std_ready"))
        block = ctx.enter_context(nc.Block())
        stats, mean, rstd, tmp = t["stats"], t["mean"], t["rstd"], t["ntmp"]
        me, m2e, mo, m2o = stats[:, :, 1], stats[:, :, 2], stats[:, :, 4], stats[:, :, 5]

        @block.vector
        def _(dve):
            if first:
                with dve.Fori(0, NT) as i:
                    nc.vector.bn_stats(stats[:, bass.ds(i, 1), :], t["x"][:, bass.ds(i, 1), :]).then_inc(step, 1)
            base = NT if first else 0
            if counts(base):
                dve.wait_ge(step, base)
            nc.vector.tensor_tensor(mean[:], me, mo, ALU.add)
            nc.vector.tensor_tensor(tmp[:, 0, :], me, mo, ALU.subtract)
            nc.vector.tensor_tensor(tmp[:, 1, :], m2e, m2o, ALU.add).then_inc(step, 1)
            dve.wait_ge(step, base + 1)
            nc.vector.tensor_scalar(mean[:], mean[:], 0.5, None, ALU.mult)
            nc.vector.scalar_tensor_tensor(out=tmp[:, 2, :], in0=tmp[:, 0, :], scalar=0.25, in1=tmp[:, 0, :],
                                           op0=ALU.mult, op1=ALU.mult).then_inc(step, 1)
            dve.wait_ge(step, base + 2)
            nc.vector.scalar_tensor_tensor(out=tmp[:, 3, :], in0=tmp[:, 1, :], scalar=1.0 / D, in1=tmp[:, 2, :],
                                           op0=ALU.mult, op1=ALU.add).then_inc(var_ready, 1)
            dve.wait_ge(std_ready, 1)
            nc.vector.reciprocal(rstd[:], tmp[:, 4, :])

        @block.scalar
        def _(act):
            act.wait_ge(var_ready, 1)
            nc.scalar.activation(tmp[:, 4, :], tmp[:, 3, :], ACT.Sqrt, bias=t["eps"][:]).then_inc(std_ready, 1)


def causal_attention(nc, t, scratch):
    NU = 6
    NB = 4
    WR, LD = 2 * NPART, NPART * NPART + NPART
    x, mean, rstd = t["x"], t["mean"], t["rstd"]
    with ExitStack() as ctx:
        def sb(name, shape, dt):
            return ctx.enter_context(nc.sbuf_tensor(name, shape, dt))

        def sem(name):
            return ctx.enter_context(nc.semaphore(name))

        xn = sb("xn", [P, TPS, D], F32)
        xnT = [sb(f"xnT{i}", [D, S], F32) for i in range(2)]
        parts = sb("parts", [P, NPART, 2, S], BF16)
        resid = sb("resid", [P, 2 * S], F32)
        mx = sb("mx", [P, TPS, H], F32)
        mres = sb("mres", [P, TPS, H], F32)
        mpad = sb("mpad", [P, TPS, P], BF16)
        mparts = mpad[:, :, 0:NPART * H].rearrange("p s (a h) -> p s a h", h=H)
        mT = sb("mT", [NPART * H, S], BF16)
        pT = [sb(f"pT{u}", [P, 3 * 512], F32) for u in range(NQ)]
        oT = [sb(f"oT{i}", [P, NQ, S], F32) for i in range(2)]
        rcp = sb("rcp", [P, TPS, H], F32)
        on = sb("on", [P, TPS, D], F32)
        onT = sb("onT", [D, S], F32)
        qst, kst, vaug = t["qst"], t["kst"], t["vaug"]
        ident, identb = t["ident"], t["identb"]

        max_ps = ctx.enter_context(nc.psum_tensor("max_ps", [P, 2, 512], F32))
        sc_ps = ctx.enter_context(nc.psum_tensor("sc_ps", [P, 3, 512], F32))
        av_ps = ctx.enter_context(nc.psum_tensor("av_ps", [P, 512], F32))
        mix_ps = ctx.enter_context(nc.psum_tensor("mix_ps", [P, 2, 512], F32))

        xn_ready, xnT_done, xnT_ready = sem("xn_ready"), sem("xnT_done"), sem("xnT_ready")
        qk_done, part1_ready, resid_ready = sem("qk_done"), sem("part1_ready"), sem("resid_ready")
        part2_ready, parts_ready = sem("part2_ready"), sem("parts_ready")
        parts_stored = [sem(f"parts_stored{i}") for i in range(2)]
        stack_loaded = [sem(f"stack_loaded{i}") for i in range(NB)]

        def transfers(c, r, n, k):
            return (c + (n - r)) * (k * 16 // n)

        unit_done, unit_reduced = sem("unit_done"), sem("unit_reduced")
        msplit, mparts_ready = sem("msplit"), sem("mparts_ready")
        mT_done, mT_ready, mrows_loaded = sem("mT_done"), sem("mT_ready"), sem("mrows_loaded")
        v_done, v_ready = sem("v_done"), sem("v_ready")
        scores_done, probs_ready, av_done, oT_ready = sem("scores_done"), sem("probs_ready"), sem("av_done"), sem("oT_ready")
        o_done, rcp_ready, on_ready = sem("o_done"), sem("rcp_ready"), sem("on_ready")
        onT_done, onT_ready, out_done, x_added = sem("onT_done"), sem("onT_ready"), sem("out_done"), sem("x_added")
        stats_done = sem("stats_done")

        block = ctx.enter_context(nc.Block())

        def run(eng, body, prologue, tail):
            prologue()
            body(0, 0, s4=False)
            body(1, 1)
            with eng.Fori(0, (NSEQ - 4) // NB) as i:
                for k in range(2, 2 + NB):
                    body(i * NB + k, k % NB)
            body(NSEQ - 2, (NSEQ - 2) % NB, s1=False)
            body(NSEQ - 1, (NSEQ - 1) % NB, s1=False, s2=False)
            tail(NSEQ - 1, (NSEQ - 1) % NB)

        @block.tensor
        def _(pe):
            def transpose_x(c, r, reduced):
                pe.wait_ge(xn_ready, c + 1)
                if reduced is not None:
                    pe.wait_ge(unit_reduced, reduced)
                elif c > 0:
                    pe.wait_ge(xnT_ready, c)
                for s in range(TPS):
                    last = nc.tensor.transpose(max_ps[:, 0, s * P:(s + 1) * P], xn[:, s, :], ident[:])
                last.then_inc(xnT_done, 1)

            def project_qk(c, r, reduced):
                pe.wait_ge(xnT_ready, c + 1)
                if reduced is not None:
                    pe.wait_ge(unit_reduced, reduced)
                elif c > 0:
                    pe.wait_ge(resid_ready, c)
                nc.tensor.matmul(max_ps[:, 1, 0:S], t["wq0"][:], xnT[r % 2][:], start=True, stop=True)
                nc.tensor.matmul(max_ps[:, 1, S:2 * S], t["wk0"][:], xnT[r % 2][:], start=True, stop=True).then_inc(qk_done, 1)

            def project_v(c, r, normed):
                pe.wait_ge(xnT_ready, c + 1)
                if counts(c):
                    pe.wait_ge(v_ready, c)
                if counts(normed):
                    pe.wait_ge(on_ready, normed)
                for s in range(TPS):
                    last = nc.tensor.matmul(mix_ps[:, 1, s * P:(s + 1) * P], xnT[r % 2][:, s * P:(s + 1) * P],
                                            t["wv0"][:], start=True, stop=True)
                last.then_inc(v_done, 1)

            def unit(c, r, k, projected):
                if k == 0:
                    pe.wait_ge(stack_loaded[r], transfers(c, r, NB, LD))
                    if counts(c):
                        pe.wait_ge(mT_ready, c)
                if k < 2:
                    pe.wait_ge(xnT_ready, projected)
                    pe.wait_ge(resid_ready, projected)
                if counts(c * NU + k):
                    pe.wait_ge(unit_reduced, c * NU + k)
                s = 0 if k < 2 else 1
                heads = range(8 * k, 8 * k + 8) if s == 0 else range(4 * (k - 2), 4 * (k - 2) + 4)
                keys = P * (s + 1)
                per_bank = 512 // keys
                for n, h in enumerate(heads):
                    bank = max_ps[:, n // per_bank, :].rearrange("p (h k) -> p h k", k=keys)
                    if n % per_bank == 0:
                        nc.tensor.matmul(bank[:, :, keys - P:keys], identb[:], t["mask_qk"][:, 0:per_bank, :],
                                         start=True, stop=False, skip_group_check=True)
                    last = nc.tensor.matmul(bank[:, n % per_bank, :], qst[r][0:KS, h, s * P:(s + 1) * P],
                                            kst[r][0:KS, h, 0:keys], start=False, stop=True, skip_group_check=True)
                last.then_inc(unit_done, 1)

            def transpose_max(c):
                pe.wait_ge(mparts_ready, c + 1)
                out = max_ps[:, 0, :].bitcast(BF16)
                for s in range(TPS):
                    last = nc.tensor.transpose(out[:, s * P:(s + 1) * P], mpad[:, s, :], identb[:])
                last.then_inc(mT_done, 1)

            def scores(c, r, u):
                if u == 0:
                    pe.wait_ge(stack_loaded[r], transfers(c, r, NB, LD))
                    pe.wait_ge(mrows_loaded, (c + 1) * 16)
                if counts(c * NQ + u):
                    pe.wait_ge(probs_ready, c * NQ + u)
                for bk in range(3):
                    keys = slice(0, P) if bk < 2 else slice(P, S)
                    if bk < 2:
                        diag = sc_ps[:, bk, :].rearrange("p (h q) -> p h q", q=S)[:, :, 0:P]
                        nc.tensor.matmul(diag, identb[:], t["mask_kq"][:, 0:2, :], start=True, stop=False, skip_group_check=True)
                        for n in range(2):
                            h = 4 * u + 2 * bk + n
                            last = nc.tensor.matmul(sc_ps[:, bk, n * S:(n + 1) * S], kst[r][0:KM, h, keys],
                                                    qst[r][0:KM, h, :], start=False, stop=True, skip_group_check=True)
                    else:
                        nc.tensor.matmul(sc_ps[:, 2, :].rearrange("p (h q) -> p h q", q=P), identb[:], t["mask_kq"][:],
                                         start=True, stop=False, skip_group_check=True)
                        for n in range(4):
                            last = nc.tensor.matmul(sc_ps[:, 2, n * P:(n + 1) * P], kst[r][0:KM, 4 * u + n, keys],
                                                    qst[r][0:KM, 4 * u + n, P:S], start=False, stop=True, skip_group_check=True)
                last.then_inc(scores_done, 1)

            def values(c, r, heads):
                for h in heads:
                    u, j = h // 4, h % 4
                    if j == 0:
                        if u == 0:
                            pe.wait_ge(v_ready, c + 1)
                        pe.wait_ge(probs_ready, c * NQ + u + 1)
                        if u % 2 == 0:
                            if counts(c * 2 + u // 2):
                                pe.wait_ge(oT_ready, c * 2 + u // 2)
                    col = (u % 2) * S
                    rows = slice(32 * j, 32 * j + 32)
                    nc.tensor.matmul(av_ps[rows, col:col + S], vaug[r % 2][:, 0, h, :], pT[u][:, j * S:(j + 1) * S],
                                     start=True, stop=False, tile_position=(0, 32 * j))
                    last = nc.tensor.matmul(av_ps[rows, col + P:col + S], vaug[r % 2][:, 1, h, :],
                                            pT[u][:, 4 * S + j * P:4 * S + (j + 1) * P], start=False, stop=True,
                                            tile_position=(0, 32 * j))
                    if j == 3:
                        last.then_inc(av_done, 1)

            def transpose_o(c, r):
                pe.wait_ge(oT_ready, 2 * (c + 1))
                if counts(c):
                    pe.wait_ge(x_added, c)
                if counts(t_v(c)):
                    pe.wait_ge(v_ready, t_v(c))
                for s in range(TPS):
                    for u in range(NQ):
                        last = nc.tensor.transpose(mix_ps[:, s, u * P:(u + 1) * P], oT[r % 2][:, u, s * P:(s + 1) * P], ident[:])
                last.then_inc(o_done, 1)

            def t_v(c):
                return c + 2 if not isinstance(c, int) else min(c + 2, NSEQ)

            def transpose_on(c):
                pe.wait_ge(on_ready, c + 1)
                for s in range(TPS):
                    last = nc.tensor.transpose(mix_ps[:, 0, s * P:(s + 1) * P], on[:, s, :], ident[:])
                last.then_inc(onT_done, 1)

            def project_out(c):
                pe.wait_ge(onT_ready, c + 1)
                for s in range(TPS):
                    last = nc.tensor.matmul(mix_ps[:, 0, S + s * P:S + (s + 1) * P], onT[:, s * P:(s + 1) * P],
                                            t["wo0"][:], start=True, stop=True)
                last.then_inc(out_done, 1)

            def prologue():
                for c in range(2):
                    transpose_x(c, c, None)
                    project_qk(c, c, None)
                project_v(0, 0, 0)
                for k in range(NU):
                    unit(0, 0, k, 2)
                transpose_max(0)

            def body(b, r, s1=True, s2=True, s4=True):
                before, after, later = (r - 1) % NB, (r + 1) % NB, (r + 2) % NB
                seen = b + 3 if s1 else NSEQ

                def next_unit(k):
                    if s2:
                        unit(b + 1, after, k, seen if k else b + 2)

                if s4:
                    values(b - 1, before, range(12, 14))
                    transpose_max(b)
                    values(b - 1, before, range(14, 15))
                next_unit(0)
                if s4:
                    values(b - 1, before, range(15, 16))
                if s1:
                    transpose_x(b + 2, later, NU * (b + 1) + 1)
                scores(b, r, 0)
                if s1:
                    project_qk(b + 2, later, NU * (b + 1) + 1)
                if s4:
                    transpose_o(b - 1, before)
                scores(b, r, 1)
                next_unit(1)
                values(b, r, range(0, 2))
                next_unit(2)
                values(b, r, range(2, 4))
                scores(b, r, 2)
                values(b, r, range(4, 6))
                next_unit(3)
                values(b, r, range(6, 8))
                if s4:
                    transpose_on(b - 1)
                next_unit(4)
                scores(b, r, 3)
                next_unit(5)
                values(b, r, range(8, 12))
                if s2:
                    project_v(b + 1, after, b)
                if s4:
                    project_out(b - 1)

            def tail(b, r):
                values(b, r, range(12, 16))
                transpose_o(b, r)
                transpose_on(b)
                project_out(b)

            run(pe, body, prologue, tail)

        @block.scalar
        def _(act):
            def copy_xT(c, r):
                act.wait_ge(xnT_done, c + 1)
                if counts(c - 1):
                    act.wait_ge(v_done, c - 1)
                if counts(c - 1):
                    act.wait_ge(qk_done, c - 1)
                nc.scalar.copy(xnT[r % 2][:], max_ps[:, 0, 0:S]).then_inc(xnT_ready, 1)

            def first_part(c, r):
                act.wait_ge(qk_done, c + 1)
                if counts(c):
                    act.wait_ge(parts_stored[1 - r % 2], transfers(c - 1, 1 - r % 2, 2, WR))
                nc.scalar.copy(parts[:, 0, :, :].rearrange("p a s -> p (a s)"), max_ps[:, 1, :]).then_inc(part1_ready, 1)

            def copy_mT(c, r):
                act.wait_ge(mT_done, c + 1)
                if counts(c * 16):
                    act.wait_ge(mrows_loaded, c * 16)
                nc.scalar.copy(mT[:], max_ps[:, 0, :].bitcast(BF16)[0:NPART * H, 0:S]).then_inc(mT_ready, 1)
                act.wait_ge(mT_ready, c + 1)
                if counts(NQ * (c - 3)):
                    act.wait_ge(scores_done, NQ * (c - 3))
                act.dma_start(qst[r][KS:KM, :, :], mT[:]).then_inc(mrows_loaded, 16)

            def exp(c, u):
                act.wait_ge(scores_done, c * NQ + u + 1)
                if counts((c - 1) * NQ + u + 1):
                    act.wait_ge(av_done, (c - 1) * NQ + u + 1)
                nc.scalar.activation(pT[u][:], sc_ps[:].rearrange("p a s -> p (a s)"), ACT.Exp,
                                     scale=float(DH) ** -0.5).then_inc(probs_ready, 1)

            def copy_onT(c):
                act.wait_ge(onT_done, c + 1)
                if counts(c):
                    act.wait_ge(out_done, c)
                nc.scalar.copy(onT[:], mix_ps[:, 0, 0:S]).then_inc(onT_ready, 1)

            def prologue():
                for c in range(2):
                    copy_xT(c, c)
                    first_part(c, c)
                copy_mT(0, 0)

            def body(b, r, s1=True, s2=True, s4=True):
                if s1:
                    copy_xT(b + 2, (r + 2) % NB)
                exp(b, 0)
                if s1:
                    first_part(b + 2, (r + 2) % NB)
                exp(b, 1)
                exp(b, 2)
                if s4:
                    copy_onT(b - 1)
                exp(b, 3)
                if s2:
                    copy_mT(b + 1, (r + 1) % NB)

            def tail(b, r):
                copy_onT(b)

            run(act, body, prologue, tail)

        @block.vector
        def _(dve):
            def normalise(c):
                if counts(c):
                    dve.wait_ge(xnT_done, c)
                for s in range(TPS):
                    i = c * TPS + s
                    last = nc.vector.tensor_scalar(xn[:, s, :], x[:, bass.ds(i, 1), :].rearrange("p a d -> p (a d)"),
                                                   mean[:, bass.ds(i, 1)], rstd[:, bass.ds(i, 1)], ALU.subtract, ALU.mult)
                last.then_inc(xn_ready, 1)

            def residual(c):
                dve.wait_ge(part1_ready, c + 1)
                if counts(c):
                    dve.wait_ge(parts_ready, c)
                nc.vector.tensor_tensor(resid[:], max_ps[:, 1, :], parts[:, 0, :, :].rearrange("p a s -> p (a s)"),
                                        ALU.subtract).then_inc(resid_ready, 1)
                dve.wait_ge(resid_ready, c + 1)
                nc.vector.tensor_copy(parts[:, 1, :, :].rearrange("p a s -> p (a s)"), resid[:]).then_inc(part2_ready, 1)

            def take_v(c, r):
                dve.wait_ge(v_done, c + 1)
                if counts(NQ * (c - 1)):
                    dve.wait_ge(av_done, NQ * (c - 1))
                nc.vector.tensor_copy(vaug[r % 2][:, :, :, 0:DH].rearrange("p s h d -> p (s h) d"),
                                      mix_ps[:, 1, 0:S].rearrange("p (g d) -> p g d", d=DH)).then_inc(v_ready, 1)

            def reduce_unit(c, k):
                dve.wait_ge(unit_done, c * NU + k + 1)
                if k == 0:
                    if counts(3 * c):
                        dve.wait_ge(msplit, 3 * c)
                    if counts(c):
                        dve.wait_ge(mparts_ready, c)
                s = 0 if k < 2 else 1
                h0, n = (8 * k, 8) if s == 0 else (4 * (k - 2), 4)
                nc.vector.reduce_max(mx[:, s, h0:h0 + n],
                                     max_ps[:].rearrange("p a s -> p (a s)").rearrange("p (h k) -> p h k", h=n),
                                     axis=AX.X).then_inc(unit_reduced, 1)

            def split_max(c):
                dve.wait_ge(unit_reduced, NU * (c + 1))
                if counts(c):
                    dve.wait_ge(mT_done, c)
                nc.vector.tensor_scalar(mparts[:, :, 0, :], mx[:], -1.0, None, ALU.mult).then_inc(msplit, 1)
                dve.wait_ge(msplit, 3 * c + 1)
                nc.vector.scalar_tensor_tensor(out=mres[:], in0=mx[:], scalar=-1.0, in1=mparts[:, :, 0, :],
                                               op0=ALU.mult, op1=ALU.subtract).then_inc(msplit, 1)
                dve.wait_ge(msplit, 3 * c + 2)
                nc.vector.tensor_copy(mparts[:, :, 1, :], mres[:]).then_inc(msplit, 1)
                dve.wait_ge(msplit, 3 * c + 3)
                nc.vector.tensor_tensor(mparts[:, :, 2, :], mres[:], mparts[:, :, 1, :], ALU.subtract).then_inc(mparts_ready, 1)

            def take_oT(c, r, pair):
                dve.wait_ge(av_done, NQ * c + 2 * pair + 2)
                if counts(c - 1):
                    dve.wait_ge(o_done, c - 1)
                nc.vector.tensor_copy(oT[r % 2][:, 2 * pair:2 * pair + 2, :].rearrange("p u s -> p (u s)"),
                                      av_ps[:]).then_inc(oT_ready, 1)

            def normalise_o(c):
                dve.wait_ge(o_done, c + 1)
                o = mix_ps[:].rearrange("p s (h r) -> p s h r", r=32)
                if counts(c):
                    dve.wait_ge(on_ready, c)
                nc.vector.reciprocal(rcp[:], o[:, :, :, DH]).then_inc(rcp_ready, 1)
                dve.wait_ge(rcp_ready, c + 1)
                if counts(c):
                    dve.wait_ge(onT_done, c)
                nc.vector.tensor_tensor(on[:].rearrange("p s (h d) -> p s h d", d=DH), o[:, :, :, 0:DH],
                                        rcp[:].unsqueeze(3).to_broadcast([P, TPS, H, DH]), ALU.mult).then_inc(on_ready, 1)

            def add_x(c):
                dve.wait_ge(out_done, c + 1)
                xs = x[:, bass.ds(c * TPS, TPS), :].rearrange("p s d -> p (s d)")
                nc.vector.tensor_tensor(xs, mix_ps[:, 0, S:2 * S], xs, ALU.add).then_inc(x_added, 1)
                dve.wait_ge(x_added, c + 1)
                for s in range(TPS):
                    last = nc.vector.bn_stats(t["stats"][:, bass.ds(c * TPS + s, 1), :], x[:, bass.ds(c * TPS + s, 1), :])
                last.then_inc(stats_done, 1)

            def prologue():
                nc.vector.memset(mpad[:], 0.0)
                for c in range(2):
                    normalise(c)
                    residual(c)
                take_v(0, 0)
                for k in range(NU):
                    reduce_unit(0, k)
                split_max(0)

            def body(b, r, s1=True, s2=True, s4=True):
                def next_unit(k):
                    if s2:
                        reduce_unit(b + 1, k)

                if s1:
                    normalise(b + 2)
                next_unit(0)
                if s4:
                    take_oT(b - 1, (r - 1) % NB, 1)
                if s1:
                    residual(b + 2)
                if s4:
                    normalise_o(b - 1)
                next_unit(1)
                next_unit(2)
                next_unit(3)
                take_oT(b, r, 0)
                next_unit(4)
                next_unit(5)
                if s2:
                    split_max(b + 1)
                    take_v(b + 1, (r + 1) % NB)
                if s4:
                    add_x(b - 1)

            def tail(b, r):
                take_oT(b, r, 1)
                normalise_o(b)
                add_x(b)

            run(dve, body, prologue, tail)

        @block.gpsimd
        def _(pool):
            def other_parts(c):
                pool.wait_ge(part2_ready, c + 1)
                nc.gpsimd.tensor_tensor(parts[:, 2, :, :].rearrange("p a s -> p (a s)"), resid[:],
                                        parts[:, 1, :, :].rearrange("p a s -> p (a s)"),
                                        ALU.subtract).then_inc(parts_ready, 1)

            def prologue():
                other_parts(0)
                other_parts(1)

            def body(b, r, s1=True, s2=True, s4=True):
                if s1:
                    other_parts(b + 2)

            def fill(b, r):
                for xs in t["sorted"]:
                    dst = xs.rearrange("(n s p) d -> p n s d", p=P, s=TPS)
                    for n in range(dst.shape[1]):
                        pool.dma_start(dst[:, n], t["zeros"][:]).then_inc(t["zero_filled"], 16)

            run(pool, body, prologue, fill)

        @block.sync
        def _(sp):
            def store_parts(c, r):
                p = r % 2
                ready, readers = value(sp, c + 1), value(sp, transfers(c - 2, (r - 2) % NB, NB, LD))
                sp.wait_ge(parts_ready, ready)
                if counts(readers):
                    sp.wait_ge(stack_loaded[(r - 2) % NB], readers)
                for w in range(2):
                    for a in range(NPART):
                        sp.dma_start(scratch[p][w, a].rearrange("d h s -> h d s"), parts[:, a, w, :]).then_inc(parts_stored[p], 16)

            def load_stack(c, r):
                p = r % 2
                stored, read = value(sp, transfers(c, p, 2, WR)), value(sp, NQ * (c - 3))
                sp.wait_ge(parts_stored[p], stored)
                if counts(read):
                    sp.wait_ge(scores_done, read)
                for i in range(NPART):
                    rows = slice(NPART * i * DH, NPART * (i + 1) * DH)
                    sp.dma_start(kst[r][rows, :, :], scratch[p][1].rearrange("a d h s -> (a d) (h s)")).then_inc(stack_loaded[r], 16)
                    for j in range(NPART):
                        rows = slice((NPART * i + j) * DH, (NPART * i + j + 1) * DH)
                        sp.dma_start(qst[r][rows, :, :], scratch[p][0, i]).then_inc(stack_loaded[r], 16)

            def prologue():
                for c in range(2):
                    store_parts(c, c)
                    load_stack(c, c)

            def body(b, r, s1=True, s2=True, s4=True):
                if s1:
                    store_parts(b + 2, (r + 2) % NB)
                    load_stack(b + 2, (r + 2) % NB)

            run(sp, body, prologue, lambda b, r: None)


E, FF = 8, 512
FC = FF // P
RT = 2 * P
PK = 2 * FF + FC + 1
RW = D + 1
NOWHERE = 1 << 20
GT = 4


def n_tiles(slots):
    return (slots * NT * P - E) // RT + E


def route_and_dispatch(nc, t, slots, w):
    NTL, J, xs = n_tiles(slots), slots * NT, t["sorted"][w]
    x, mean, rstd, cst = t["x"], t["mean"], t["rstd"], t["cst"]
    rev, thr, tix = cst[:, 0:E], cst[:, E:E + 16], cst[:, E + 16:E + 16 + NTL]
    gates, pos, eidx = t["gates"], t["pos"], t["eidx"]
    with ExitStack() as ctx:
        def sb(name, shape, dt):
            return ctx.enter_context(nc.sbuf_tensor(f"{name}_{w}", shape, dt))

        def ps(name, shape):
            return ctx.enter_context(nc.psum_tensor(f"{name}_{w}", shape, F32))

        def sem(name):
            return ctx.enter_context(nc.semaphore(name))

        xr = [sb(f"xr{i}", [P, GT, D], F32) for i in range(2)]
        xrT = [sb(f"xrT{i}", [P, GT * P], F32) for i in range(2)]
        xall = sb("xall", [P, NT, RW], F32)
        lg, cand, l2 = sb("lg", [P, NT, E], F32), sb("cand", [P, NT, E], F32), sb("l2", [P, NT, E], F32)
        top, cmax = sb("top", [P, 2, NT], F32), sb("cmax", [P, NT], F32)
        gtmp = sb("gtmp", [P, 3, NT], F32)
        pick = sb("pick", [P, slots, NT, E], BF16)
        scan = [sb(f"scan{i}", [P, J, E], F32) for i in range(3)]
        place = sb("place", [P, J, E], F32)
        tcmp, tl, start = sb("tcmp", [P, E, 16], F32), sb("tl", [P, E], F32), sb("start", [P, E], F32)
        tscan = [sb(f"tscan{i}", [P, E], F32) for i in range(2)]
        ecmp, ef, posf = sb("ecmp", [P, NTL, E], F32), sb("ef", [P, NTL], F32), sb("posf", [P, J], F32)
        xT_ps = [ps(f"xT_ps{i}", [P, 512]) for i in range(2)]
        lg_ps, pre_ps, tot_ps = ps("lg_ps", [P, NT, E]), ps("pre_ps", [P, J, E]), ps("tot_ps", [P, J, E])

        xr_ready, xr_kept, xT_done, xT_ready = sem("xr_ready"), sem("xr_kept"), sem("xT_done"), sem("xT_ready")
        lg_done, counted = sem("lg_done"), sem("counted")
        gate_in, gate_exp, places_ready, scattered = sem("gate_in"), sem("gate_exp"), sem("places_ready"), sem("scattered")
        step = sem("step")
        block = ctx.enter_context(nc.Block())

        def run(eng, body):
            body(0, 0)
            body(1, 1)
            with eng.Fori(1, NT // GT // 2) as i:
                body(i * 2, 0)
                body(i * 2 + 1, 1)

        @block.vector
        def _(dve):
            def body(g, par):
                if counts(g - 1):
                    dve.wait_ge(xT_done, g - 1)
                if counts(g - 1):
                    dve.wait_ge(xr_kept, g - 1)
                for k in range(GT):
                    i = g * GT + k
                    last = nc.vector.tensor_scalar(xr[par][:, k, :], x[:, bass.ds(i, 1), :].rearrange("p a d -> p (a d)"),
                                                   mean[:, bass.ds(i, 1)], rstd[:, bass.ds(i, 1)], ALU.subtract, ALU.mult)
                last.then_inc(xr_ready, 1)

            run(dve, body)
            done = [0]

            def link(ins):
                done[0] += 1
                ins.then_inc(step, 1)
                dve.wait_ge(step, done[0])

            def over_e(a):
                return a.unsqueeze(2).to_broadcast([P, a.shape[1], E])

            def pick_first(src, k):
                link(nc.vector.reduce_max(top[:, k, :], src[:], axis=AX.X))
                link(nc.vector.tensor_tensor(cand[:], src[:], over_e(top[:, k, :]), ALU.is_equal))
                link(nc.vector.tensor_tensor(cand[:], cand[:], rev.unsqueeze(1).to_broadcast([P, NT, E]), ALU.mult))
                link(nc.vector.reduce_max(cmax[:], cand[:], axis=AX.X))
                link(nc.vector.tensor_tensor(pick[:, k, :, :], cand[:], over_e(cmax[:]), ALU.is_equal))

            dve.wait_ge(lg_done, NT // GT)
            link(nc.vector.tensor_tensor(lg[:], lg_ps[:], t[f"br{w}"][:].unsqueeze(1).to_broadcast([P, NT, E]), ALU.add))
            pick_first(lg, 0)
            if slots == 2:
                link(nc.vector.scalar_tensor_tensor(out=l2[:], in0=pick[:, 0, :, :], scalar=MASKED, in1=lg[:],
                                                    op0=ALU.mult, op1=ALU.add))
                pick_first(l2, 1)
                nc.vector.tensor_tensor(gtmp[:, 0, :], top[:, 1, :], top[:, 0, :], ALU.subtract).then_inc(gate_in, 1)
            else:
                nc.vector.tensor_tensor(l2[:], lg[:], over_e(top[:, 0, :]), ALU.subtract).then_inc(gate_in, 1)
            dve.wait_ge(counted, 1)
            link(nc.vector.tensor_copy(scan[2][:], tot_ps[:]))
            src, dst, k = scan[2], scan[0], 1
            while k < J:
                nc.vector.tensor_copy(dst[:, 0:k, :], src[:, 0:k, :])
                link(nc.vector.tensor_tensor(dst[:, k:J, :], src[:, k:J, :], src[:, 0:J - k, :], ALU.add))
                src, dst, k = dst, (scan[1] if dst is scan[0] else scan[0]), 2 * k
            total = src[:, J - 1, :]
            link(nc.vector.tensor_tensor(tcmp[:], total.unsqueeze(2).to_broadcast([P, E, 16]),
                                         thr.unsqueeze(1).to_broadcast([P, E, 16]), ALU.is_gt))
            link(nc.vector.reduce_sum(tl[:], tcmp[:], axis=AX.X))
            a, b, k = tl, tscan[0], 1
            while k < E:
                nc.vector.tensor_copy(b[:, 0:k], a[:, 0:k])
                link(nc.vector.tensor_tensor(b[:, k:E], a[:, k:E], a[:, 0:E - k], ALU.add))
                a, b, k = b, (tscan[1] if b is tscan[0] else tscan[0]), 2 * k
            ends = a
            link(nc.vector.tensor_tensor(start[:], ends[:], tl[:], ALU.subtract))
            link(nc.vector.tensor_scalar(start[:], start[:], float(RT), None, ALU.mult))
            link(nc.vector.tensor_tensor(place[:], pre_ps[:], src[:], ALU.add))
            link(nc.vector.tensor_tensor(place[:], place[:], scan[2][:], ALU.subtract))
            link(nc.vector.tensor_tensor(place[:], place[:], start[:].unsqueeze(1).to_broadcast([P, J, E]), ALU.add))
            link(nc.vector.tensor_tensor(place[:], place[:], pick[:].rearrange("p k t e -> p (k t) e"), ALU.mult))
            link(nc.vector.reduce_sum(posf[:], place[:], axis=AX.X))
            nc.vector.tensor_copy(pos[:, 0:J], posf[:]).then_inc(places_ready, 1)
            link(nc.vector.tensor_tensor(ecmp[:], ends[:].unsqueeze(1).to_broadcast([P, NTL, E]), over_e(tix), ALU.is_le))
            link(nc.vector.reduce_sum(ef[:], ecmp[:], axis=AX.X))
            nc.vector.tensor_scalar(eidx[:, 0:NTL], ef[:], float(E - 1), None, ALU.min)
            dve.wait_ge(gate_exp, 1)
            if slots == 2:
                link(nc.vector.tensor_scalar(gtmp[:, 2, :], gtmp[:, 1, :], 1.0, None, ALU.add))
                link(nc.vector.reciprocal(gates[:, 0, :], gtmp[:, 2, :]))
                nc.vector.tensor_tensor(gates[:, 1, :], gtmp[:, 1, :], gates[:, 0, :], ALU.mult)
            else:
                link(nc.vector.reduce_sum(gtmp[:, 2, :], cand[:], axis=AX.X))
                nc.vector.reciprocal(gates[:, 0, :], gtmp[:, 2, :])

        @block.scalar
        def _(act):
            def body(g, par):
                act.wait_ge(xT_done, g + 1)
                if counts(g - 1):
                    act.wait_ge(lg_done, g - 1)
                nc.scalar.copy(xrT[par][:], xT_ps[par][:]).then_inc(xT_ready, 1)

            run(act, body)
            act.wait_ge(gate_in, 1)
            if slots == 2:
                nc.scalar.activation(gtmp[:, 1, :], gtmp[:, 0, :], ACT.Exp).then_inc(gate_exp, 1)
            else:
                nc.scalar.activation(cand[:], l2[:], ACT.Exp).then_inc(gate_exp, 1)

        @block.tensor
        def _(pe):
            def body(g, par):
                pe.wait_ge(xr_ready, g + 1)
                if counts(g - 1):
                    pe.wait_ge(xT_ready, g - 1)
                for k in range(GT):
                    last = nc.tensor.transpose(xT_ps[par][:, k * P:(k + 1) * P], xr[par][:, k, :], t["ident"][:])
                last.then_inc(xT_done, 1)
                pe.wait_ge(xT_ready, g + 1)
                for k in range(GT):
                    last = nc.tensor.matmul(lg_ps[:, bass.ds(g * GT + k, 1), :].rearrange("p a e -> p (a e)"),
                                            xrT[par][:, k * P:(k + 1) * P], t[f"wr{w}"][:], start=True, stop=True)
                last.then_inc(lg_done, 1)

            run(pe, body)
            pe.wait_ge(gate_in, 1)
            nc.tensor.matmul(pre_ps[:].rearrange("p j e -> p (j e)"), t["before"][:],
                             pick[:].rearrange("p k t e -> p (k t e)"), start=True, stop=True)
            nc.tensor.matmul(tot_ps[:].rearrange("p j e -> p (j e)"), t["onesb"][:],
                             pick[:].rearrange("p k t e -> p (k t e)"), start=True, stop=True).then_inc(counted, 1)

        @block.gpsimd
        def _(pool):
            def body(g, par):
                pool.wait_ge(xr_ready, g + 1)
                nc.gpsimd.tensor_copy(xall[:, bass.ds(g * GT, GT), 0:D], xr[par][:]).then_inc(xr_kept, 1)

            run(pool, body)
            nc.gpsimd.tensor_copy(xall[:, :, D], cst[:, E + 16 + n_tiles(2):]).then_inc(xr_kept, 1)
            pool.wait_ge(xr_kept, NT // GT + 1)
            pool.wait_ge(places_ready, 1)
            pool.wait_ge(t["zero_filled"], 16 * (n_tiles(1) + n_tiles(2)))
            for j in range(J):
                if j == NT:
                    pool.wait_ge(scattered, 16 * NT)
                    nc.gpsimd.tensor_scalar(xall[:, :, D], xall[:, :, D], float(NT * P), None, ALU.add).then_inc(xr_kept, 1)
                    pool.wait_ge(xr_kept, NT // GT + 2)
                nc.gpsimd.indirect_dma_start(out=xs, out_offset=bass.IndirectOffsetOnAxis(ap=pos[:, j:j + 1], axis=0),
                                             in_=xall[:, j % NT, :], in_offset=None).then_inc(scattered, 16)
            pool.wait_ge(scattered, 16 * J)


def experts(nc, t, slots, w, ys):
    NTL, xs = n_tiles(slots), t["sorted"][w]
    ident, wpack, eidx = t["ident"], t[f"wpack{w}"], t["eidx"]
    xs_v = xs[0:NTL * RT, :].rearrange("(i s p) d -> p i s d", s=2, p=P)
    with ExitStack() as ctx:
        def sb(name, shape):
            return [ctx.enter_context(nc.sbuf_tensor(f"{name}{i}_{w}", shape, F32)) for i in range(2)]

        def ps(name, shape):
            return ctx.enter_context(nc.psum_tensor(f"{name}_{w}", shape, F32))

        def sem(name):
            return ctx.enter_context(nc.semaphore(name))

        xt, xT, hT, yT, yt = sb("xt", [P, 2, RW]), sb("xT", [P, RT]), sb("hT", [P, FC, RT]), sb("yT", [P, RT]), sb("yt", [P, 2, D])
        w1, w2 = sb("w1b", [P, FF + FC]), sb("w2b", [P, FF + 1])
        goes = ctx.enter_context(nc.sbuf_tensor(f"goes_{w}", [P, NTL, 2], F32))
        places = [ctx.enter_context(nc.sbuf_tensor(f"places{i}_{w}", [P, 2], mybir.dt.uint32)) for i in range(2)]
        h_ps = [ps(f"h_ps{i}", [P, 2, 512]) for i in range(2)]
        xT_ps, yT_ps, y_ps = ps("xT_ps", [P, 512]), ps("yT_ps", [P, 512]), ps("y_ps", [P, 512])
        xt_loaded = [sem(f"xt_loaded{i}") for i in range(2)]
        y_stored = [sem(f"y_stored{i}") for i in range(2)]
        xT_done, xT_ready, w1_ready, w2_ready = sem("xT_done"), sem("xT_ready"), sem("w1_ready"), sem("w2_ready")
        goes_kept = sem("goes_kept")
        h_done, hT_ready, yT_done, yT_ready, y_done, y_ready = (sem("h_done"), sem("hT_ready"), sem("yT_done"),
                                                                sem("yT_ready"), sem("y_done"), sem("y_ready"))
        block = ctx.enter_context(nc.Block())

        def run(eng, body):
            for i in range(4):
                body(i, i % 2)
            with eng.Fori(2, (NTL - 1) // 2) as i:
                body(i * 2, 0)
                body(i * 2 + 1, 1)
            body(NTL - 1, 0)
            body(NTL, 1)
            body(NTL + 1, 0)

        def has(i):
            return not isinstance(i, int) or 0 <= i < NTL

        @block.sync
        def _(sp):
            def load(i, par):
                free, kept = value(sp, i - 1), value(sp, i - 1)
                if counts(free):
                    sp.wait_ge(xT_done, free)
                    sp.wait_ge(goes_kept, kept)
                sp.dma_start(xt[par][:], xs_v[:, bass.ds(i, 1)].rearrange("p a s d -> p (a s) d")).then_inc(xt_loaded[par], 16)

            load(0, 0)
            load(1, 1)

            def body(i, par):
                load(i + 2, par)

            for i in range(2):
                body(i, i % 2)
            with sp.Fori(1, (NTL - 3) // 2) as i:
                body(i * 2, 0)
                body(i * 2 + 1, 1)
            body(NTL - 3, (NTL - 3) % 2)

        @block.gpsimd
        def _(pool):
            last_place = pool.to_reg(slots * NT * P - 1)

            def scatter(i, par):
                ready = value(pool, i + 1)
                pool.wait_ge(xt_loaded[0], 16)
                pool.wait_ge(y_ready, ready)
                for s in range(2):
                    nc.gpsimd.indirect_dma_start(out=ys, out_offset=bass.IndirectOffsetOnAxis(ap=places[par][:, s:s + 1], axis=0),
                                                 in_=yt[par][:, s, :], in_offset=None, bounds_check=last_place,
                                                 oob_is_err=False).then_inc(y_stored[par], 16)

            scatter(0, 0)
            with pool.Fori(0, (NTL - 1) // 2) as i:
                scatter(i * 2 + 1, 1)
                scatter(i * 2 + 2, 0)
            for par in range(2):
                pool.wait_ge(y_stored[par], 32 * ((NTL + 1 - par) // 2))

        @block.vector
        def _(dve):
            def expert(i):
                return nc.vector.value_load(eidx[0:1, bass.ds(i, 1)], min_val=0, max_val=E - 1)

            def copy_w1(i, par):
                e = expert(i)
                if counts(i - 1):
                    dve.wait_ge(h_done, i - 1)
                if counts(i - 1):
                    dve.wait_ge(hT_ready, i - 1)
                nc.vector.tensor_copy(w1[par][:], wpack[:, bass.ds(e, 1), 0:FF + FC].rearrange("p a f -> p (a f)")).then_inc(w1_ready, 1)

            def copy_w2(i, par):
                e = expert(i)
                if counts(i - 1):
                    dve.wait_ge(yT_done, i - 1)
                if counts(i - 1):
                    dve.wait_ge(yT_ready, i - 1)
                nc.vector.tensor_copy(w2[par][:], wpack[:, bass.ds(e, 1), FF + FC:PK].rearrange("p a f -> p (a f)")).then_inc(w2_ready, 1)

            def take_xT(i, par):
                dve.wait_ge(xT_done, i + 1)
                if counts(i - 1):
                    dve.wait_ge(h_done, i - 1)
                nc.vector.tensor_copy(xT[par][:], xT_ps[:, 0:RT]).then_inc(xT_ready, 1)
                nc.vector.tensor_copy(goes[:, bass.ds(i, 1), :].rearrange("p a s -> p (a s)"), xt[par][:, :, D]).then_inc(goes_kept, 1)

            def take_y(i, par):
                dve.wait_ge(y_done, i + 1)
                if not isinstance(i, int) or i >= 2:
                    dve.wait_ge(y_stored[par], (i - par) * 16)
                nc.vector.tensor_scalar(places[par][:], goes[:, bass.ds(i, 1), :].rearrange("p a s -> p (a s)"),
                                        float(NOWHERE), None, ALU.add)
                nc.vector.tensor_copy(yt[par][:].rearrange("p s d -> p (s d)"), y_ps[:, 0:RT]).then_inc(y_ready, 1)

            dve.wait_ge(t["packs_loaded"], 16 * (w + 1))
            copy_w1(0, 0)
            take_xT(0, 0)

            def body(i, par):
                if has(i - 2):
                    take_y(i - 2, par)
                if has(i + 1):
                    copy_w1(i + 1, 1 - par)
                    take_xT(i + 1, 1 - par)
                if has(i):
                    copy_w2(i, par)

            run(dve, body)

        @block.scalar
        def _(act):
            def relu(i, par):
                act.wait_ge(h_done, i + 1)
                if counts(i - 1):
                    act.wait_ge(yT_done, i - 1)
                for c in range(FC):
                    last = nc.scalar.activation(hT[par][:, c, :], h_ps[par][:, c // 2, (c % 2) * RT:(c % 2 + 1) * RT],
                                                ACT.Relu, bias=w1[par][:, FF + c:FF + c + 1])
                last.then_inc(hT_ready, 1)

            def take_yT(i, par):
                act.wait_ge(yT_done, i + 1)
                if counts(i - 1):
                    act.wait_ge(y_done, i - 1)
                nc.scalar.activation(yT[par][:], yT_ps[:, 0:RT], ACT.Identity, bias=w2[par][:, FF:FF + 1]).then_inc(yT_ready, 1)

            def body(i, par):
                if has(i):
                    relu(i, par)
                if has(i - 1):
                    take_yT(i - 1, 1 - par)

            run(act, body)

        @block.tensor
        def _(pe):
            def transpose_in(i, par):
                if isinstance(i, int):
                    if counts(16 * (i // 2 + 1)):
                        pe.wait_ge(xt_loaded[par], 16 * (i // 2 + 1))
                else:
                    if counts((i + (2 - par)) * 8):
                        pe.wait_ge(xt_loaded[par], (i + (2 - par)) * 8)
                if counts(i):
                    pe.wait_ge(xT_ready, i)
                for s in range(2):
                    last = nc.tensor.transpose(xT_ps[:, s * P:(s + 1) * P], xt[par][:, s, 0:D], ident[:])
                last.then_inc(xT_done, 1)

            def hidden(i, par):
                pe.wait_ge(xT_ready, i + 1)
                pe.wait_ge(w1_ready, i + 1)
                if counts(i - 1):
                    pe.wait_ge(hT_ready, i - 1)
                for c in range(FC):
                    last = nc.tensor.matmul(h_ps[par][:, c // 2, (c % 2) * RT:(c % 2 + 1) * RT], w1[par][:, c * P:(c + 1) * P],
                                            xT[par][:], start=True, stop=True)
                last.then_inc(h_done, 1)

            def second(i, par):
                pe.wait_ge(hT_ready, i + 1)
                pe.wait_ge(w2_ready, i + 1)
                if counts(i):
                    pe.wait_ge(yT_ready, i)
                for c in range(FC):
                    last = nc.tensor.matmul(yT_ps[:, 0:RT], w2[par][:, c * P:(c + 1) * P], hT[par][:, c, :],
                                            start=(c == 0), stop=(c == FC - 1))
                last.then_inc(yT_done, 1)

            def transpose_back(i, par):
                pe.wait_ge(yT_ready, i + 1)
                if counts(i):
                    pe.wait_ge(y_ready, i)
                for s in range(2):
                    last = nc.tensor.transpose(y_ps[:, s * P:(s + 1) * P], yT[par][:, s * P:(s + 1) * P], ident[:])
                last.then_inc(y_done, 1)

            transpose_in(0, 0)

            def body(i, par):
                if has(i + 1):
                    transpose_in(i + 1, 1 - par)
                if has(i):
                    hidden(i, par)
                if has(i - 2):
                    transpose_back(i - 2, par)
                if has(i - 1):
                    second(i - 1, 1 - par)

            run(pe, body)


def combine(nc, t, slots, w, ys):
    x, gates = t["x"], t["gates"]
    NCH = 8
    CT = NT // NCH
    ys_v = ys.rearrange("(k c t p) d -> k c p t d", k=2, c=NCH, p=P)
    with ExitStack() as ctx:
        back = ctx.enter_context(nc.sbuf_tensor(f"back_{w}", [P, slots, NT, D], F32))
        loaded = [ctx.enter_context(nc.semaphore(f"loaded{i}")) for i in range(NCH)]
        added = ctx.enter_context(nc.semaphore("added"))
        block = ctx.enter_context(nc.Block())

        @block.sync
        def _(sp):
            for c in range(NCH):
                for k in range(slots):
                    sp.dma_start(back[:, k, c * CT:(c + 1) * CT, :], ys_v[k, c]).then_inc(loaded[c], 16)

        @block.vector
        def _(dve):
            for i in range(NT):
                if i % CT == 0:
                    dve.wait_ge(loaded[i // CT], 16 * slots)
                for k in range(slots):
                    nc.vector.scalar_tensor_tensor(out=x[:, i, :], in0=back[:, k, i, :], scalar=gates[:, k, i:i + 1],
                                                   in1=x[:, i, :], op0=ALU.mult, op1=ALU.add).then_inc(added, 1)
                    dve.wait_ge(added, i * slots + k + 1)
                nc.vector.bn_stats(t["stats"][:, i, :], x[:, i, :])


DL = 64


def linear_attention(nc, t, dram):
    x, mean, rstd, ident = t["x"], t["mean"], t["rstd"], t["ident"]
    LAST = 4
    with ExitStack() as ctx:
        def sb(name, shape):
            return [ctx.enter_context(nc.sbuf_tensor(f"{name}{i}", shape, F32)) for i in range(2)]

        def ps(name, shape):
            return ctx.enter_context(nc.psum_tensor(name, shape, F32))

        def sem(name):
            return ctx.enter_context(nc.semaphore(name))

        xn, xnT, kv = sb("lxn", [P, TPS, D]), sb("lxnT", [D, S]), sb("lkv", [P, TPS, 2 * DL])
        qT = [ctx.enter_context(nc.sbuf_tensor(f"lqT{i}", [DL, S], F32)) for i in range(4)]
        eT, f = sb("leT", [DL, P]), sb("lf", [DL, D])
        x_ps, e_ps, f_ps = ps("lx_ps", [P, 512]), ps("le_ps", [P, 512]), ps("lf_ps", [P, 512])
        qkv_ps = [ps(f"lqkv_ps{i}", [P, 512]) for i in range(2)]
        o_ps = [ps(f"lo_ps{i}", [P, 512]) for i in range(2)]
        zeroed, xn_ready, x_done, xnT_ready = sem("zeroed"), sem("xn_ready"), sem("x_done"), sem("xnT_ready")
        qkv_done, qkv_ready, e_done, e_ready = sem("qkv_done"), sem("qkv_ready"), sem("e_done"), sem("e_ready")
        f_done, f_ready, o_done, x_added, stats_done = sem("f_done"), sem("f_ready"), sem("o_done"), sem("x_added"), sem("stats_done")
        block = ctx.enter_context(nc.Block())

        def has(i):
            return not isinstance(i, int) or 0 <= i < NSEQ

        def run(eng, body):
            for i in range(6):
                body(i, i % 4)
            with eng.Fori(1, NSEQ // 4 - 1) as i:
                for r in range(4):
                    body(i * 4 + (2 + r), (2 + r) % 4)
            for i in range(NSEQ - 2, NSEQ + LAST):
                body(i, i % 4)

        @block.sync
        def _(sp):
            sp.dma_start(t["wpack1"][:], dram["wpack1"]).then_inc(t["packs_loaded"], 16)

        @block.vector
        def _(dve):
            def normalise(i, r):
                if counts(i - 1):
                    dve.wait_ge(x_done, i - 1)
                for s in range(TPS):
                    k = i * TPS + s
                    last = nc.vector.tensor_scalar(xn[r % 2][:, s, :], x[:, bass.ds(k, 1), :].rearrange("p a d -> p (a d)"),
                                                   mean[:, bass.ds(k, 1)], rstd[:, bass.ds(k, 1)], ALU.subtract, ALU.mult)
                last.then_inc(xn_ready, 1)

            def add_x(i, r):
                dve.wait_ge(o_done, i + 1)
                xs = x[:, bass.ds(i * TPS, TPS), :].rearrange("p s d -> p (s d)")
                nc.vector.tensor_tensor(xs, o_ps[r % 2][:, 0:S], xs, ALU.add).then_inc(x_added, 1)
                dve.wait_ge(x_added, i + 1)
                for s in range(TPS):
                    last = nc.vector.bn_stats(t["stats"][:, bass.ds(i * TPS + s, 1), :], x[:, bass.ds(i * TPS + s, 1), :])
                last.then_inc(stats_done, 1)

            for i in range(2):
                nc.vector.memset(eT[i][:], 0.0).then_inc(zeroed, 1)
            normalise(0, 0)

            def body(i, r):
                if has(i + 1) and not (isinstance(i, int) and i + 1 >= NSEQ):
                    normalise_next(i, r)
                if has(i - 4):
                    add_x(i - 4, r)

            def normalise_next(i, r):
                normalise(i + 1, r + 1)

            run(dve, body)

        @block.scalar
        def _(act):
            act.wait_ge(zeroed, 2)

            def body(i, r):
                if has(i):
                    act.wait_ge(x_done, i + 1)
                    if counts(i - 1):
                        act.wait_ge(qkv_done, i - 1)
                    nc.scalar.copy(xnT[r % 2][:], x_ps[:, 0:S]).then_inc(xnT_ready, 1)
                if has(i - 1):
                    p = (r + 1) % 2
                    if counts(i):
                        act.wait_ge(qkv_done, i)
                    if counts(i - 3):
                        act.wait_ge(e_done, i - 3)
                    if counts(i - 4):
                        act.wait_ge(o_done, i - 4)
                    nc.scalar.copy(qT[(r + 3) % 4][:], qkv_ps[p][0:DL, 0:S])
                    nc.scalar.copy(kv[p][:].rearrange("p s d -> p (s d)"), qkv_ps[p][:, S:2 * S]).then_inc(qkv_ready, 1)
                if has(i - 2):
                    if counts(i - 1):
                        act.wait_ge(e_done, i - 1)
                    if counts(i - 4):
                        act.wait_ge(f_done, i - 4)
                    nc.scalar.copy(eT[r % 2][:, 0:DL], e_ps[0:DL, 0:DL]).then_inc(e_ready, 1)
                if has(i - 3):
                    if counts(i - 2):
                        act.wait_ge(f_done, i - 2)
                    if counts(i - 4):
                        act.wait_ge(o_done, i - 4)
                    nc.scalar.mul(f[(r + 1) % 2][:], f_ps[0:DL, 0:D], (3.0 / DL) ** 0.5).then_inc(f_ready, 1)

            run(act, body)

        @block.tensor
        def _(pe):
            def body(i, r):
                p, q = r % 2, (r + 1) % 2
                if has(i - 4):
                    if counts(i - 3):
                        pe.wait_ge(f_ready, i - 3)
                    if counts(i - 5):
                        pe.wait_ge(x_added, i - 5)
                    for s in range(TPS):
                        last = nc.tensor.matmul(o_ps[p][:, s * P:(s + 1) * P], qT[r % 4][:, s * P:(s + 1) * P], f[p][:],
                                                start=True, stop=True)
                    last.then_inc(o_done, 1)
                if has(i - 3):
                    if counts(i - 2):
                        pe.wait_ge(e_ready, i - 2)
                    if counts(i - 3):
                        pe.wait_ge(f_ready, i - 3)
                    nc.tensor.matmul(f_ps[:, 0:D], eT[q][:], t["wo1"][:], start=True, stop=True).then_inc(f_done, 1)
                if has(i - 2):
                    if counts(i - 1):
                        pe.wait_ge(qkv_ready, i - 1)
                    if counts(i - 2):
                        pe.wait_ge(e_ready, i - 2)
                    for s in range(TPS):
                        last = nc.tensor.matmul(e_ps[0:DL, 0:DL], kv[p][:, s, DL:2 * DL], kv[p][:, s, 0:DL],
                                                start=(s == 0), stop=(s == TPS - 1))
                    last.then_inc(e_done, 1)
                if has(i - 1):
                    if counts(i):
                        pe.wait_ge(xnT_ready, i)
                    if counts(i - 2):
                        pe.wait_ge(qkv_ready, i - 2)
                    nc.tensor.matmul(qkv_ps[q][0:DL, 0:S], t["wq1"][:], xnT[q][:], start=True, stop=True)
                    for s in range(TPS):
                        last = nc.tensor.matmul(qkv_ps[q][:, S + s * P:S + (s + 1) * P], xnT[q][:, s * P:(s + 1) * P],
                                                t["wkv1"][:], start=True, stop=True)
                    last.then_inc(qkv_done, 1)
                if has(i):
                    pe.wait_ge(xn_ready, i + 1)
                    if counts(i):
                        pe.wait_ge(xnT_ready, i)
                    for s in range(TPS):
                        last = nc.tensor.transpose(x_ps[:, s * P:(s + 1) * P], xn[p][:, s, :], ident[:])
                    last.then_inc(x_done, 1)

            run(pe, body)


def store_out(nc, t, dram):
    with ExitStack() as ctx:
        stored = ctx.enter_context(nc.semaphore("stored"))
        block = ctx.enter_context(nc.Block())

        @block.sync
        def _(sp):
            sp.dma_start(dram["out"].rearrange("(t p) d -> p t d", p=P), t["x"][:]).then_inc(stored, 16)
            sp.wait_ge(stored, 16)


def program(nc, dram, stages=5):
    ys = nc.dram_tensor("expert_rows", (2 * NT * P, D), F32).ap()
    scratch = [nc.dram_tensor(f"parts_scratch{i}", (2, NPART, DH, H, S), BF16).ap() for i in range(2)]
    with ExitStack() as ctx:
        t = {"sorted": [nc.dram_tensor(f"sorted_rows{w}", (n_tiles(2 - w) * RT, RW), F32).ap() for w in range(2)],
             "zero_filled": ctx.enter_context(nc.semaphore("zero_filled")),
             "packs_loaded": ctx.enter_context(nc.semaphore("packs_loaded"))}

        def alloc(c, *named):
            for name, shape, dt in named:
                t[name] = c.enter_context(nc.sbuf_tensor(name, shape, dt))

        alloc(ctx, ("x", [P, NT, D], F32), ("stats", [P, NT, 6], F32), ("mean", [P, NT], F32), ("rstd", [P, NT], F32),
              ("ntmp", [P, 5, NT], F32), ("eps", [P, 1], F32), ("ident", [P, P], F32), ("identb", [P, P], BF16),
              ("wr0", [D, E], F32), ("br0", [P, E], F32), ("wr1", [D, E], F32), ("br1", [P, E], F32),
              ("cst", [P, E + 16 + n_tiles(2) + NT], F32), ("tri", [P, 2 * P], F32), ("before", [P, P], BF16), ("onesb", [P, P], BF16),
              ("wq1", [D, DL], F32), ("wkv1", [D, 2 * DL], F32), ("wo1", [DL, D], F32),
              ("gates", [P, 2, NT], F32), ("pos", [P, 2 * NT], mybir.dt.uint32), ("eidx", [P, n_tiles(2)], mybir.dt.int32),
              ("wpack0", [P, E, PK], F32))
        with ExitStack() as c1:
            alloc(c1, ("wq0", [D, D], F32), ("wk0", [D, D], F32), ("wv0", [D, D], F32), ("wo0", [D, D], F32),
                  ("mask_qk", [P, 4, P], BF16), ("mask_kq", [P, 4, P], BF16), ("zeros", [P, TPS, RW], F32))
            t["qst"] = [c1.enter_context(nc.sbuf_tensor(f"qst{i}", [P, H, S], BF16)) for i in range(4)]
            t["kst"] = [c1.enter_context(nc.sbuf_tensor(f"kst{i}", [P, H, S], BF16)) for i in range(4)]
            t["vaug"] = [c1.enter_context(nc.sbuf_tensor(f"vaug{i}", [P, TPS, H, 32], F32)) for i in range(2)]
            load_inputs(nc, t, dram)
            norm_scales(nc, t, first=True)
            causal_attention(nc, t, scratch)
        alloc(ctx, ("wpack1", [P, E, PK], F32))
        if stages >= 2:
            norm_scales(nc, t)
            route_and_dispatch(nc, t, 2, 0)
            experts(nc, t, 2, 0, ys)
            combine(nc, t, 2, 0, ys)
        if stages >= 3:
            norm_scales(nc, t)
            linear_attention(nc, t, dram)
        if stages >= 4:
            norm_scales(nc, t)
            route_and_dispatch(nc, t, 1, 1)
            experts(nc, t, 1, 1, ys)
            combine(nc, t, 1, 1, ys)
        store_out(nc, t, dram)


def kernel(**inputs):
    import numpy as _np
    import concourse.bacc as _bacc
    from concourse.bass_utils import run_bass_kernel_spmd as _run

    def lay(a):
        return _np.ascontiguousarray(a)

    def pack(w1, b1, w2, b2):
        w1, b1, w2, b2 = (_np.asarray(a) for a in (w1, b1, w2, b2))
        parts = [w1, b1.reshape(E, FC, P).transpose(0, 2, 1), w2.reshape(E, FC, P, D).transpose(0, 2, 1, 3).reshape(E, P, FF),
                 b2.reshape(E, P, 1)]
        return lay(_np.concatenate(parts, axis=2).transpose(1, 0, 2))

    nc = _bacc.Bacc("TRN2", target_bir_lowering=False, num_devices=1)
    i = {k: _np.asarray(v) for k, v in inputs.items()}
    x = i["L0_attn_in_features"]
    ntl = n_tiles(2)
    shape_constants = _np.broadcast_to(_np.concatenate([E - _np.arange(E), RT * _np.arange(16), _np.arange(ntl)]), (P, E + 16 + ntl))
    token_ids = _np.arange(NT * P).reshape(NT, P).T - NOWHERE
    arrays = {
        "x": lay(x.reshape(NT * P, D)),
        "wq0": lay(i["L0_attn_Wq"].T), "wk0": lay(i["L0_attn_Wk"].T), "wv0": lay(i["L0_attn_Wv"].T), "wo0": lay(i["L0_attn_Wo"].T),
        "wr0": lay(i["L0_ffn_router_w"]), "br0": lay(i["L0_ffn_router_b"].reshape(1, E)),
        "wr1": lay(i["L1_ffn_w_gate"]), "br1": lay(i["L1_ffn_b_gate"].reshape(1, E)),
        "wq1": lay(i["L1_attn_wq"].T), "wkv1": lay(_np.concatenate([i["L1_attn_wk"].T, i["L1_attn_wv"].T], axis=1)),
        "wo1": lay(i["L1_attn_wo"].T),
        "wpack0": pack(i["L0_ffn_w1"], i["L0_ffn_b1"], i["L0_ffn_w2"], i["L0_ffn_b2"]),
        "wpack1": pack(i["L1_ffn_W1"], i["L1_ffn_b1"], i["L1_ffn_W2"], i["L1_ffn_b2"]),
        "cst": lay(_np.concatenate([shape_constants, token_ids], axis=1).astype(_np.float32)),
        "tri": lay(_np.concatenate([_np.triu(_np.ones((P, P), _np.float32), 1), _np.ones((P, P), _np.float32)], axis=1)),
    }
    dram = {k: nc.dram_tensor(f"in_{k}", a.shape, mybir.dt.from_np(a.dtype), kind="ExternalInput").ap() for k, a in arrays.items()}
    dram["out"] = nc.dram_tensor("out_x", (NT * P, D), F32, kind="ExternalOutput").ap()
    program(nc, dram)
    r = _run(nc, [{f"in_{k}": a for k, a in arrays.items()}], core_ids=[0])
    return r.results[0]["out_x"].reshape(x.shape)
```

```python
import concourse.bass as bass
from concourse import mybir
from concourse.alu_op_type import AluOpType as ALU
from contextlib import ExitStack

F32 = mybir.dt.float32
BF16 = mybir.dt.bfloat16
I32 = mybir.dt.int32
ACT = mybir.ActivationFunctionType
AX = mybir.AxisListType

P = 128
NSEQ, S, D = 16, 256, 128
TPS = S // P
NT = NSEQ * TPS
H, DH = 16, 8
NQ = H // 4
EPS = 1e-5
NPART = 3
KS = NPART * NPART * DH
KM = KS + NPART
MASKED = -1e30


def counts(value):
    return not isinstance(value, int) or value > 0


def value(eng, v):
    return v if isinstance(v, int) else eng.to_reg(v)


def load_inputs(nc, t, dram):
    with ExitStack() as ctx:
        loaded = ctx.enter_context(nc.semaphore("loaded"))
        iota_base = ctx.enter_context(nc.semaphore("iota_base"))
        zeroed = ctx.enter_context(nc.semaphore("zeroed"))
        x_loaded = [ctx.enter_context(nc.semaphore(f"x_loaded{i}")) for i in range(2)]
        block = ctx.enter_context(nc.Block())

        @block.sync
        def _(sp):
            n = 0
            for half in range(2):
                tiles = slice(half * NT // 2, (half + 1) * NT // 2)
                sp.dma_start(t["x"][:, tiles, :], dram["x"].rearrange("(t p) d -> p t d", p=P)[:, tiles, :]).then_inc(x_loaded[half], 16)
            for name in ("wq0", "wk0", "wv0", "wo0", "wr0", "wr1", "wq1", "wkv1", "wo1", "cst", "tri"):
                sp.dma_start(t[name][:], dram[name]).then_inc(loaded, 16)
                n += 1
            for name in ("br0", "br1"):
                sp.dma_start(t[name][:], dram[name].to_broadcast([P, E])).then_inc(loaded, 16)
                n += 1
            sp.wait_ge(loaded, 16 * n)
            sp.dma_start(t["wpack0"][:], dram["wpack0"]).then_inc(t["packs_loaded"], 16)

        @block.gpsimd
        def _(pool):
            nc.gpsimd.memset(t["ident"][:], 0.0).then_inc(iota_base, 1)
            nc.gpsimd.memset(t["identb"][:], 0.0).then_inc(iota_base, 1)
            nc.gpsimd.memset(t["mask_qk"][:], 0.0).then_inc(iota_base, 1)
            nc.gpsimd.memset(t["mask_kq"][:], 0.0).then_inc(iota_base, 1)
            pool.wait_ge(iota_base, 4)
            for name in ("ident", "identb"):
                nc.gpsimd.affine_select(out=t[name][:], in_=t[name][:], compare_op=ALU.not_equal, fill=1.0,
                                        base=0, pattern=[[-1, P]], channel_multiplier=1).then_inc(iota_base, 1)
            nc.gpsimd.affine_select(out=t["mask_qk"][:], in_=t["mask_qk"][:], compare_op=ALU.is_ge, fill=MASKED,
                                    base=0, pattern=[[0, 4], [-1, P]], channel_multiplier=1).then_inc(iota_base, 1)
            nc.gpsimd.affine_select(out=t["mask_kq"][:], in_=t["mask_kq"][:], compare_op=ALU.is_ge, fill=MASKED,
                                    base=0, pattern=[[0, 4], [1, P]], channel_multiplier=-1).then_inc(iota_base, 1)
            pool.wait_ge(iota_base, 8)
            for kst in t["kst"]:
                nc.gpsimd.memset(kst[64:96, :, :], 1.0)

        @block.vector
        def _(dve):
            for n, vaug in enumerate(t["vaug"]):
                nc.vector.memset(vaug[:], 0.0).then_inc(zeroed, 1)
                dve.wait_ge(zeroed, n + 1)
                nc.vector.memset(vaug[:, :, :, DH:DH + 1], 1.0)
            nc.vector.memset(t["eps"][:], EPS)
            for half in range(2):
                dve.wait_ge(x_loaded[half], 16)
                for i in range(half * NT // 2, (half + 1) * NT // 2):
                    nc.vector.bn_stats(t["stats"][:, i, :], t["x"][:, i, :])
            dve.wait_ge(loaded, 16 * 13)
            nc.vector.tensor_copy(t["before"][:], t["tri"][:, 0:P])
            nc.vector.tensor_copy(t["onesb"][:], t["tri"][:, P:2 * P])
            nc.vector.tensor_copy(t["iotab"][:], t["cst"][:, E + 17 + n_tiles(2):])
            nc.vector.tensor_scalar(t["afterb"][:], t["cst"][:, E + 17 + n_tiles(2):], 1.0, None, ALU.add)


def norm_scales(nc, t):
    with ExitStack() as ctx:
        step = ctx.enter_context(nc.semaphore("norm_step"))
        var_ready = ctx.enter_context(nc.semaphore("var_ready"))
        std_ready = ctx.enter_context(nc.semaphore("std_ready"))
        block = ctx.enter_context(nc.Block())
        stats, mean, rstd, tmp = t["stats"], t["mean"], t["rstd"], t["ntmp"]
        me, m2e, mo, m2o = stats[:, :, 1], stats[:, :, 2], stats[:, :, 4], stats[:, :, 5]

        @block.vector
        def _(dve):
            nc.vector.tensor_tensor(mean[:], me, mo, ALU.add)
            nc.vector.tensor_tensor(tmp[:, 0, :], me, mo, ALU.subtract)
            nc.vector.tensor_tensor(tmp[:, 1, :], m2e, m2o, ALU.add).then_inc(step, 1)
            dve.wait_ge(step, 1)
            nc.vector.tensor_scalar(mean[:], mean[:], 0.5, None, ALU.mult)
            nc.vector.scalar_tensor_tensor(out=tmp[:, 2, :], in0=tmp[:, 0, :], scalar=0.25, in1=tmp[:, 0, :],
                                           op0=ALU.mult, op1=ALU.mult).then_inc(step, 1)
            dve.wait_ge(step, 2)
            nc.vector.scalar_tensor_tensor(out=tmp[:, 3, :], in0=tmp[:, 1, :], scalar=1.0 / D, in1=tmp[:, 2, :],
                                           op0=ALU.mult, op1=ALU.add).then_inc(var_ready, 1)
            dve.wait_ge(std_ready, 1)
            nc.vector.reciprocal(rstd[:], tmp[:, 4, :])

        @block.scalar
        def _(act):
            act.wait_ge(var_ready, 1)
            nc.scalar.activation(tmp[:, 4, :], tmp[:, 3, :], ACT.Sqrt, bias=t["eps"][:]).then_inc(std_ready, 1)


def causal_attention(nc, t, scratch):
    NU = 12
    NB = 4
    WR, LD = 1, 1 + NPART
    x, mean, rstd = t["x"], t["mean"], t["rstd"]
    with ExitStack() as ctx:
        def sb(name, shape, dt):
            return ctx.enter_context(nc.sbuf_tensor(name, shape, dt))

        def sem(name):
            return ctx.enter_context(nc.semaphore(name))

        xn = sb("xn", [P, TPS, D], F32)
        xnT = [sb(f"xnT{i}", [D, S], F32) for i in range(2)]
        parts = sb("parts", [P, 2, NPART, S], BF16)
        resid = sb("resid", [P, 2, S], F32)
        mx = sb("mx", [P, TPS, H], F32)
        mres = sb("mres", [P, TPS, H], F32)
        mpad = sb("mpad", [P, TPS, P], BF16)
        mparts = mpad[:, :, 0:NPART * H].rearrange("p s (a h) -> p s a h", h=H)
        mT = sb("mT", [NPART * H, S], BF16)
        pT = [sb(f"pT{u}", [P, 3 * 512], F32) for u in range(NQ)]
        oT = [sb(f"oT{i}", [P, NQ, S], F32) for i in range(2)]
        rcp = sb("rcp", [P, TPS, H], F32)
        on = sb("on", [P, TPS, D], F32)
        onT = sb("onT", [D, S], F32)
        qst, kst, vaug = t["qst"], t["kst"], t["vaug"]
        ident, identb = t["ident"], t["identb"]

        max_ps = ctx.enter_context(nc.psum_tensor("max_ps", [P, 2, 512], F32))
        sc_ps = ctx.enter_context(nc.psum_tensor("sc_ps", [P, 3, 512], F32))
        av_ps = ctx.enter_context(nc.psum_tensor("av_ps", [P, 512], F32))
        mix_ps = ctx.enter_context(nc.psum_tensor("mix_ps", [P, 2, 512], F32))

        xn_ready, xnT_done, xnT_ready = sem("xn_ready"), sem("xnT_done"), sem("xnT_ready")
        qk_done, part1_ready, resid_ready = sem("qk_done"), sem("part1_ready"), sem("resid_ready")
        part2_ready, parts_ready = sem("part2_ready"), sem("parts_ready")
        parts_stored = [sem(f"parts_stored{i}") for i in range(2)]
        stack_loaded = [sem(f"stack_loaded{i}") for i in range(NB)]

        def transfers(c, r, n, k):
            return (c + (n - r)) * (k * 16 // n)

        unit_done, unit_reduced = sem("unit_done"), sem("unit_reduced")
        msplit, mparts_ready = sem("msplit"), sem("mparts_ready")
        mT_done, mT_ready, mrows_loaded = sem("mT_done"), sem("mT_ready"), sem("mrows_loaded")
        v_done, v_ready = sem("v_done"), sem("v_ready")
        scores_done, probs_ready, av_done, oT_ready = sem("scores_done"), sem("probs_ready"), sem("av_done"), sem("oT_ready")
        o_done, rcp_ready, on_ready = sem("o_done"), sem("rcp_ready"), sem("on_ready")
        onT_done, onT_ready, out_done, x_added = sem("onT_done"), sem("onT_ready"), sem("out_done"), sem("x_added")
        stats_done = sem("stats_done")

        def unit_heads(k):
            return (0, 4 * k, 4) if k < 4 else (1, 2 * (k - 4), 2)

        block = ctx.enter_context(nc.Block())

        def run(eng, body, prologue, tail):
            prologue()
            body(0, 0, s4=False)
            body(1, 1)
            with eng.Fori(0, (NSEQ - 4) // NB) as i:
                for k in range(2, 2 + NB):
                    body(i * NB + k, k % NB)
            body(NSEQ - 2, (NSEQ - 2) % NB, s1=False)
            body(NSEQ - 1, (NSEQ - 1) % NB, s1=False, s2=False)
            tail(NSEQ - 1, (NSEQ - 1) % NB)

        @block.tensor
        def _(pe):
            def transpose_x(c, r, reduced):
                pe.wait_ge(xn_ready, c + 1)
                if reduced is not None:
                    pe.wait_ge(unit_reduced, reduced)
                elif c > 0:
                    pe.wait_ge(xnT_ready, c)
                for s in range(TPS):
                    last = nc.tensor.transpose(max_ps[:, 0, s * P:(s + 1) * P], xn[:, s, :], ident[:])
                last.then_inc(xnT_done, 1)

            def project_qk(c, r, reduced):
                pe.wait_ge(xnT_ready, c + 1)
                if reduced is not None:
                    pe.wait_ge(unit_reduced, reduced)
                elif c > 0:
                    pe.wait_ge(resid_ready, c)
                nc.tensor.matmul(max_ps[:, 1, 0:S], t["wq0"][:], xnT[r % 2][:], start=True, stop=True)
                nc.tensor.matmul(max_ps[:, 1, S:2 * S], t["wk0"][:], xnT[r % 2][:], start=True, stop=True).then_inc(qk_done, 1)

            def project_v(c, r, normed):
                pe.wait_ge(xnT_ready, c + 1)
                if counts(c):
                    pe.wait_ge(v_ready, c)
                if counts(normed):
                    pe.wait_ge(on_ready, normed)
                for s in range(TPS):
                    last = nc.tensor.matmul(mix_ps[:, 1, s * P:(s + 1) * P], xnT[r % 2][:, s * P:(s + 1) * P],
                                            t["wv0"][:], start=True, stop=True)
                last.then_inc(v_done, 1)

            def unit(c, r, k, projected):
                if k == 0:
                    pe.wait_ge(stack_loaded[r], transfers(c, r, NB, LD))
                    if counts(c):
                        pe.wait_ge(mT_ready, c)
                if k in (0, 2):
                    pe.wait_ge(xnT_ready, projected)
                if k in (1, 3):
                    pe.wait_ge(resid_ready, projected)
                if counts(c * NU + k - 1):
                    pe.wait_ge(unit_reduced, c * NU + k - 1)
                s, h0, n = unit_heads(k)
                keys = P * (s + 1)
                bank = max_ps[:, k % 2, :].rearrange("p (h k) -> p h k", k=keys)
                nc.tensor.matmul(bank[:, :, keys - P:keys], identb[:], t["mask_qk"][:, 0:n, :],
                                 start=True, stop=False, skip_group_check=True)
                for j in range(n):
                    last = nc.tensor.matmul(bank[:, j, :], qst[r][0:KS, h0 + j, s * P:(s + 1) * P],
                                            kst[r][0:KS, h0 + j, 0:keys], start=False, stop=True, skip_group_check=True)
                last.then_inc(unit_done, 1)

            def transpose_max(c):
                pe.wait_ge(mparts_ready, c + 1)
                out = max_ps[:, 0, :].bitcast(BF16)
                for s in range(TPS):
                    last = nc.tensor.transpose(out[:, s * P:(s + 1) * P], mpad[:, s, :], identb[:])
                last.then_inc(mT_done, 1)

            def scores(c, r, u):
                if u == 0:
                    pe.wait_ge(stack_loaded[r], transfers(c, r, NB, LD))
                    pe.wait_ge(mrows_loaded, (c + 1) * 16)
                if counts(c * NQ + u):
                    pe.wait_ge(probs_ready, c * NQ + u)
                for bk in range(3):
                    keys = slice(0, P) if bk < 2 else slice(P, S)
                    if bk < 2:
                        diag = sc_ps[:, bk, :].rearrange("p (h q) -> p h q", q=S)[:, :, 0:P]
                        nc.tensor.matmul(diag, identb[:], t["mask_kq"][:, 0:2, :], start=True, stop=False, skip_group_check=True)
                        for n in range(2):
                            h = 4 * u + 2 * bk + n
                            last = nc.tensor.matmul(sc_ps[:, bk, n * S:(n + 1) * S], kst[r][0:KM, h, keys],
                                                    qst[r][0:KM, h, :], start=False, stop=True, skip_group_check=True)
                    else:
                        nc.tensor.matmul(sc_ps[:, 2, :].rearrange("p (h q) -> p h q", q=P), identb[:], t["mask_kq"][:],
                                         start=True, stop=False, skip_group_check=True)
                        for n in range(4):
                            last = nc.tensor.matmul(sc_ps[:, 2, n * P:(n + 1) * P], kst[r][0:KM, 4 * u + n, keys],
                                                    qst[r][0:KM, 4 * u + n, P:S], start=False, stop=True, skip_group_check=True)
                last.then_inc(scores_done, 1)

            def values(c, r, heads):
                for h in heads:
                    u, j = h // 4, h % 4
                    if j == 0:
                        if u == 0:
                            pe.wait_ge(v_ready, c + 1)
                        pe.wait_ge(probs_ready, c * NQ + u + 1)
                        if u % 2 == 0:
                            if counts(c * 2 + u // 2):
                                pe.wait_ge(oT_ready, c * 2 + u // 2)
                    col = (u % 2) * S
                    rows = slice(32 * j, 32 * j + 32)
                    nc.tensor.matmul(av_ps[rows, col:col + S], vaug[r % 2][:, 0, h, :], pT[u][:, j * S:(j + 1) * S],
                                     start=True, stop=False, tile_position=(0, 32 * j))
                    last = nc.tensor.matmul(av_ps[rows, col + P:col + S], vaug[r % 2][:, 1, h, :],
                                            pT[u][:, 4 * S + j * P:4 * S + (j + 1) * P], start=False, stop=True,
                                            tile_position=(0, 32 * j))
                    if j == 3:
                        last.then_inc(av_done, 1)

            def transpose_o(c, r):
                pe.wait_ge(oT_ready, 2 * (c + 1))
                if counts(c):
                    pe.wait_ge(x_added, c)
                if counts(t_v(c)):
                    pe.wait_ge(v_ready, t_v(c))
                for s in range(TPS):
                    for u in range(NQ):
                        last = nc.tensor.transpose(mix_ps[:, s, u * P:(u + 1) * P], oT[r % 2][:, u, s * P:(s + 1) * P], ident[:])
                last.then_inc(o_done, 1)

            def t_v(c):
                return c + 2 if not isinstance(c, int) else min(c + 2, NSEQ)

            def transpose_on(c):
                pe.wait_ge(on_ready, c + 1)
                for s in range(TPS):
                    last = nc.tensor.transpose(mix_ps[:, 0, s * P:(s + 1) * P], on[:, s, :], ident[:])
                last.then_inc(onT_done, 1)

            def project_out(c):
                pe.wait_ge(onT_ready, c + 1)
                for s in range(TPS):
                    last = nc.tensor.matmul(mix_ps[:, 0, S + s * P:S + (s + 1) * P], onT[:, s * P:(s + 1) * P],
                                            t["wo0"][:], start=True, stop=True)
                last.then_inc(out_done, 1)

            def prologue():
                for c in range(2):
                    transpose_x(c, c, None)
                    project_qk(c, c, None)
                project_v(0, 0, 0)
                for k in range(NU):
                    unit(0, 0, k, 2)
                transpose_max(0)

            def body(b, r, s1=True, s2=True, s4=True):
                before, after, later = (r - 1) % NB, (r + 1) % NB, (r + 2) % NB
                seen = b + 3 if s1 else NSEQ

                def next_units(*ks):
                    if s2:
                        for k in ks:
                            unit(b + 1, after, k, b + 2 if k < 2 else seen)

                if s4:
                    values(b - 1, before, range(12, 14))
                    transpose_max(b)
                    values(b - 1, before, range(14, 15))
                next_units(0)
                if s4:
                    values(b - 1, before, range(15, 16))
                next_units(1)
                if s1:
                    transpose_x(b + 2, later, NU * (b + 1) + 1)
                scores(b, r, 0)
                if s1:
                    project_qk(b + 2, later, NU * (b + 1) + 2)
                if s4:
                    transpose_o(b - 1, before)
                next_units(2)
                scores(b, r, 1)
                values(b, r, range(0, 2))
                next_units(3)
                values(b, r, range(2, 4))
                next_units(4)
                scores(b, r, 2)
                next_units(5)
                values(b, r, range(4, 6))
                next_units(6)
                values(b, r, range(6, 8))
                next_units(7)
                scores(b, r, 3)
                if s4:
                    transpose_on(b - 1)
                next_units(8, 9)
                values(b, r, range(8, 10))
                next_units(10, 11)
                values(b, r, range(10, 12))
                if s2:
                    project_v(b + 1, after, b)
                if s4:
                    project_out(b - 1)

            def tail(b, r):
                values(b, r, range(12, 16))
                transpose_o(b, r)
                transpose_on(b)
                project_out(b)

            run(pe, body, prologue, tail)

        @block.scalar
        def _(act):
            def copy_xT(c, r):
                act.wait_ge(xnT_done, c + 1)
                if counts(c - 1):
                    act.wait_ge(v_done, c - 1)
                if counts(c - 1):
                    act.wait_ge(qk_done, c - 1)
                nc.scalar.copy(xnT[r % 2][:], max_ps[:, 0, 0:S]).then_inc(xnT_ready, 1)

            def first_part(c, r):
                act.wait_ge(qk_done, c + 1)
                if counts(c):
                    act.wait_ge(parts_stored[1 - r % 2], transfers(c - 1, 1 - r % 2, 2, WR))
                nc.scalar.copy(parts[:, :, 0, :], max_ps[:, 1, :].rearrange("p (w s) -> p w s", w=2)).then_inc(part1_ready, 1)

            def copy_mT(c, r):
                act.wait_ge(mT_done, c + 1)
                if counts(c * 16):
                    act.wait_ge(mrows_loaded, c * 16)
                nc.scalar.copy(mT[:], max_ps[:, 0, :].bitcast(BF16)[0:NPART * H, 0:S]).then_inc(mT_ready, 1)
                act.wait_ge(mT_ready, c + 1)
                if counts(NQ * (c - 3)):
                    act.wait_ge(scores_done, NQ * (c - 3))
                act.dma_start(qst[r][KS:KM, :, :], mT[:]).then_inc(mrows_loaded, 16)

            def exp(c, u):
                act.wait_ge(scores_done, c * NQ + u + 1)
                if counts((c - 1) * NQ + u + 1):
                    act.wait_ge(av_done, (c - 1) * NQ + u + 1)
                nc.scalar.activation(pT[u][:], sc_ps[:].rearrange("p a s -> p (a s)"), ACT.Exp,
                                     scale=float(DH) ** -0.5).then_inc(probs_ready, 1)

            def copy_onT(c):
                act.wait_ge(onT_done, c + 1)
                if counts(c):
                    act.wait_ge(out_done, c)
                nc.scalar.copy(onT[:], mix_ps[:, 0, 0:S]).then_inc(onT_ready, 1)

            def prologue():
                for c in range(2):
                    copy_xT(c, c)
                    first_part(c, c)
                copy_mT(0, 0)

            def body(b, r, s1=True, s2=True, s4=True):
                if s1:
                    copy_xT(b + 2, (r + 2) % NB)
                exp(b, 0)
                if s1:
                    first_part(b + 2, (r + 2) % NB)
                exp(b, 1)
                exp(b, 2)
                exp(b, 3)
                if s4:
                    copy_onT(b - 1)
                if s2:
                    copy_mT(b + 1, (r + 1) % NB)

            def tail(b, r):
                copy_onT(b)

            run(act, body, prologue, tail)

        @block.vector
        def _(dve):
            def normalise(c):
                if counts(c):
                    dve.wait_ge(xnT_done, c)
                for s in range(TPS):
                    i = c * TPS + s
                    last = nc.vector.tensor_scalar(xn[:, s, :], x[:, bass.ds(i, 1), :].rearrange("p a d -> p (a d)"),
                                                   mean[:, bass.ds(i, 1)], rstd[:, bass.ds(i, 1)], ALU.subtract, ALU.mult)
                last.then_inc(xn_ready, 1)

            def residual(c):
                dve.wait_ge(part1_ready, c + 1)
                if counts(c):
                    dve.wait_ge(parts_ready, c)
                nc.vector.tensor_tensor(resid[:], max_ps[:, 1, :].rearrange("p (w s) -> p w s", w=2), parts[:, :, 0, :],
                                        ALU.subtract).then_inc(resid_ready, 1)
                dve.wait_ge(resid_ready, c + 1)
                nc.vector.tensor_copy(parts[:, :, 1, :], resid[:]).then_inc(part2_ready, 1)

            def take_v(c, r):
                dve.wait_ge(v_done, c + 1)
                if counts(NQ * (c - 1)):
                    dve.wait_ge(av_done, NQ * (c - 1))
                nc.vector.tensor_copy(vaug[r % 2][:, :, :, 0:DH].rearrange("p s h d -> p (s h) d"),
                                      mix_ps[:, 1, 0:S].rearrange("p (g d) -> p g d", d=DH)).then_inc(v_ready, 1)

            def reduce_unit(c, k):
                dve.wait_ge(unit_done, c * NU + k + 1)
                if k == 0:
                    if counts(3 * c):
                        dve.wait_ge(msplit, 3 * c)
                    if counts(c):
                        dve.wait_ge(mparts_ready, c)
                s, h0, n = unit_heads(k)
                nc.vector.reduce_max(mx[:, s, h0:h0 + n], max_ps[:, k % 2, :].rearrange("p (h k) -> p h k", h=n),
                                     axis=AX.X).then_inc(unit_reduced, 1)

            def split_max(c):
                dve.wait_ge(unit_reduced, NU * (c + 1))
                if counts(c):
                    dve.wait_ge(mT_done, c)
                nc.vector.tensor_scalar(mparts[:, :, 0, :], mx[:], -1.0, None, ALU.mult).then_inc(msplit, 1)
                dve.wait_ge(msplit, 3 * c + 1)
                nc.vector.scalar_tensor_tensor(out=mres[:], in0=mx[:], scalar=-1.0, in1=mparts[:, :, 0, :],
                                               op0=ALU.mult, op1=ALU.subtract).then_inc(msplit, 1)
                dve.wait_ge(msplit, 3 * c + 2)
                nc.vector.tensor_copy(mparts[:, :, 1, :], mres[:]).then_inc(msplit, 1)
                dve.wait_ge(msplit, 3 * c + 3)
                nc.vector.tensor_tensor(mparts[:, :, 2, :], mres[:], mparts[:, :, 1, :], ALU.subtract).then_inc(mparts_ready, 1)

            def take_oT(c, r, pair):
                dve.wait_ge(av_done, NQ * c + 2 * pair + 2)
                if counts(c - 1):
                    dve.wait_ge(o_done, c - 1)
                nc.vector.tensor_copy(oT[r % 2][:, 2 * pair:2 * pair + 2, :].rearrange("p u s -> p (u s)"),
                                      av_ps[:]).then_inc(oT_ready, 1)

            def normalise_o(c):
                dve.wait_ge(o_done, c + 1)
                o = mix_ps[:].rearrange("p s (h r) -> p s h r", r=32)
                if counts(c):
                    dve.wait_ge(on_ready, c)
                nc.vector.reciprocal(rcp[:], o[:, :, :, DH]).then_inc(rcp_ready, 1)
                dve.wait_ge(rcp_ready, c + 1)
                if counts(c):
                    dve.wait_ge(onT_done, c)
                nc.vector.tensor_tensor(on[:].rearrange("p s (h d) -> p s h d", d=DH), o[:, :, :, 0:DH],
                                        rcp[:].unsqueeze(3).to_broadcast([P, TPS, H, DH]), ALU.mult).then_inc(on_ready, 1)

            def add_x(c):
                dve.wait_ge(out_done, c + 1)
                xs = x[:, bass.ds(c * TPS, TPS), :].rearrange("p s d -> p (s d)")
                nc.vector.tensor_tensor(xs, mix_ps[:, 0, S:2 * S], xs, ALU.add).then_inc(x_added, 1)
                dve.wait_ge(x_added, c + 1)
                for s in range(TPS):
                    last = nc.vector.bn_stats(t["stats"][:, bass.ds(c * TPS + s, 1), :], x[:, bass.ds(c * TPS + s, 1), :])
                last.then_inc(stats_done, 1)

            def prologue():
                nc.vector.memset(mpad[:], 0.0)
                for c in range(2):
                    normalise(c)
                    residual(c)
                take_v(0, 0)
                for k in range(NU):
                    reduce_unit(0, k)
                split_max(0)

            def body(b, r, s1=True, s2=True, s4=True):
                def next_units(*ks):
                    if s2:
                        for k in ks:
                            reduce_unit(b + 1, k)

                if s1:
                    normalise(b + 2)
                next_units(0, 1)
                if s4:
                    take_oT(b - 1, (r - 1) % NB, 1)
                if s1:
                    residual(b + 2)
                if s4:
                    normalise_o(b - 1)
                next_units(2, 3, 4, 5, 6)
                take_oT(b, r, 0)
                next_units(7, 8, 9, 10, 11)
                if s2:
                    split_max(b + 1)
                    take_v(b + 1, (r + 1) % NB)
                if s4:
                    add_x(b - 1)

            def tail(b, r):
                take_oT(b, r, 1)
                normalise_o(b)
                add_x(b)

            run(dve, body, prologue, tail)

        @block.gpsimd
        def _(pool):
            def other_parts(c):
                pool.wait_ge(part2_ready, c + 1)
                nc.gpsimd.tensor_tensor(parts[:, :, 2, :], resid[:], parts[:, :, 1, :],
                                        ALU.subtract).then_inc(parts_ready, 1)

            def prologue():
                other_parts(0)
                other_parts(1)

            def body(b, r, s1=True, s2=True, s4=True):
                if s1:
                    other_parts(b + 2)

            run(pool, body, prologue, lambda b, r: None)

        @block.sync
        def _(sp):
            def store_parts(c, r):
                p = r % 2
                ready, readers = value(sp, c + 1), value(sp, transfers(c - 2, (r - 2) % NB, NB, LD))
                sp.wait_ge(parts_ready, ready)
                if counts(readers):
                    sp.wait_ge(stack_loaded[(r - 2) % NB], readers)
                sp.dma_start(scratch[p].rearrange("w a d h s -> (d h) (w a) s"), parts[:].rearrange("p w a s -> p (w a) s")
                             ).then_inc(parts_stored[p], 16)

            def load_stack(c, r):
                p = r % 2
                stored, read = value(sp, transfers(c, p, 2, WR)), value(sp, NQ * (c - 3))
                sp.wait_ge(parts_stored[p], stored)
                if counts(read):
                    sp.wait_ge(scores_done, read)
                sp.dma_start(kst[r][0:KS, :, :], scratch[p][1].rearrange("a d h s -> (a d) (h s)").unsqueeze(0)
                             .to_broadcast([NPART, NPART * DH, H * S])).then_inc(stack_loaded[r], 16)
                for i in range(NPART):
                    rows = slice(NPART * i * DH, NPART * (i + 1) * DH)
                    sp.dma_start(qst[r][rows, :, :], scratch[p][0, i].rearrange("d h s -> d (h s)").unsqueeze(0)
                                 .to_broadcast([NPART, DH, H * S])).then_inc(stack_loaded[r], 16)

            def prologue():
                for c in range(2):
                    store_parts(c, c)
                    load_stack(c, c)

            def body(b, r, s1=True, s2=True, s4=True):
                if s1:
                    store_parts(b + 2, (r + 2) % NB)
                    load_stack(b + 2, (r + 2) % NB)

            run(sp, body, prologue, lambda b, r: None)


E, FF = 8, 512
FC = FF // P
RT = 2 * P
PK = 2 * FF + FC + 1
NOWHERE = 1 << 20
GT = 4


def n_tiles(slots):
    return (slots * NT * P - E) // RT + E


def route(nc, t, slots, w):
    NTL, J = n_tiles(slots), slots * NT
    NPL = 2 * NTL
    JC = 8
    rows_v = t["rows"].rearrange("(t p) d -> p t d", p=P)
    x, mean, rstd, cst = t["x"], t["mean"], t["rstd"], t["cst"]
    rev, thr, tix = cst[:, 0:E], cst[:, E:E + 16], cst[:, E + 16:E + 16 + NTL]
    pcol, iota = cst[:, E + 16 + n_tiles(2):E + 17 + n_tiles(2)], t["iotab"]
    ones = t["tri"][:, P:2 * P]
    after = t["afterb"]
    gates, takes, goes, eidx = t["gates"], t["takes"], t["goes"], t["eidx"]
    with ExitStack() as ctx:
        def sb(name, shape, dt):
            return ctx.enter_context(nc.sbuf_tensor(f"{name}_{w}", shape, dt))

        def ps(name, shape):
            return ctx.enter_context(nc.psum_tensor(f"{name}_{w}", shape, F32))

        def sem(name):
            return ctx.enter_context(nc.semaphore(name))

        xr = [sb(f"xr{i}", [P, GT, D], F32) for i in range(2)]
        xrT = [sb(f"xrT{i}", [P, GT * P], F32) for i in range(2)]
        posi, lowi, highi = sb("posi", [P, J], I32), sb("lowi", [P, J], I32), sb("highi", [P, J], I32)
        low, high = sb("low", [P, J], BF16), sb("high", [P, J], BF16)
        at = sb("at", [P, J, NPL], BF16)
        at_low = sb("at_low", [P, J, P], BF16)
        at_high = sb("at_high", [P, J, 2, NPL], BF16)
        took, gone = sb("took", [P, 2, NPL], F32), sb("gone", [P, 2, NPL], F32)
        lg, cand, l2 = sb("lg", [P, NT, E], F32), sb("cand", [P, NT, E], F32), sb("l2", [P, NT, E], F32)
        top, cmax = sb("top", [P, 2, NT], F32), sb("cmax", [P, NT], F32)
        gtmp = sb("gtmp", [P, 3, NT], F32)
        pick = sb("pick", [P, slots, NT, E], BF16)
        upto = sb("upto", [P, J, E], F32)
        place = sb("place", [P, J, E], F32)
        tcmp, tl, start = sb("tcmp", [P, E, 16], F32), sb("tl", [P, E], F32), sb("start", [P, E], F32)
        ends = sb("ends", [P, E], F32)
        ecmp, ef, posf = sb("ecmp", [P, NTL, E], F32), sb("ef", [P, NTL], F32), sb("posf", [P, J], F32)
        xT_ps = [ps(f"xT_ps{i}", [P, 512]) for i in range(2)]
        lg_ps, pre_ps, tot_ps = ps("lg_ps", [P, NT, E]), ps("pre_ps", [P, J, E]), ps("tot_ps", [P, J, E])
        place_ps = ps("place_ps", [P, 2, NPL])

        rows_stored = [sem(f"rows_stored{i}") for i in range(2)]
        xr_ready, xT_done, xT_ready = sem("xr_ready"), sem("xT_done"), sem("xT_ready")
        lg_done, counted = sem("lg_done"), sem("counted")
        gate_in, gate_exp, ordered = sem("gate_in"), sem("gate_exp"), sem("ordered")
        hot_ready, low_ready, p_ready, j_ready = sem("hot_ready"), sem("low_ready"), sem("p_ready"), sem("j_ready")
        step = sem("step")
        block = ctx.enter_context(nc.Block())

        def run(eng, body):
            body(0, 0)
            body(1, 1)
            with eng.Fori(1, NT // GT // 2) as i:
                body(i * 2, 0)
                body(i * 2 + 1, 1)

        @block.vector
        def _(dve):
            def body(g, par):
                if counts(g - 1):
                    dve.wait_ge(xT_done, g - 1)
                if counts(g - 1):
                    dve.wait_ge(rows_stored[par], (g - par) * 8)
                for k in range(GT):
                    i = g * GT + k
                    last = nc.vector.tensor_scalar(xr[par][:, k, :], x[:, bass.ds(i, 1), :].rearrange("p a d -> p (a d)"),
                                                   mean[:, bass.ds(i, 1)], rstd[:, bass.ds(i, 1)], ALU.subtract, ALU.mult)
                last.then_inc(xr_ready, 1)

            run(dve, body)
            done = [0]

            def link(ins):
                done[0] += 1
                ins.then_inc(step, 1)
                dve.wait_ge(step, done[0])

            def over_e(a):
                return a.unsqueeze(2).to_broadcast([P, a.shape[1], E])

            def pick_first(src, k):
                link(nc.vector.reduce_max(top[:, k, :], src[:], axis=AX.X))
                link(nc.vector.tensor_tensor(cand[:], src[:], over_e(top[:, k, :]), ALU.is_equal))
                link(nc.vector.tensor_tensor(cand[:], cand[:], rev.unsqueeze(1).to_broadcast([P, NT, E]), ALU.mult))
                link(nc.vector.reduce_max(cmax[:], cand[:], axis=AX.X))
                link(nc.vector.tensor_tensor(pick[:, k, :, :], cand[:], over_e(cmax[:]), ALU.is_equal))

            dve.wait_ge(lg_done, NT // GT)
            link(nc.vector.tensor_tensor(lg[:], lg_ps[:], t[f"br{w}"][:].unsqueeze(1).to_broadcast([P, NT, E]), ALU.add))
            pick_first(lg, 0)
            if slots == 2:
                link(nc.vector.scalar_tensor_tensor(out=l2[:], in0=pick[:, 0, :, :], scalar=MASKED, in1=lg[:],
                                                    op0=ALU.mult, op1=ALU.add))
                pick_first(l2, 1)
                nc.vector.tensor_tensor(gtmp[:, 0, :], top[:, 1, :], top[:, 0, :], ALU.subtract).then_inc(gate_in, 1)
            else:
                nc.vector.tensor_tensor(l2[:], lg[:], over_e(top[:, 0, :]), ALU.subtract).then_inc(gate_in, 1)
            dve.wait_ge(counted, 1)
            for e in range(E):
                last = nc.vector.tensor_tensor_scan(upto[:, :, e], ones[:, 0:J], tot_ps[:, :, e], 0.0, ALU.mult, ALU.add)
            link(last)
            total = upto[:, J - 1, :]
            link(nc.vector.tensor_tensor(tcmp[:], total.unsqueeze(2).to_broadcast([P, E, 16]),
                                         thr.unsqueeze(1).to_broadcast([P, E, 16]), ALU.is_gt))
            link(nc.vector.reduce_sum(tl[:], tcmp[:], axis=AX.X))
            link(nc.vector.tensor_tensor_scan(ends[:], ones[:, 0:E], tl[:], 0.0, ALU.mult, ALU.add))
            link(nc.vector.tensor_tensor(start[:], ends[:], tl[:], ALU.subtract))
            link(nc.vector.tensor_scalar(start[:], start[:], float(RT), None, ALU.mult))
            link(nc.vector.tensor_tensor(place[:], pre_ps[:], upto[:], ALU.add))
            link(nc.vector.tensor_tensor(place[:], place[:], tot_ps[:], ALU.subtract))
            link(nc.vector.tensor_tensor(place[:], place[:], start[:].unsqueeze(1).to_broadcast([P, J, E]), ALU.add))
            link(nc.vector.tensor_tensor(place[:], place[:], pick[:].rearrange("p k t e -> p (k t) e"), ALU.mult))
            link(nc.vector.reduce_sum(posf[:], place[:], axis=AX.X))
            link(nc.vector.tensor_copy(posi[:], posf[:]))
            nc.vector.tensor_scalar(lowi[:], posi[:], P - 1, None, ALU.bitwise_and)
            link(nc.vector.tensor_scalar(highi[:], posi[:], 7, None, ALU.arith_shift_right))
            nc.vector.tensor_copy(low[:], lowi[:])
            link(nc.vector.tensor_copy(high[:], highi[:]))
            for j in range(0, J, JC):
                js = slice(j, j + JC)
                nc.vector.tensor_tensor(at[:, js, :], high[:, js].unsqueeze(2).to_broadcast([P, JC, NPL]),
                                        iota[:, 0:NPL].unsqueeze(1).to_broadcast([P, JC, NPL]), ALU.is_equal).then_inc(hot_ready, 1)
                nc.vector.tensor_tensor(at_low[:, js, :], low[:, js].unsqueeze(2).to_broadcast([P, JC, P]),
                                        iota[:].unsqueeze(1).to_broadcast([P, JC, P]), ALU.is_equal).then_inc(low_ready, 1)
            link(nc.vector.tensor_tensor(ecmp[:], ends[:].unsqueeze(1).to_broadcast([P, NTL, E]), over_e(tix), ALU.is_le))
            link(nc.vector.reduce_sum(ef[:], ecmp[:], axis=AX.X))
            nc.vector.tensor_scalar(eidx[:, 0:NTL], ef[:], float(E - 1), None, ALU.min)
            dve.wait_ge(gate_exp, 1)
            if slots == 2:
                link(nc.vector.tensor_scalar(gtmp[:, 2, :], gtmp[:, 1, :], 1.0, None, ALU.add))
                link(nc.vector.reciprocal(gates[:, 0, :], gtmp[:, 2, :]))
                nc.vector.tensor_tensor(gates[:, 1, :], gtmp[:, 1, :], gates[:, 0, :], ALU.mult)
            else:
                link(nc.vector.reduce_sum(gtmp[:, 2, :], cand[:], axis=AX.X))
                nc.vector.reciprocal(gates[:, 0, :], gtmp[:, 2, :])
            dve.wait_ge(ordered, 1)
            link(nc.vector.tensor_copy(took[:], place_ps[:]))
            link(nc.vector.scalar_tensor_tensor(out=gone[:, 0, :], in0=took[:, 1, :], scalar=float(P), in1=took[:, 0, :],
                                                op0=ALU.mult, op1=ALU.add))
            link(nc.vector.tensor_scalar(gone[:, 0, :], gone[:, 0, :], float(-P), None, ALU.add))
            link(nc.vector.tensor_scalar(gone[:, 1, :], took[:, 1, :], 0.0, float(NOWHERE), ALU.is_equal, ALU.mult))
            nc.vector.tensor_tensor(goes[:, 0:NPL], gone[:, 0, :], gone[:, 1, :], ALU.add)
            link(nc.vector.tensor_copy(takes[:, 0:NPL], gone[:, 0, :]))
            nc.vector.tensor_scalar(takes[:, 0:NPL], takes[:, 0:NPL], NT * P - 1, None, ALU.bitwise_and)

        @block.gpsimd
        def _(pool):
            for j in range(0, J, JC):
                js = slice(j, j + JC)
                pool.wait_ge(hot_ready, j // JC + 1)
                nc.gpsimd.tensor_tensor(at_high[:, js, 1, :], at[:, js, :], after[:, js].unsqueeze(2).to_broadcast([P, JC, NPL]),
                                        ALU.mult).then_inc(j_ready, 1)

        @block.sync
        def _(sp):
            def body(g, par):
                ready = value(sp, g + 1)
                sp.wait_ge(xr_ready, ready)
                sp.dma_start(rows_v[:, bass.ds(g * GT, GT), :], xr[par][:]).then_inc(rows_stored[par], 16)

            run(sp, body)
            for par in range(2):
                sp.wait_ge(rows_stored[par], 16 * (NT // GT // 2))

        @block.scalar
        def _(act):
            def body(g, par):
                act.wait_ge(xT_done, g + 1)
                if counts(g - 1):
                    act.wait_ge(lg_done, g - 1)
                nc.scalar.copy(xrT[par][:], xT_ps[par][:]).then_inc(xT_ready, 1)

            run(act, body)
            act.wait_ge(gate_in, 1)
            if slots == 2:
                nc.scalar.activation(gtmp[:, 1, :], gtmp[:, 0, :], ACT.Exp).then_inc(gate_exp, 1)
            else:
                nc.scalar.activation(cand[:], l2[:], ACT.Exp).then_inc(gate_exp, 1)
            for j in range(0, J, JC):
                act.wait_ge(hot_ready, j // JC + 1)
                nc.scalar.mul(at_high[:, j:j + JC, 0, :], at[:, j:j + JC, :], pcol).then_inc(p_ready, 1)

        @block.tensor
        def _(pe):
            def transposes(g, par):
                pe.wait_ge(xr_ready, g + 1)
                if counts(g - 1):
                    pe.wait_ge(xT_ready, g - 1)
                for k in range(GT):
                    last = nc.tensor.transpose(xT_ps[par][:, k * P:(k + 1) * P], xr[par][:, k, :], t["ident"][:])
                last.then_inc(xT_done, 1)

            def logits(g, par):
                pe.wait_ge(xT_ready, g + 1)
                for k in range(GT):
                    last = nc.tensor.matmul(lg_ps[:, bass.ds(g * GT + k, 1), :].rearrange("p a e -> p (a e)"),
                                            xrT[par][:, k * P:(k + 1) * P], t[f"wr{w}"][:], start=True, stop=True)
                last.then_inc(lg_done, 1)

            transposes(0, 0)
            transposes(1, 1)
            logits(0, 0)
            with pe.Fori(1, NT // GT // 2) as i:
                transposes(i * 2, 0)
                logits(i * 2 - 1, 1)
                transposes(i * 2 + 1, 1)
                logits(i * 2, 0)
            logits(NT // GT - 1, 1)
            pe.wait_ge(gate_in, 1)
            nc.tensor.matmul(pre_ps[:].rearrange("p j e -> p (j e)"), t["before"][:],
                             pick[:].rearrange("p k t e -> p (k t e)"), start=True, stop=True)
            nc.tensor.matmul(tot_ps[:].rearrange("p j e -> p (j e)"), t["onesb"][:],
                             pick[:].rearrange("p k t e -> p (k t e)"), start=True, stop=True).then_inc(counted, 1)
            for j in range(J):
                if j % JC == 0:
                    pe.wait_ge(low_ready, j // JC + 1)
                    pe.wait_ge(p_ready, j // JC + 1)
                    pe.wait_ge(j_ready, j // JC + 1)
                last = nc.tensor.matmul(place_ps[:].rearrange("p a n -> p (a n)"), at_low[:, j, :],
                                        at_high[:, j, :, :].rearrange("p a n -> p (a n)"), start=(j == 0), stop=(j == J - 1))
            last.then_inc(ordered, 1)


def experts(nc, t, slots, w, ys):
    NTL, takes, goes = n_tiles(slots), t["takes"], t["goes"]
    ident, wpack, eidx = t["ident"], t[f"wpack{w}"], t["eidx"]
    with ExitStack() as ctx:
        def sb(name, shape, n=2, dt=F32):
            return [ctx.enter_context(nc.sbuf_tensor(f"{name}{i}_{w}", shape, dt)) for i in range(n)]

        def ps(name, shape):
            return ctx.enter_context(nc.psum_tensor(f"{name}_{w}", shape, F32))

        def sem(name):
            return ctx.enter_context(nc.semaphore(name))

        xt, xT, hT, yT, yt = sb("xt", [P, 2, D], 4), sb("xT", [P, RT]), sb("hT", [P, FC, RT]), sb("yT", [P, RT]), sb("yt", [P, 2, D])
        w1, w2 = sb("w1b", [P, FF + FC]), sb("w2b", [P, FF + 1])
        take, go = sb("take", [P, 2], 4, mybir.dt.uint32), sb("go", [P, 2], 2, mybir.dt.uint32)
        h_ps = [ps(f"h_ps{i}", [P, 2, 512]) for i in range(2)]
        xT_ps, yT_ps, y_ps = ps("xT_ps", [P, 512]), ps("yT_ps", [P, 512]), ps("y_ps", [P, 512])
        xt_loaded = [sem(f"xt_loaded{i}") for i in range(4)]
        y_stored = [sem(f"y_stored{i}") for i in range(2)]
        xT_done, xT_ready, w1_ready, w2_ready = sem("xT_done"), sem("xT_ready"), sem("w1_ready"), sem("w2_ready")
        take_ready = sem("take_ready")
        h_done, hT_ready, yT_done, yT_ready, y_done, y_ready = (sem("h_done"), sem("hT_ready"), sem("yT_done"),
                                                                sem("yT_ready"), sem("y_done"), sem("y_ready"))
        block = ctx.enter_context(nc.Block())

        def run(eng, body):
            for i in range(4):
                body(i, i)
            with eng.Fori(1, (NTL - 3) // 4) as i:
                for r in range(4):
                    body(i * 4 + r, r)
            for i in range(NTL - 3, NTL + 2):
                body(i, i % 4)

        def has(i):
            return not isinstance(i, int) or 0 <= i < NTL

        def gathered(i, r):
            return (i + (4 - r)) * 8

        @block.gpsimd
        def _(pool):
            last_place = pool.to_reg(slots * NT * P - 1)

            def gather(i, r):
                free, ready = value(pool, i - 3), value(pool, i + 1)
                pool.wait_ge(t["packs_loaded"], 16)
                if counts(free):
                    pool.wait_ge(xT_done, free)
                pool.wait_ge(take_ready, ready)
                for s in range(2):
                    nc.gpsimd.indirect_dma_start(out=xt[r][:, s, :], out_offset=None, in_=t["rows"],
                                                 in_offset=bass.IndirectOffsetOnAxis(ap=take[r][:, s:s + 1], axis=0)
                                                 ).then_inc(xt_loaded[r], 16)

            def scatter(i, par):
                ready = value(pool, i + 1)
                pool.wait_ge(t["packs_loaded"], 16)
                pool.wait_ge(y_ready, ready)
                for s in range(2):
                    nc.gpsimd.indirect_dma_start(out=ys, out_offset=bass.IndirectOffsetOnAxis(ap=go[par][:, s:s + 1], axis=0),
                                                 in_=yt[par][:, s, :], in_offset=None, bounds_check=last_place,
                                                 oob_is_err=False).then_inc(y_stored[par], 16)

            for i in range(3):
                gather(i, i)

            def body(i, r):
                if has(i + 3):
                    gather(i + 3, (r + 3) % 4)
                if has(i - 2):
                    scatter(i - 2, r % 2)

            run(pool, body)
            for par in range(2):
                pool.wait_ge(y_stored[par], 32 * ((NTL + 1 - par) // 2))

        @block.vector
        def _(dve):
            def expert(i):
                return nc.vector.value_load(eidx[0:1, bass.ds(i, 1)], min_val=0, max_val=E - 1)

            def copy_w1(i, par):
                e = expert(i)
                if counts(i - 1):
                    dve.wait_ge(h_done, i - 1)
                if counts(i - 1):
                    dve.wait_ge(hT_ready, i - 1)
                nc.vector.tensor_copy(w1[par][:], wpack[:, bass.ds(e, 1), 0:FF + FC].rearrange("p a f -> p (a f)")).then_inc(w1_ready, 1)

            def copy_w2(i, par):
                e = expert(i)
                if counts(i - 1):
                    dve.wait_ge(yT_done, i - 1)
                if counts(i - 1):
                    dve.wait_ge(yT_ready, i - 1)
                nc.vector.tensor_copy(w2[par][:], wpack[:, bass.ds(e, 1), FF + FC:PK].rearrange("p a f -> p (a f)")).then_inc(w2_ready, 1)

            def take_xT(i, par):
                dve.wait_ge(xT_done, i + 1)
                if counts(i - 1):
                    dve.wait_ge(h_done, i - 1)
                nc.vector.tensor_copy(xT[par][:], xT_ps[:, 0:RT]).then_inc(xT_ready, 1)

            def take_y(i, par):
                dve.wait_ge(y_done, i + 1)
                if not isinstance(i, int) or i >= 2:
                    dve.wait_ge(y_stored[par], (i - par) * 16)
                nc.vector.tensor_copy(go[par][:], goes[:, bass.ds(i * 2, 2)])
                nc.vector.tensor_copy(yt[par][:].rearrange("p s d -> p (s d)"), y_ps[:, 0:RT]).then_inc(y_ready, 1)

            dve.wait_ge(t["packs_loaded"], 16 * (w + 1))
            copy_w1(0, 0)
            take_xT(0, 0)

            def body(i, r):
                par = r % 2
                if has(i + 1):
                    copy_w1(i + 1, 1 - par)
                    take_xT(i + 1, 1 - par)
                if has(i - 2):
                    take_y(i - 2, par)
                if has(i):
                    copy_w2(i, par)

            run(dve, body)

        @block.scalar
        def _(act):
            def relu(i, par):
                act.wait_ge(h_done, i + 1)
                if counts(i - 1):
                    act.wait_ge(yT_done, i - 1)
                for c in range(FC):
                    last = nc.scalar.activation(hT[par][:, c, :], h_ps[par][:, c // 2, (c % 2) * RT:(c % 2 + 1) * RT],
                                                ACT.Relu, bias=w1[par][:, FF + c:FF + c + 1])
                last.then_inc(hT_ready, 1)

            def take_yT(i, par):
                act.wait_ge(yT_done, i + 1)
                if counts(i - 1):
                    act.wait_ge(y_done, i - 1)
                nc.scalar.activation(yT[par][:], yT_ps[:, 0:RT], ACT.Identity, bias=w2[par][:, FF:FF + 1]).then_inc(yT_ready, 1)

            def copy_take(i, r):
                if not isinstance(i, int) or i >= 4:
                    act.wait_ge(xt_loaded[r], gathered(i - 4, r))
                nc.scalar.copy(take[r][:], takes[:, bass.ds(i * 2, 2)]).then_inc(take_ready, 1)

            for i in range(3):
                copy_take(i, i)

            def body(i, r):
                par = r % 2
                if has(i):
                    relu(i, par)
                if has(i + 3):
                    copy_take(i + 3, (r + 3) % 4)
                if has(i - 1):
                    take_yT(i - 1, 1 - par)

            run(act, body)

        @block.tensor
        def _(pe):
            def transpose_in(i, r):
                pe.wait_ge(xt_loaded[r], gathered(i, r))
                if counts(i):
                    pe.wait_ge(xT_ready, i)
                for s in range(2):
                    last = nc.tensor.transpose(xT_ps[:, s * P:(s + 1) * P], xt[r][:, s, :], ident[:])
                last.then_inc(xT_done, 1)

            def hidden(i, par):
                pe.wait_ge(xT_ready, i + 1)
                pe.wait_ge(w1_ready, i + 1)
                if counts(i - 1):
                    pe.wait_ge(hT_ready, i - 1)
                for c in range(FC):
                    last = nc.tensor.matmul(h_ps[par][:, c // 2, (c % 2) * RT:(c % 2 + 1) * RT], w1[par][:, c * P:(c + 1) * P],
                                            xT[par][:], start=True, stop=True)
                last.then_inc(h_done, 1)

            def second(i, par):
                pe.wait_ge(hT_ready, i + 1)
                pe.wait_ge(w2_ready, i + 1)
                if counts(i):
                    pe.wait_ge(yT_ready, i)
                for c in range(FC):
                    last = nc.tensor.matmul(yT_ps[:, 0:RT], w2[par][:, c * P:(c + 1) * P], hT[par][:, c, :],
                                            start=(c == 0), stop=(c == FC - 1))
                last.then_inc(yT_done, 1)

            def transpose_back(i, par):
                pe.wait_ge(yT_ready, i + 1)
                if counts(i):
                    pe.wait_ge(y_ready, i)
                for s in range(2):
                    last = nc.tensor.transpose(y_ps[:, s * P:(s + 1) * P], yT[par][:, s * P:(s + 1) * P], ident[:])
                last.then_inc(y_done, 1)

            transpose_in(0, 0)

            def body(i, r):
                par = r % 2
                first = isinstance(i, int) and i == 0
                if first:
                    hidden(i, par)
                if has(i + 1):
                    transpose_in(i + 1, (r + 1) % 4)
                if has(i) and not first:
                    hidden(i, par)
                if has(i - 2):
                    transpose_back(i - 2, par)
                if has(i - 1):
                    second(i - 1, 1 - par)

            run(pe, body)


def combine(nc, t, slots, w, ys, out=None):
    x, gates = t["x"], t["gates"]
    NCH = 8
    CT = NT // NCH
    ys_v = ys.rearrange("(k c t p) d -> k c p t d", k=2, c=NCH, p=P)
    if out is not None:
        out_v = out.rearrange("(c t p) d -> c p t d", c=NCH, p=P)
    with ExitStack() as ctx:
        back = ctx.enter_context(nc.sbuf_tensor(f"back_{w}", [P, slots, NT, D], F32))
        loaded = [ctx.enter_context(nc.semaphore(f"loaded{i}")) for i in range(NCH)]
        added = [ctx.enter_context(nc.semaphore(f"added{k}")) for k in range(slots)]
        weighed, stored = ctx.enter_context(nc.semaphore("weighed")), ctx.enter_context(nc.semaphore("stored"))
        block = ctx.enter_context(nc.Block())

        @block.sync
        def _(sp):
            for c in range(NCH):
                for k in range(slots):
                    sp.dma_start(back[:, k, c * CT:(c + 1) * CT, :], ys_v[k, c]).then_inc(loaded[c], 16)
            if out is not None:
                for c in range(NCH):
                    sp.wait_ge(added[slots - 1], (c + 1) * CT)
                    sp.dma_start(out_v[c], x[:, c * CT:(c + 1) * CT, :]).then_inc(stored, 16)
                sp.wait_ge(stored, 16 * NCH)

        if slots == 2:
            @block.scalar
            def _(act):
                for j in range(NT):
                    if j % CT == 0:
                        act.wait_ge(loaded[j // CT], 16 * slots)
                    nc.scalar.mul(back[:, 0, j, :], back[:, 0, j, :], gates[:, 0, j:j + 1]).then_inc(weighed, 1)

            @block.gpsimd
            def _(pool):
                for j in range(NT):
                    pool.wait_ge(weighed, j + 1)
                    nc.gpsimd.tensor_tensor(x[:, j, :], back[:, 0, j, :], x[:, j, :], ALU.add).then_inc(added[0], 1)

        @block.vector
        def _(dve):
            for i in range(NT + 1):
                if i < NT:
                    if slots == 2:
                        dve.wait_ge(added[0], i + 1)
                    elif i % CT == 0:
                        dve.wait_ge(loaded[i // CT], 16 * slots)
                    nc.vector.scalar_tensor_tensor(out=x[:, i, :], in0=back[:, slots - 1, i, :], scalar=gates[:, slots - 1, i:i + 1],
                                                   in1=x[:, i, :], op0=ALU.mult, op1=ALU.add).then_inc(added[slots - 1], 1)
                if out is None and i > 0:
                    dve.wait_ge(added[slots - 1], i)
                    nc.vector.bn_stats(t["stats"][:, i - 1, :], x[:, i - 1, :])


DL = 64


def linear_attention(nc, t, dram):
    x, mean, rstd, ident = t["x"], t["mean"], t["rstd"], t["ident"]
    LAST = 4
    with ExitStack() as ctx:
        def sb(name, shape):
            return [ctx.enter_context(nc.sbuf_tensor(f"{name}{i}", shape, F32)) for i in range(2)]

        def ps(name, shape):
            return ctx.enter_context(nc.psum_tensor(name, shape, F32))

        def sem(name):
            return ctx.enter_context(nc.semaphore(name))

        xn, xnT, kv = sb("lxn", [P, TPS, D]), sb("lxnT", [D, S]), sb("lkv", [P, TPS, 2 * DL])
        qT = [ctx.enter_context(nc.sbuf_tensor(f"lqT{i}", [DL, S], F32)) for i in range(4)]
        eT, f = sb("leT", [DL, P]), sb("lf", [DL, D])
        x_ps, e_ps, f_ps = ps("lx_ps", [P, 512]), ps("le_ps", [P, 512]), ps("lf_ps", [P, 512])
        qkv_ps = [ps(f"lqkv_ps{i}", [P, 512]) for i in range(2)]
        o_ps = [ps(f"lo_ps{i}", [P, 512]) for i in range(2)]
        zeroed, xn_ready, x_done, xnT_ready = sem("zeroed"), sem("xn_ready"), sem("x_done"), sem("xnT_ready")
        qkv_done, qkv_ready, e_done, e_ready = sem("qkv_done"), sem("qkv_ready"), sem("e_done"), sem("e_ready")
        f_done, f_ready, o_done, x_added, stats_done = sem("f_done"), sem("f_ready"), sem("o_done"), sem("x_added"), sem("stats_done")
        block = ctx.enter_context(nc.Block())

        def has(i):
            return not isinstance(i, int) or 0 <= i < NSEQ

        def run(eng, body):
            for i in range(6):
                body(i, i % 4)
            with eng.Fori(1, NSEQ // 4 - 1) as i:
                for r in range(4):
                    body(i * 4 + (2 + r), (2 + r) % 4)
            for i in range(NSEQ - 2, NSEQ + LAST):
                body(i, i % 4)

        @block.sync
        def _(sp):
            sp.dma_start(t["wpack1"][:], dram["wpack1"]).then_inc(t["packs_loaded"], 16)

        @block.vector
        def _(dve):
            def normalise(i, r):
                if counts(i - 1):
                    dve.wait_ge(x_done, i - 1)
                for s in range(TPS):
                    k = i * TPS + s
                    last = nc.vector.tensor_scalar(xn[r % 2][:, s, :], x[:, bass.ds(k, 1), :].rearrange("p a d -> p (a d)"),
                                                   mean[:, bass.ds(k, 1)], rstd[:, bass.ds(k, 1)], ALU.subtract, ALU.mult)
                last.then_inc(xn_ready, 1)

            def add_x(i, r):
                dve.wait_ge(o_done, i + 1)
                xs = x[:, bass.ds(i * TPS, TPS), :].rearrange("p s d -> p (s d)")
                nc.vector.tensor_tensor(xs, o_ps[r % 2][:, 0:S], xs, ALU.add).then_inc(x_added, 1)
                dve.wait_ge(x_added, i + 1)
                for s in range(TPS):
                    last = nc.vector.bn_stats(t["stats"][:, bass.ds(i * TPS + s, 1), :], x[:, bass.ds(i * TPS + s, 1), :])
                last.then_inc(stats_done, 1)

            for i in range(2):
                nc.vector.memset(eT[i][:], 0.0).then_inc(zeroed, 1)
            normalise(0, 0)

            def body(i, r):
                if has(i + 1) and not (isinstance(i, int) and i + 1 >= NSEQ):
                    normalise_next(i, r)
                if has(i - 4):
                    add_x(i - 4, r)

            def normalise_next(i, r):
                normalise(i + 1, r + 1)

            run(dve, body)

        @block.scalar
        def _(act):
            act.wait_ge(zeroed, 2)

            def body(i, r):
                if has(i - 3):
                    if counts(i - 2):
                        act.wait_ge(f_done, i - 2)
                    if counts(i - 4):
                        act.wait_ge(o_done, i - 4)
                    nc.scalar.mul(f[(r + 1) % 2][:], f_ps[0:DL, 0:D], (3.0 / DL) ** 0.5).then_inc(f_ready, 1)
                if has(i - 2):
                    if counts(i - 1):
                        act.wait_ge(e_done, i - 1)
                    if counts(i - 4):
                        act.wait_ge(f_done, i - 4)
                    nc.scalar.copy(eT[r % 2][:, 0:DL], e_ps[0:DL, 0:DL]).then_inc(e_ready, 1)
                if has(i - 1):
                    p = (r + 1) % 2
                    if counts(i):
                        act.wait_ge(qkv_done, i)
                    if counts(i - 3):
                        act.wait_ge(e_done, i - 3)
                    if counts(i - 4):
                        act.wait_ge(o_done, i - 4)
                    nc.scalar.copy(qT[(r + 3) % 4][:], qkv_ps[p][0:DL, 0:S])
                    nc.scalar.copy(kv[p][:].rearrange("p s d -> p (s d)"), qkv_ps[p][:, S:2 * S]).then_inc(qkv_ready, 1)
                if has(i):
                    act.wait_ge(x_done, i + 1)
                    if counts(i - 1):
                        act.wait_ge(qkv_done, i - 1)
                    nc.scalar.copy(xnT[r % 2][:], x_ps[:, 0:S]).then_inc(xnT_ready, 1)

            run(act, body)

        @block.tensor
        def _(pe):
            def body(i, r):
                p, q = r % 2, (r + 1) % 2
                if has(i - 4):
                    if counts(i - 3):
                        pe.wait_ge(f_ready, i - 3)
                    if counts(i - 5):
                        pe.wait_ge(x_added, i - 5)
                    for s in range(TPS):
                        last = nc.tensor.matmul(o_ps[p][:, s * P:(s + 1) * P], qT[r % 4][:, s * P:(s + 1) * P], f[p][:],
                                                start=True, stop=True)
                    last.then_inc(o_done, 1)
                if has(i - 3):
                    if counts(i - 2):
                        pe.wait_ge(e_ready, i - 2)
                    if counts(i - 3):
                        pe.wait_ge(f_ready, i - 3)
                    nc.tensor.matmul(f_ps[:, 0:D], eT[q][:], t["wo1"][:], start=True, stop=True).then_inc(f_done, 1)
                if has(i - 2):
                    if counts(i - 1):
                        pe.wait_ge(qkv_ready, i - 1)
                    if counts(i - 2):
                        pe.wait_ge(e_ready, i - 2)
                    for s in range(TPS):
                        last = nc.tensor.matmul(e_ps[0:DL, 0:DL], kv[p][:, s, DL:2 * DL], kv[p][:, s, 0:DL],
                                                start=(s == 0), stop=(s == TPS - 1))
                    last.then_inc(e_done, 1)
                if has(i - 1):
                    if counts(i):
                        pe.wait_ge(xnT_ready, i)
                    if counts(i - 2):
                        pe.wait_ge(qkv_ready, i - 2)
                    nc.tensor.matmul(qkv_ps[q][0:DL, 0:S], t["wq1"][:], xnT[q][:], start=True, stop=True)
                    for s in range(TPS):
                        last = nc.tensor.matmul(qkv_ps[q][:, S + s * P:S + (s + 1) * P], xnT[q][:, s * P:(s + 1) * P],
                                                t["wkv1"][:], start=True, stop=True)
                    last.then_inc(qkv_done, 1)
                if has(i):
                    pe.wait_ge(xn_ready, i + 1)
                    if counts(i):
                        pe.wait_ge(xnT_ready, i)
                    for s in range(TPS):
                        last = nc.tensor.transpose(x_ps[:, s * P:(s + 1) * P], xn[p][:, s, :], ident[:])
                    last.then_inc(x_done, 1)

            run(pe, body)


def program(nc, dram):
    ys = nc.dram_tensor("expert_rows", (2 * NT * P, D), F32).ap()
    scratch = [nc.dram_tensor(f"parts_scratch{i}", (2, NPART, DH, H, S), BF16).ap() for i in range(2)]
    with ExitStack() as ctx:
        t = {"rows": nc.dram_tensor("normed_rows", (NT * P, D), F32).ap(), "packs_loaded": ctx.enter_context(nc.semaphore("packs_loaded"))}

        def alloc(c, *named):
            for name, shape, dt in named:
                t[name] = c.enter_context(nc.sbuf_tensor(name, shape, dt))

        alloc(ctx, ("x", [P, NT, D], F32), ("stats", [P, NT, 6], F32), ("mean", [P, NT], F32), ("rstd", [P, NT], F32),
              ("ntmp", [P, 5, NT], F32), ("eps", [P, 1], F32), ("ident", [P, P], F32), ("identb", [P, P], BF16),
              ("wr0", [D, E], F32), ("br0", [P, E], F32), ("wr1", [D, E], F32), ("br1", [P, E], F32),
              ("cst", [P, E + 17 + n_tiles(2) + P], F32), ("iotab", [P, P], BF16),
              ("afterb", [P, P], BF16), ("tri", [P, 2 * P], F32), ("before", [P, P], BF16), ("onesb", [P, P], BF16),
              ("wq1", [D, DL], F32), ("wkv1", [D, 2 * DL], F32), ("wo1", [DL, D], F32),
              ("gates", [P, 2, NT], F32), ("takes", [P, 2 * n_tiles(2)], I32), ("goes", [P, 2 * n_tiles(2)], I32),
              ("eidx", [P, n_tiles(2)], I32),
              ("wpack0", [P, E, PK], F32))
        with ExitStack() as c1:
            alloc(c1, ("wq0", [D, D], F32), ("wk0", [D, D], F32), ("wv0", [D, D], F32), ("wo0", [D, D], F32),
                  ("mask_qk", [P, 4, P], BF16), ("mask_kq", [P, 4, P], BF16))
            t["qst"] = [c1.enter_context(nc.sbuf_tensor(f"qst{i}", [P, H, S], BF16)) for i in range(4)]
            t["kst"] = [c1.enter_context(nc.sbuf_tensor(f"kst{i}", [P, H, S], BF16)) for i in range(4)]
            t["vaug"] = [c1.enter_context(nc.sbuf_tensor(f"vaug{i}", [P, TPS, H, 32], F32)) for i in range(2)]
            load_inputs(nc, t, dram)
            norm_scales(nc, t)
            causal_attention(nc, t, scratch)
        alloc(ctx, ("wpack1", [P, E, PK], F32))
        norm_scales(nc, t)
        route(nc, t, 2, 0)
        experts(nc, t, 2, 0, ys)
        combine(nc, t, 2, 0, ys)
        norm_scales(nc, t)
        linear_attention(nc, t, dram)
        norm_scales(nc, t)
        route(nc, t, 1, 1)
        experts(nc, t, 1, 1, ys)
        combine(nc, t, 1, 1, ys, dram["out"])


def kernel(**inputs):
    import numpy as _np
    import concourse.bacc as _bacc
    from concourse.bass_utils import run_bass_kernel_spmd as _run

    def lay(a):
        return _np.ascontiguousarray(a)

    def by_feature(w):
        return lay(w.reshape(H, DH, D).transpose(2, 1, 0).reshape(D, D))

    def pack(w1, b1, w2, b2):
        w1, b1, w2, b2 = (_np.asarray(a) for a in (w1, b1, w2, b2))
        parts = [w1, b1.reshape(E, FC, P).transpose(0, 2, 1), w2.reshape(E, FC, P, D).transpose(0, 2, 1, 3).reshape(E, P, FF),
                 b2.reshape(E, P, 1)]
        return lay(_np.concatenate(parts, axis=2).transpose(1, 0, 2))

    nc = _bacc.Bacc("TRN2", target_bir_lowering=False, num_devices=1)
    i = {k: _np.asarray(v) for k, v in inputs.items()}
    x = i["L0_attn_in_features"]
    ntl = n_tiles(2)
    shape_constants = _np.broadcast_to(_np.concatenate([E - _np.arange(E), RT * _np.arange(16), _np.arange(ntl)]), (P, E + 16 + ntl))
    arrays = {
        "x": lay(x.reshape(NT * P, D)),
        "wq0": by_feature(i["L0_attn_Wq"]), "wk0": by_feature(i["L0_attn_Wk"]),
        "wv0": lay(i["L0_attn_Wv"].T), "wo0": lay(i["L0_attn_Wo"].T),
        "wr0": lay(i["L0_ffn_router_w"]), "br0": lay(i["L0_ffn_router_b"].reshape(1, E)),
        "wr1": lay(i["L1_ffn_w_gate"]), "br1": lay(i["L1_ffn_b_gate"].reshape(1, E)),
        "wq1": lay(i["L1_attn_wq"].T), "wkv1": lay(_np.concatenate([i["L1_attn_wk"].T, i["L1_attn_wv"].T], axis=1)),
        "wo1": lay(i["L1_attn_wo"].T),
        "wpack0": pack(i["L0_ffn_w1"], i["L0_ffn_b1"], i["L0_ffn_w2"], i["L0_ffn_b2"]),
        "wpack1": pack(i["L1_ffn_W1"], i["L1_ffn_b1"], i["L1_ffn_W2"], i["L1_ffn_b2"]),
        "cst": lay(_np.concatenate([shape_constants, _np.arange(P)[:, None], _np.tile(_np.arange(P), (P, 1))], axis=1).astype(_np.float32)),
        "tri": lay(_np.concatenate([_np.triu(_np.ones((P, P), _np.float32), 1), _np.ones((P, P), _np.float32)], axis=1)),
    }
    dram = {k: nc.dram_tensor(f"in_{k}", a.shape, mybir.dt.from_np(a.dtype), kind="ExternalInput").ap() for k, a in arrays.items()}
    dram["out"] = nc.dram_tensor("out_x", (NT * P, D), F32, kind="ExternalOutput").ap()
    program(nc, dram)
    r = _run(nc, [{f"in_{k}": a for k, a in arrays.items()}], core_ids=[0])
    return r.results[0]["out_x"].reshape(x.shape)
```
